# Optimizing a Trainium2 kernel written in Bass

```python
import numpy as np
import jax
import jax.numpy as jnp

def _softmax(x, axis=-1):
    return jax.nn.softmax(x, axis=axis)

def _gelu(x):
    return jax.nn.gelu(x, approximate=True)

def _silu(x):
    return jax.nn.silu(x)

def _sigmoid(x):
    return jax.nn.sigmoid(x)

def _layernorm(x, axis=-1, eps=1e-05):
    m = jnp.mean(x, axis=axis, keepdims=True)
    v = jnp.var(x, axis=axis, keepdims=True)
    return (x - m) / jnp.sqrt(v + eps)

def _scatter_add(tgt, idx, src, axis=0):
    return tgt.at[idx].add(src)

def _segment_sum(src, seg, n):
    return jax.ops.segment_sum(src, seg, n)
kernel_name = 'mk_early_fusion_d4_tok_img256_r4_21d20f'

def setup_inputs(seed: int=0):
    np.random.seed(seed)
    _w = jnp.asarray

    def _rec_inputs():
        import jax
        import jax.numpy as jnp
        _rk = jax.random.key(seed)
        x = -0.000596345 + 1.00056 * jax.random.normal(jax.random.fold_in(_rk, 1), (64, 64, 64, 3), jnp.float32)
        txt = 0.00441585 + 0.02 * jax.random.normal(jax.random.fold_in(_rk, 2), (64, 32, 64), jnp.float32)
        return (x, txt)
    x, txt = _rec_inputs()

    def _L0_tok_setup():
        import jax, jax.numpy as jnp
        import numpy as np
        from jax import lax
        NEG_SLOPE = 0.01

        def leaky(v):
            return jnp.where(v >= 0, v, NEG_SLOPE * v)
        key = jax.random.key(seed)
        ks = jax.random.split(key, 12)
        B, H, W = (16, 64, 64)
        width, mx, my, L, nl = (32, 16, 16, 3, 4)
        scale = 1.0 / (width * width)
        return {'x': jax.random.normal(ks[0], (B, H, W, 3), jnp.float32), 'input_grid': jax.random.uniform(ks[1], (H, W, 2), jnp.float32), 'P_w': jax.random.normal(ks[2], (5, width), jnp.float32) * 0.3, 'P_b': jax.random.normal(ks[3], (width,), jnp.float32) * 0.05, 'spec_wr': jax.random.uniform(ks[4], (nl, width, width, mx, my), jnp.float32) * scale, 'spec_wi': jax.random.uniform(ks[5], (nl, width, width, mx, my), jnp.float32) * scale, 'conv_w': jax.random.normal(ks[6], (nl, width, width, L, L), jnp.float32) * 0.05, 'conv_b': jax.random.normal(ks[7], (nl, width), jnp.float32) * 0.05, 'Q1_w': jax.random.normal(ks[8], (width, width), jnp.float32) * 0.15, 'Q1_b': jax.random.normal(ks[9], (width,), jnp.float32) * 0.05, 'Q2_w': jax.random.normal(ks[10], (width, 1), jnp.float32) * 0.15, 'Q2_b': jax.random.normal(ks[11], (1,), jnp.float32) * 0.05}
    _L0_tok_all = _L0_tok_setup()
    _L0_tok_in = {k: v for k, v in _L0_tok_all.items() if k in ('input_grid', 'P_w', 'P_b', 'spec_wr', 'spec_wi', 'conv_w', 'conv_b', 'Q1_w', 'Q1_b', 'Q2_w', 'Q2_b')}
    del _L0_tok_all

    def _L0_attn_setup():
        import jax, jax.numpy as jnp
        import numpy as np
        key = jax.random.key(seed)
        ks = jax.random.split(key, 5)
        b, t, e, h = (8, 256, 64, 8)
        w = lambda k, shape: jax.random.normal(k, shape, dtype=jnp.float32) * 0.02
        return {'x': jax.random.normal(ks[0], (b, t, e), dtype=jnp.float32), 'Wq': w(ks[1], (e, e * h)), 'bq': jnp.zeros((e * h,), jnp.float32), 'Wk': w(ks[2], (e, e * h)), 'bk': jnp.zeros((e * h,), jnp.float32), 'Wv': w(ks[3], (e, e * h)), 'bv': jnp.zeros((e * h,), jnp.float32), 'Wu': w(ks[4], (e * h, e)), 'bu': jnp.zeros((e,), jnp.float32)}
    _L0_attn_all = _L0_attn_setup()
    _L0_attn_in = {k: v for k, v in _L0_attn_all.items() if k in ('Wq', 'bq', 'Wk', 'bk', 'Wv', 'bv', 'Wu', 'bu')}
    del _L0_attn_all

    def _L0_ffn_setup():
        import jax, jax.numpy as jnp
        import numpy as np
        B, S, H, F, E, K = (8, 1024, 64, 128, 16, 2)
        EPS = 1e-05
        key = jax.random.key(seed)
        ks = jax.random.split(key, 9)
        sc = 0.02
        return {'x': jax.random.normal(ks[0], (B, S, H), dtype=jnp.float32), 'gate_w': jax.random.normal(ks[1], (H, E), dtype=jnp.float32) * sc, 'gate_b': jnp.zeros((E,), dtype=jnp.float32), 'w1': jax.random.normal(ks[2], (E, H, F), dtype=jnp.float32) * sc, 'b1': jnp.zeros((E, F), dtype=jnp.float32), 'w2': jax.random.normal(ks[3], (E, F, H), dtype=jnp.float32) * sc, 'b2': jnp.zeros((E, H), dtype=jnp.float32), 'gamma': jnp.ones((H,), dtype=jnp.float32), 'beta': jnp.zeros((H,), dtype=jnp.float32)}
    _L0_ffn_all = _L0_ffn_setup()
    _L0_ffn_in = {k: v for k, v in _L0_ffn_all.items() if k in ('gate_w', 'gate_b', 'w1', 'b1', 'w2', 'b2', 'gamma', 'beta')}
    del _L0_ffn_all

    def _L1_attn_setup():
        import jax, jax.numpy as jnp
        import numpy as np
        BN_EPS = 1e-05
        key = jax.random.key(seed)
        ks = jax.random.split(key, 4)
        B, N, D = (8, 2048, 64)
        outD = 64
        s = 1.0 / np.sqrt(D)
        return {'feature': jax.random.normal(ks[0], (B, N, D), dtype=jnp.float32), 'W_qk': jax.random.normal(ks[1], (2, D, D), dtype=jnp.float32) * s, 'b_qk': jnp.zeros((2, D), dtype=jnp.float32), 'W_v': jax.random.normal(ks[2], (D, outD), dtype=jnp.float32) * s, 'b_v': jnp.zeros((outD,), dtype=jnp.float32), 'gamma': jnp.ones((D,), dtype=jnp.float32), 'beta': jnp.zeros((D,), dtype=jnp.float32)}
    _L1_attn_all = _L1_attn_setup()
    _L1_attn_in = {k: v for k, v in _L1_attn_all.items() if k in ('W_qk', 'b_qk', 'W_v', 'b_v', 'gamma', 'beta')}
    del _L1_attn_all

    def _L1_ffn_setup():
        import math
        import jax, jax.numpy as jnp
        import numpy as np
        CAPACITY_FACTOR = 1.25
        key = jax.random.key(seed)
        ks = jax.random.split(key, 5)
        B, L, D, F, E = (8, 2048, 64, 256, 8)
        h = jax.random.normal(ks[0], (B, L, D), dtype=jnp.float32)
        gate_w = jax.random.normal(ks[1], (D, E), dtype=jnp.float32) * 0.02
        gate_b = jnp.zeros((E,), dtype=jnp.float32)
        w1 = jax.random.normal(ks[2], (E, D, F), dtype=jnp.float32) * (1.0 / math.sqrt(D))
        b1 = jnp.zeros((E, F), dtype=jnp.float32)
        w2 = jax.random.normal(ks[3], (E, F, D), dtype=jnp.float32) * (1.0 / math.sqrt(F))
        b2 = jnp.zeros((E, D), dtype=jnp.float32)
        return {'h': h, 'gate_w': gate_w, 'gate_b': gate_b, 'w1': w1, 'b1': b1, 'w2': w2, 'b2': b2}
    _L1_ffn_all = _L1_ffn_setup()
    _L1_ffn_in = {k: v for k, v in _L1_ffn_all.items() if k in ('gate_w', 'gate_b', 'w1', 'b1', 'w2', 'b2')}
    del _L1_ffn_all

    def _L2_attn_setup():
        import jax, jax.numpy as jnp
        import numpy as np
        EPS = 1e-05

        def _ln(x, scale):
            mu = jnp.mean(x, axis=-1, keepdims=True)
            var = jnp.var(x, axis=-1, keepdims=True)
            return (x - mu) / jnp.sqrt(var + EPS) * scale
        key = jax.random.key(seed)
        k = jax.random.split(key, 8)
        B, S, E, H = (4, 512, 64, 8)
        n_layer = 12
        x = jax.random.normal(k[0], (B, S, E), dtype=jnp.float32)
        e = jax.random.normal(k[1], (B, S, E), dtype=jnp.float32)
        p = jax.random.normal(k[2], (S, E), dtype=jnp.float32)
        W_q = 0.02 * jax.random.normal(k[3], (H, E, E), dtype=jnp.float32)
        W_k = 0.02 * jax.random.normal(k[4], (H, E, E), dtype=jnp.float32)
        W_v = 0.02 * jax.random.normal(k[5], (H, E, E), dtype=jnp.float32)
        W_o = 0.02 / np.sqrt(2 * n_layer) * jax.random.normal(k[6], (E, H * E), dtype=jnp.float32)
        gamma = jnp.ones((1, H, 1, 1), dtype=jnp.float32)
        ln_scale = jnp.ones((E,), dtype=jnp.float32)
        return {'x': x, 'e': e, 'p': p, 'ln_scale': ln_scale, 'W_q': W_q, 'W_k': W_k, 'W_v': W_v, 'W_o': W_o, 'gamma': gamma}
    _L2_attn_all = _L2_attn_setup()
    _L2_attn_in = {k: v for k, v in _L2_attn_all.items() if k in ('e', 'p', 'ln_scale', 'W_q', 'W_k', 'W_v', 'W_o', 'gamma')}
    del _L2_attn_all

    def _L2_ffn_setup():
        import jax, jax.numpy as jnp
        import numpy as np
        B, A = (1024, 8)
        IN, OUT = (64, 64)
        SH1, SH2 = (64, 128)
        EH1, EH2 = (128, 64)
        E, TOPK = (4, 2)

        def _shared_mlp(x, W1, b1, W2, b2, W3, b3):
            h = jax.nn.relu(x @ W1 + b1)
            h = jax.nn.relu(h @ W2 + b2)
            return h @ W3 + b3

        def _experts_mlp(x, eW1, eb1, eW2, eb2, eW3, eb3):
            h = jax.nn.relu(jnp.einsum('baf,efh->ebah', x, eW1) + eb1[:, None, None, :])
            h = jax.nn.relu(jnp.einsum('ebah,ehg->ebag', h, eW2) + eb2[:, None, None, :])
            o = jnp.einsum('ebag,ego->ebao', h, eW3) + eb3[:, None, None, :]
            return jnp.moveaxis(o, 0, -1)
        key = jax.random.key(seed)
        ks = jax.random.split(key, 16)
        s = 0.05
        return {'x': jax.random.normal(ks[0], (B, A, IN), jnp.float32), 'sW1': jax.random.normal(ks[1], (IN, SH1), jnp.float32) * s, 'sb1': jnp.zeros((SH1,), jnp.float32), 'sW2': jax.random.normal(ks[2], (SH1, SH2), jnp.float32) * s, 'sb2': jnp.zeros((SH2,), jnp.float32), 'sW3': jax.random.normal(ks[3], (SH2, OUT), jnp.float32) * s, 'sb3': jnp.zeros((OUT,), jnp.float32), 'eW1': jax.random.normal(ks[4], (E, IN, EH1), jnp.float32) * s, 'eb1': jnp.zeros((E, EH1), jnp.float32), 'eW2': jax.random.normal(ks[5], (E, EH1, EH2), jnp.float32) * s, 'eb2': jnp.zeros((E, EH2), jnp.float32), 'eW3': jax.random.normal(ks[6], (E, EH2, OUT), jnp.float32) * s, 'eb3': jnp.zeros((E, OUT), jnp.float32), 'gW': jax.random.normal(ks[7], (IN, E), jnp.float32) * s, 'gb': jnp.zeros((E,), jnp.float32)}
    _L2_ffn_all = _L2_ffn_setup()
    _L2_ffn_in = {k: v for k, v in _L2_ffn_all.items() if k in ('sW1', 'sb1', 'sW2', 'sb2', 'sW3', 'sb3', 'eW1', 'eb1', 'eW2', 'eb2', 'eW3', 'eb3', 'gW', 'gb')}
    del _L2_ffn_all

    def _L3_attn_setup():
        import jax, jax.numpy as jnp
        import numpy as np
        D_ATT = 64
        D_GROUP = 32
        N_GROUP = D_ATT // D_GROUP
        key = jax.random.key(seed)
        ks = jax.random.split(key, 6)
        B, L = (4, 128)
        import math
        s = 1.0 / math.sqrt(D_ATT)
        return {'x': jax.random.normal(ks[0], (B, L, D_ATT), dtype=jnp.float32), 'Wq': jax.random.normal(ks[1], (D_ATT, D_ATT), dtype=jnp.float32) * s * 0.06, 'Wk': jax.random.normal(ks[2], (D_ATT, D_ATT), dtype=jnp.float32) * s * 0.06, 'Wv': jax.random.normal(ks[3], (D_ATT, D_ATT), dtype=jnp.float32) * s * 0.06, 'w_mlp': jax.random.normal(ks[4], (D_GROUP,), dtype=jnp.float32) * 0.1, 'b_mlp': jax.random.normal(ks[5], (1,), dtype=jnp.float32) * 0.1}
    _L3_attn_all = _L3_attn_setup()
    _L3_attn_in = {k: v for k, v in _L3_attn_all.items() if k in ('Wq', 'Wk', 'Wv', 'w_mlp', 'b_mlp')}
    del _L3_attn_all

    def _L3_ffn_setup():
        import jax, jax.numpy as jnp
        import numpy as np
        DIM = 64
        HEADS = 8
        NUM_KEYS = 64
        NUM_KV = NUM_KEYS ** 2
        PK_TOPK = 16
        FINAL_TOPK = 16
        DIM_KEY = DIM // 2
        P = 2

        def _pk(x, Wq_pk, pk_keys):
            b, n, _ = x.shape
            q = (x @ Wq_pk).reshape(b, n, P, HEADS, DIM_KEY).transpose(2, 0, 1, 3, 4)
            sim = jnp.einsum('pbnhd,pkhd->pbnhk', q, pk_keys)
            scores, idx = jax.lax.top_k(sim, PK_TOPK)
            idx0 = idx[0]
            idx1 = idx[1] * NUM_KEYS
            index = (idx0[..., :, None] + idx1[..., None, :]).reshape(b, n, HEADS, PK_TOPK * PK_TOPK)
            score = (scores[0][..., :, None] + scores[1][..., None, :]).reshape(b, n, HEADS, PK_TOPK * PK_TOPK)
            final_scores, pk_idx = jax.lax.top_k(score, FINAL_TOPK)
            final_indices = jnp.take_along_axis(index, pk_idx, axis=-1)
            final_scores = jax.nn.softmax(final_scores, axis=-1)
            return (final_scores, final_indices)
        key = jax.random.key(seed)
        ks = jax.random.split(key, 7)
        b, n = (2, 256)
        std = 0.02
        x = jax.random.normal(ks[0], (b, n, DIM), dtype=jnp.float32)
        Wq_pk = jax.random.normal(ks[1], (DIM, P * HEADS * DIM_KEY), dtype=jnp.float32) * std
        pk_keys = jax.random.normal(ks[2], (P, NUM_KEYS, HEADS, DIM_KEY), dtype=jnp.float32) * std
        Wq = jax.random.normal(ks[3], (DIM, HEADS * DIM), dtype=jnp.float32) * std
        keys_table = jax.random.normal(ks[4], (NUM_KV * HEADS, DIM), dtype=jnp.float32) * std
        values_table = jax.random.normal(ks[5], (NUM_KV * HEADS, DIM), dtype=jnp.float32) * std
        Wo = jax.random.normal(ks[6], (DIM * HEADS, DIM), dtype=jnp.float32) * std
        return {'x': x, 'Wq_pk': Wq_pk, 'pk_keys': pk_keys, 'Wq': Wq, 'keys_table': keys_table, 'values_table': values_table, 'Wo': Wo}
    _L3_ffn_all = _L3_ffn_setup()
    _L3_ffn_in = {k: v for k, v in _L3_ffn_all.items() if k in ('Wq_pk', 'pk_keys', 'Wq', 'keys_table', 'values_table', 'Wo')}
    del _L3_ffn_all
    return {'x': x, 'txt': txt, 'L0_tok_input_grid': _L0_tok_in['input_grid'], 'L0_tok_P_w': _L0_tok_in['P_w'], 'L0_tok_P_b': _L0_tok_in['P_b'], 'L0_tok_spec_wr': _L0_tok_in['spec_wr'], 'L0_tok_spec_wi': _L0_tok_in['spec_wi'], 'L0_tok_conv_w': _L0_tok_in['conv_w'], 'L0_tok_conv_b': _L0_tok_in['conv_b'], 'L0_tok_Q1_w': _L0_tok_in['Q1_w'], 'L0_tok_Q1_b': _L0_tok_in['Q1_b'], 'L0_tok_Q2_w': _L0_tok_in['Q2_w'], 'L0_tok_Q2_b': _L0_tok_in['Q2_b'], 'L0_attn_Wq': _L0_attn_in['Wq'], 'L0_attn_bq': _L0_attn_in['bq'], 'L0_attn_Wk': _L0_attn_in['Wk'], 'L0_attn_bk': _L0_attn_in['bk'], 'L0_attn_Wv': _L0_attn_in['Wv'], 'L0_attn_bv': _L0_attn_in['bv'], 'L0_attn_Wu': _L0_attn_in['Wu'], 'L0_attn_bu': _L0_attn_in['bu'], 'L0_ffn_gate_w': _L0_ffn_in['gate_w'], 'L0_ffn_gate_b': _L0_ffn_in['gate_b'], 'L0_ffn_w1': _L0_ffn_in['w1'], 'L0_ffn_b1': _L0_ffn_in['b1'], 'L0_ffn_w2': _L0_ffn_in['w2'], 'L0_ffn_b2': _L0_ffn_in['b2'], 'L0_ffn_gamma': _L0_ffn_in['gamma'], 'L0_ffn_beta': _L0_ffn_in['beta'], 'L1_attn_W_qk': _L1_attn_in['W_qk'], 'L1_attn_b_qk': _L1_attn_in['b_qk'], 'L1_attn_W_v': _L1_attn_in['W_v'], 'L1_attn_b_v': _L1_attn_in['b_v'], 'L1_attn_gamma': _L1_attn_in['gamma'], 'L1_attn_beta': _L1_attn_in['beta'], 'L1_ffn_gate_w': _L1_ffn_in['gate_w'], 'L1_ffn_gate_b': _L1_ffn_in['gate_b'], 'L1_ffn_w1': _L1_ffn_in['w1'], 'L1_ffn_b1': _L1_ffn_in['b1'], 'L1_ffn_w2': _L1_ffn_in['w2'], 'L1_ffn_b2': _L1_ffn_in['b2'], 'L2_attn_e': _L2_attn_in['e'], 'L2_attn_p': _L2_attn_in['p'], 'L2_attn_ln_scale': _L2_attn_in['ln_scale'], 'L2_attn_W_q': _L2_attn_in['W_q'], 'L2_attn_W_k': _L2_attn_in['W_k'], 'L2_attn_W_v': _L2_attn_in['W_v'], 'L2_attn_W_o': _L2_attn_in['W_o'], 'L2_attn_gamma': _L2_attn_in['gamma'], 'L2_ffn_sW1': _L2_ffn_in['sW1'], 'L2_ffn_sb1': _L2_ffn_in['sb1'], 'L2_ffn_sW2': _L2_ffn_in['sW2'], 'L2_ffn_sb2': _L2_ffn_in['sb2'], 'L2_ffn_sW3': _L2_ffn_in['sW3'], 'L2_ffn_sb3': _L2_ffn_in['sb3'], 'L2_ffn_eW1': _L2_ffn_in['eW1'], 'L2_ffn_eb1': _L2_ffn_in['eb1'], 'L2_ffn_eW2': _L2_ffn_in['eW2'], 'L2_ffn_eb2': _L2_ffn_in['eb2'], 'L2_ffn_eW3': _L2_ffn_in['eW3'], 'L2_ffn_eb3': _L2_ffn_in['eb3'], 'L2_ffn_gW': _L2_ffn_in['gW'], 'L2_ffn_gb': _L2_ffn_in['gb'], 'L3_attn_Wq': _L3_attn_in['Wq'], 'L3_attn_Wk': _L3_attn_in['Wk'], 'L3_attn_Wv': _L3_attn_in['Wv'], 'L3_attn_w_mlp': _L3_attn_in['w_mlp'], 'L3_attn_b_mlp': _L3_attn_in['b_mlp'], 'L3_ffn_Wq_pk': _L3_ffn_in['Wq_pk'], 'L3_ffn_pk_keys': _L3_ffn_in['pk_keys'], 'L3_ffn_Wq': _L3_ffn_in['Wq'], 'L3_ffn_keys_table': _L3_ffn_in['keys_table'], 'L3_ffn_values_table': _L3_ffn_in['values_table'], 'L3_ffn_Wo': _L3_ffn_in['Wo']}

def reference(x, txt, L0_tok_input_grid, L0_tok_P_w, L0_tok_P_b, L0_tok_spec_wr, L0_tok_spec_wi, L0_tok_conv_w, L0_tok_conv_b, L0_tok_Q1_w, L0_tok_Q1_b, L0_tok_Q2_w, L0_tok_Q2_b, L0_attn_Wq, L0_attn_bq, L0_attn_Wk, L0_attn_bk, L0_attn_Wv, L0_attn_bv, L0_attn_Wu, L0_attn_bu, L0_ffn_gate_w, L0_ffn_gate_b, L0_ffn_w1, L0_ffn_b1, L0_ffn_w2, L0_ffn_b2, L0_ffn_gamma, L0_ffn_beta, L1_attn_W_qk, L1_attn_b_qk, L1_attn_W_v, L1_attn_b_v, L1_attn_gamma, L1_attn_beta, L1_ffn_gate_w, L1_ffn_gate_b, L1_ffn_w1, L1_ffn_b1, L1_ffn_w2, L1_ffn_b2, L2_attn_e, L2_attn_p, L2_attn_ln_scale, L2_attn_W_q, L2_attn_W_k, L2_attn_W_v, L2_attn_W_o, L2_attn_gamma, L2_ffn_sW1, L2_ffn_sb1, L2_ffn_sW2, L2_ffn_sb2, L2_ffn_sW3, L2_ffn_sb3, L2_ffn_eW1, L2_ffn_eb1, L2_ffn_eW2, L2_ffn_eb2, L2_ffn_eW3, L2_ffn_eb3, L2_ffn_gW, L2_ffn_gb, L3_attn_Wq, L3_attn_Wk, L3_attn_Wv, L3_attn_w_mlp, L3_attn_b_mlp, L3_ffn_Wq_pk, L3_ffn_pk_keys, L3_ffn_Wq, L3_ffn_keys_table, L3_ffn_values_table, L3_ffn_Wo):
    import jax
    import jax.numpy as jnp

    def _L0_tok_ref(x, input_grid, P_w, P_b, spec_wr, spec_wi, conv_w, conv_b, Q1_w, Q1_b, Q2_w, Q2_b):
        import jax, jax.numpy as jnp
        import numpy as np
        from jax import lax
        NEG_SLOPE = 0.01

        def leaky(v):
            return jnp.where(v >= 0, v, NEG_SLOPE * v)
        B, H, W, _ = x.shape
        nl, _, _, mx, my = spec_wr.shape
        grid = jnp.broadcast_to(input_grid[None], (B, H, W, input_grid.shape[-1]))
        h = jnp.concatenate([grid, x], axis=-1) @ P_w + P_b
        h = jnp.transpose(h, (0, 3, 1, 2))
        dn = ('NCHW', 'OIHW', 'NCHW')
        for i in range(nl):
            h_ft = jnp.fft.rfft2(h)
            w_c = spec_wr[i] + 1j * spec_wi[i]
            out_modes = jnp.einsum('bixy,ioxy->boxy', h_ft[:, :, :mx, :my], w_c)
            spec = jnp.fft.irfft2(out_modes, s=(H, W))
            conv = lax.conv_general_dilated(h, conv_w[i], (1, 1), 'SAME', dimension_numbers=dn)
            conv = conv + conv_b[i][None, :, None, None]
            h = leaky(spec + conv)
        h = jnp.transpose(h, (0, 2, 3, 1))
        h = leaky(h @ Q1_w + Q1_b)
        out = (h @ Q2_w + Q2_b)[..., 0]
        return out

    def _L0_attn_ref(x, Wq, bq, Wk, bk, Wv, bv, Wu, bu):
        import jax, jax.numpy as jnp
        import numpy as np
        b, t, e = x.shape
        h = Wq.shape[1] // e
        q = (x @ Wq + bq).reshape(b, t, h, e)
        k = (x @ Wk + bk).reshape(b, t, h, e)
        v = (x @ Wv + bv).reshape(b, t, h, e)
        scores = jnp.einsum('bihe,bjhe->bhij', q, k) / jnp.sqrt(jnp.asarray(e, jnp.float32))
        i = jnp.arange(t)[:, None]
        j = jnp.arange(t)[None, :]
        scores = jnp.where(j >= i, -jnp.inf, scores)
        scores = jnp.where(i == 0, 0.0, scores)
        att = jax.nn.softmax(scores, axis=-1)
        att = jnp.where(i == 0, 0.0, att)
        out = jnp.einsum('bhij,bjhe->bihe', att, v).reshape(b, t, h * e)
        return out @ Wu + bu

    def _L0_ffn_ref(x, gate_w, gate_b, w1, b1, w2, b2, gamma, beta):
        import jax, jax.numpy as jnp
        import numpy as np
        B, S, H, F, E, K = (8, 1024, 64, 128, 16, 2)
        EPS = 1e-05
        gate_logits = x @ gate_w + gate_b
        topk_vals, topk_idx = jax.lax.top_k(gate_logits, K)
        topk_w = jax.nn.softmax(topk_vals, axis=-1)
        h = jax.nn.relu(jnp.einsum('bsh,ehf->bsef', x, w1) + b1)
        expert_out = jnp.einsum('bsef,efh->bseh', h, w2) + b2
        sel = jnp.take_along_axis(expert_out, topk_idx[:, :, :, None], axis=2)
        moe = jnp.sum(topk_w[..., None] * sel, axis=2)
        y = x + moe
        mu = jnp.mean(y, axis=-1, keepdims=True)
        var = jnp.var(y, axis=-1, keepdims=True)
        return (y - mu) / jnp.sqrt(var + EPS) * gamma + beta

    def _L1_attn_ref(feature, W_qk, b_qk, W_v, b_v, gamma, beta):
        import jax, jax.numpy as jnp
        import numpy as np
        BN_EPS = 1e-05
        QK = jnp.einsum('bnd,kde->bkne', feature, W_qk) + b_qk[None, :, None, :]
        value = jnp.einsum('bnd,de->bne', feature, W_v) + b_v
        query = QK[:, 0]
        key = QK[:, 1]
        sm = jax.nn.softmax(key, axis=1)
        lam = jnp.einsum('bnd,bne->bde', sm, value)
        mean = jnp.mean(lam, axis=(0, 2), keepdims=True)
        var = jnp.var(lam, axis=(0, 2), keepdims=True)
        bn = (lam - mean) * jax.lax.rsqrt(var + BN_EPS)
        bn = bn * gamma[None, :, None] + beta[None, :, None]
        return jnp.einsum('bnd,bde->bne', query, bn)

    def _L1_ffn_ref(h, gate_w, gate_b, w1, b1, w2, b2):
        import math
        import jax, jax.numpy as jnp
        import numpy as np
        CAPACITY_FACTOR = 1.25
        B, L, D = h.shape
        E = gate_w.shape[1]
        T = B * L
        C = max(1, math.ceil(CAPACITY_FACTOR * T / E))
        x = h.reshape(T, D)
        logits = x @ gate_w + gate_b
        probs = jax.nn.softmax(logits, axis=-1)
        idx = jnp.argmax(probs, axis=-1)
        prb = jnp.take_along_axis(probs, idx[:, None], axis=1)[:, 0]
        one_hot = jax.nn.one_hot(idx, E, dtype=jnp.float32)
        pos = (jnp.cumsum(one_hot, axis=0) * one_hot).sum(-1).astype(jnp.int32) - 1
        kept = pos < C
        pos_safe = jnp.where(kept, pos, C)
        buf = jnp.zeros((E, C, D), dtype=h.dtype).at[idx, pos_safe].set(x, mode='drop')
        hmid = jax.nn.relu(jnp.einsum('ecd,edf->ecf', buf, w1) + b1[:, None, :])
        ybuf = jnp.einsum('ecf,efd->ecd', hmid, w2) + b2[:, None, :]
        pos_g = jnp.minimum(pos, C - 1)
        y_tok = ybuf[idx, pos_g] * (prb * kept)[:, None]
        y = y_tok.reshape(B, L, D)
        y = jnp.nan_to_num(y, nan=0.0, posinf=10000.0, neginf=-10000.0)
        return y

    def _L2_attn_ref(x, e, p, ln_scale, W_q, W_k, W_v, W_o, gamma):
        import jax, jax.numpy as jnp
        import numpy as np
        EPS = 1e-05

        def _ln(x, scale):
            mu = jnp.mean(x, axis=-1, keepdims=True)
            var = jnp.var(x, axis=-1, keepdims=True)
            return (x - mu) / jnp.sqrt(var + EPS) * scale
        B, S, E = x.shape
        H = W_q.shape[0]
        xn = _ln(x, ln_scale)
        Q = jnp.einsum('bse,hef->bhsf', xn, W_q)
        K = jnp.einsum('bse,hef->bhsf', xn, W_k)
        V = jnp.einsum('bse,hef->bhsf', xn, W_v)
        q2 = jnp.sum(Q * Q, axis=-1)[..., :, None]
        k2 = jnp.sum(K * K, axis=-1)[..., None, :]
        qk = jnp.einsum('bhsf,bhtf->bhst', Q, K)
        sqdist = jnp.maximum(q2 + k2 - 2.0 * qk, 0.0)
        scores = jnp.exp(-gamma * sqdist)
        out = jnp.einsum('bhst,bhtf->bhsf', scores, V)
        out = out.transpose(0, 2, 1, 3).reshape(B, S, H * E)
        return out @ W_o.T

    def _L2_ffn_ref(x, sW1, sb1, sW2, sb2, sW3, sb3, eW1, eb1, eW2, eb2, eW3, eb3, gW, gb):
        import jax, jax.numpy as jnp
        import numpy as np
        B, A = (1024, 8)
        IN, OUT = (64, 64)
        SH1, SH2 = (64, 128)
        EH1, EH2 = (128, 64)
        E, TOPK = (4, 2)

        def _shared_mlp(x, W1, b1, W2, b2, W3, b3):
            h = jax.nn.relu(x @ W1 + b1)
            h = jax.nn.relu(h @ W2 + b2)
            return h @ W3 + b3

        def _experts_mlp(x, eW1, eb1, eW2, eb2, eW3, eb3):
            h = jax.nn.relu(jnp.einsum('baf,efh->ebah', x, eW1) + eb1[:, None, None, :])
            h = jax.nn.relu(jnp.einsum('ebah,ehg->ebag', h, eW2) + eb2[:, None, None, :])
            o = jnp.einsum('ebag,ego->ebao', h, eW3) + eb3[:, None, None, :]
            return jnp.moveaxis(o, 0, -1)
        all_out = _experts_mlp(x, eW1, eb1, eW2, eb2, eW3, eb3)
        shared = _shared_mlp(x, sW1, sb1, sW2, sb2, sW3, sb3)
        gates = jax.nn.softmax(x @ gW + gb, axis=-1)
        topv, topi = jax.lax.top_k(gates, TOPK)
        topw = jax.nn.softmax(topv, axis=-1)
        sel = jnp.take_along_axis(all_out, topi[:, :, None, :], axis=-1)
        gated = jnp.sum(sel * topw[:, :, None, :], axis=-1)
        return shared + gated

    def _L3_attn_ref(x, Wq, Wk, Wv, w_mlp, b_mlp):
        import jax, jax.numpy as jnp
        import numpy as np
        D_ATT = 64
        D_GROUP = 32
        N_GROUP = D_ATT // D_GROUP
        B, L, d_att = x.shape
        G, Dg = (N_GROUP, D_GROUP)
        Q = x @ Wq.T
        K = x @ Wk.T
        V = x @ Wv.T
        Qg = Q.reshape(B, L, 1, G, Dg)
        Kg = K.reshape(B, 1, L, G, Dg)
        diff = Qg - Kg
        attn = jnp.einsum('bqkgd,d->bqkg', jax.nn.relu(diff), w_mlp) + b_mlp[0]
        attn = jax.nn.relu(attn)
        attn = jax.nn.softmax(attn, axis=2)
        Vg = V.reshape(B, L, Dg, G)
        out = jnp.einsum('bqkg,bkdg->bqdg', attn, Vg)
        return out.reshape(B, L, d_att)

    def _L3_ffn_ref(x, Wq_pk, pk_keys, Wq, keys_table, values_table, Wo):
        import jax, jax.numpy as jnp
        import numpy as np
        DIM = 64
        HEADS = 8
        NUM_KEYS = 64
        NUM_KV = NUM_KEYS ** 2
        PK_TOPK = 16
        FINAL_TOPK = 16
        DIM_KEY = DIM // 2
        P = 2

        def _pk(x, Wq_pk, pk_keys):
            b, n, _ = x.shape
            q = (x @ Wq_pk).reshape(b, n, P, HEADS, DIM_KEY).transpose(2, 0, 1, 3, 4)
            sim = jnp.einsum('pbnhd,pkhd->pbnhk', q, pk_keys)
            scores, idx = jax.lax.top_k(sim, PK_TOPK)
            idx0 = idx[0]
            idx1 = idx[1] * NUM_KEYS
            index = (idx0[..., :, None] + idx1[..., None, :]).reshape(b, n, HEADS, PK_TOPK * PK_TOPK)
            score = (scores[0][..., :, None] + scores[1][..., None, :]).reshape(b, n, HEADS, PK_TOPK * PK_TOPK)
            final_scores, pk_idx = jax.lax.top_k(score, FINAL_TOPK)
            final_indices = jnp.take_along_axis(index, pk_idx, axis=-1)
            final_scores = jax.nn.softmax(final_scores, axis=-1)
            return (final_scores, final_indices)
        b, n, d = x.shape
        q = (x @ Wq).reshape(b, n, HEADS, DIM) * DIM ** (-0.5)
        kv_scores, indices = _pk(x, Wq_pk, pk_keys)
        offsets = jnp.arange(HEADS, dtype=indices.dtype) * NUM_KV
        ind = indices + offsets[None, None, :, None]
        k = jnp.einsum('bnhk,bnhkd->bnhd', kv_scores, keys_table[ind])
        v = jnp.einsum('bnhk,bnhkd->bnhd', kv_scores, values_table[ind])
        sim = jnp.einsum('bihd,bjhd->bhij', q, k)
        neg = -jnp.finfo(sim.dtype).max
        causal = jnp.tril(jnp.ones((n, n), dtype=bool))
        sim = jnp.where(causal, sim, neg)
        attn = jax.nn.softmax(sim, axis=-1)
        out = jnp.einsum('bhij,bjhd->bhid', attn, v)
        out = out.transpose(0, 2, 1, 3).reshape(b, n, HEADS * DIM)
        return out @ Wo
    h = _L0_tok_ref(x, L0_tok_input_grid, L0_tok_P_w, L0_tok_P_b, L0_tok_spec_wr, L0_tok_spec_wi, L0_tok_conv_w, L0_tok_conv_b, L0_tok_Q1_w, L0_tok_Q1_b, L0_tok_Q2_w, L0_tok_Q2_b)
    h = jnp.concatenate([h, txt], axis=1)
    h = h + _L0_attn_ref(_layernorm(h, axis=-1), L0_attn_Wq, L0_attn_bq, L0_attn_Wk, L0_attn_bk, L0_attn_Wv, L0_attn_bv, L0_attn_Wu, L0_attn_bu)
    h = h + _L0_ffn_ref(_layernorm(h, axis=-1), L0_ffn_gate_w, L0_ffn_gate_b, L0_ffn_w1, L0_ffn_b1, L0_ffn_w2, L0_ffn_b2, L0_ffn_gamma, L0_ffn_beta)
    h = h + _L1_attn_ref(_layernorm(h, axis=-1), L1_attn_W_qk, L1_attn_b_qk, L1_attn_W_v, L1_attn_b_v, L1_attn_gamma, L1_attn_beta)
    h = h + _L1_ffn_ref(_layernorm(h, axis=-1), L1_ffn_gate_w, L1_ffn_gate_b, L1_ffn_w1, L1_ffn_b1, L1_ffn_w2, L1_ffn_b2)
    h = h + _L2_attn_ref(_layernorm(h, axis=-1), L2_attn_e, L2_attn_p, L2_attn_ln_scale, L2_attn_W_q, L2_attn_W_k, L2_attn_W_v, L2_attn_W_o, L2_attn_gamma)
    h = h + _L2_ffn_ref(_layernorm(h, axis=-1), L2_ffn_sW1, L2_ffn_sb1, L2_ffn_sW2, L2_ffn_sb2, L2_ffn_sW3, L2_ffn_sb3, L2_ffn_eW1, L2_ffn_eb1, L2_ffn_eW2, L2_ffn_eb2, L2_ffn_eW3, L2_ffn_eb3, L2_ffn_gW, L2_ffn_gb)
    h = h + _L3_attn_ref(_layernorm(h, axis=-1), L3_attn_Wq, L3_attn_Wk, L3_attn_Wv, L3_attn_w_mlp, L3_attn_b_mlp)
    h = h + _L3_ffn_ref(_layernorm(h, axis=-1), L3_ffn_Wq_pk, L3_ffn_pk_keys, L3_ffn_Wq, L3_ffn_keys_table, L3_ffn_values_table, L3_ffn_Wo)
    return h

_drawn_inputs = setup_inputs


def setup_inputs(seed=0):
    import zlib

    import numpy as np

    out = dict(_drawn_inputs(seed))
    spreads = {'L0_attn_bq': (0.0, 0.8),
     'L0_attn_bk': (0.0, 2.0),
     'L0_attn_bv': (0.0, 0.1),
     'L0_attn_bu': (0.0, 0.1),
     'L0_ffn_gate_b': (0.0, 0.1),
     'L0_ffn_b1': (0.0, 0.8),
     'L0_ffn_b2': (0.0, 0.1),
     'L0_ffn_gamma': (1.0, 0.2),
     'L0_ffn_beta': (0.0, 0.1),
     'L1_attn_b_qk': (0.0, 0.1),
     'L1_attn_b_v': (0.0, 0.1),
     'L1_attn_gamma': (1.0, 0.2),
     'L1_attn_beta': (0.0, 0.1),
     'L1_ffn_gate_b': (0.0, 0.8),
     'L1_ffn_b1': (0.0, 0.8),
     'L1_ffn_b2': (0.0, 2.0),
     'L2_attn_ln_scale': (1.0, 0.6),
     'L2_attn_gamma': (1.0, 0.6),
     'L2_ffn_sb1': (0.0, 0.8),
     'L2_ffn_sb2': (0.0, 0.8),
     'L2_ffn_sb3': (0.0, 2.0),
     'L2_ffn_eb1': (0.0, 0.8),
     'L2_ffn_eb2': (0.0, 0.8),
     'L2_ffn_eb3': (0.0, 2.0),
     'L2_ffn_gb': (0.0, 0.8)}
    factors = {'L0_tok_spec_wr': 8.0,
     'L0_tok_spec_wi': 8.0,
     'L0_attn_Wq': 8.0,
     'L0_attn_Wk': 8.0,
     'L0_ffn_w1': 3.306,
     'L0_ffn_w2': 3.75,
     'L1_ffn_gate_w': 8.0,
     'L1_ffn_w1': 8.0,
     'L1_ffn_w2': 8.0,
     'L2_attn_W_q': 8.0,
     'L2_attn_W_k': 8.0,
     'L2_attn_W_v': 5.197,
     'L2_attn_W_o': 5.422,
     'L2_ffn_sW1': 8.0,
     'L2_ffn_sW2': 8.0,
     'L2_ffn_sW3': 6.499,
     'L2_ffn_eW1': 8.0,
     'L2_ffn_eW2': 8.0,
     'L2_ffn_eW3': 8.0,
     'L2_ffn_gW': 8.0,
     'L3_attn_Wq': 64.0,
     'L3_attn_Wk': 64.0,
     'L3_attn_Wv': 37.6,
     'L3_attn_w_mlp': 64.0,
     'L3_ffn_Wq_pk': 64.0,
     'L3_ffn_pk_keys': 64.0,
     'L3_ffn_Wq': 64.0,
     'L3_ffn_keys_table': 64.0,
     'L3_ffn_values_table': 64.0,
     'L3_ffn_Wo': 64.0}
    for name, (base, spread) in spreads.items():
        noise = np.random.default_rng([zlib.crc32(name.encode()), seed]).standard_normal(out[name].shape)
        drawn = base * np.exp(spread * noise) if base else spread * noise
        out[name] = jnp.asarray(drawn.astype(out[name].dtype))
    for name, factor in factors.items():
        out[name] = (out[name] * factor).astype(out[name].dtype)
    return out
```

```python
from contextlib import ExitStack

import concourse.bass as bass
from concourse import mybir

F32 = mybir.dt.float32
BF16 = mybir.dt.bfloat16
ALU = mybir.AluOpType
ACT = mybir.ActivationFunctionType
AX = mybir.AxisListType


T, S, E, G = 96, 64, 64, 4
NG = S // G
TG = T * G
EPS = 1e-5
HEADS = 8
NEG = -1e30


class Stage(ExitStack):

    def __init__(self, nc):
        super().__init__()
        self.nc, self.sems = nc, []

    def sem(self, name):
        self.sems.append(self.enter_context(self.nc.semaphore(name)))
        return self.sems[-1]

    def block(self):
        self.callback(self.clear)
        return self.enter_context(self.nc.Block())

    def clear(self):
        with self.nc.Block() as block:

            @block.sync
            def _(sp):
                for s in self.sems:
                    sp.sem_clear(s)


BASE = 4


def start_at_base(nc, sems):
    with nc.Block() as block:

        @block.sync
        def _(sp):
            for s in sems:
                sp.sem_inc(s, BASE)


class Link:

    def __init__(self, eng, sem, n, per, first=0):
        self.eng, self.sem, self.n, self.per, self.k, self.first = eng, sem, n, per, 0, first

    def __call__(self, ins):
        self.mark(ins)
        self.wait()

    def mark(self, ins):
        ins.then_inc(self.sem, 1)
        self.k += 1

    def wait(self):
        self.eng.wait_ge(self.sem, self.per * self.n + self.first + self.k)

    def done(self):
        assert self.k == self.per, f"{self.k} links, not {self.per}"


def group_of(H, g):
    return H[:, bass.ds(G * g, G), :]


def over(x, n):
    return x.unsqueeze(2).to_broadcast([x.shape[0], x.shape[1], n])


class Norm:

    LINKS = 6

    def __init__(self, ctx, nc, tag):
        self.st = ctx.enter_context(nc.sbuf_tensor(f"{tag}_st", [T, 5, G], F32))
        self.xc = ctx.enter_context(nc.sbuf_tensor(f"{tag}_xc", [T, G, E], F32))
        self.xn = ctx.enter_context(nc.sbuf_tensor(f"{tag}_xn", [T, G, 128], F32))
        self.xt = ctx.enter_context(nc.sbuf_tensor(f"{tag}_xt", [E + 1, TG], F32))
        self.var_ready = ctx.sem(f"{tag}_var_ready")
        self.std_ready = ctx.sem(f"{tag}_std_ready")
        self.xn_ready = ctx.sem(f"{tag}_xn_ready")
        self.turned = ctx.sem(f"{tag}_turned")
        self.xt_ready = ctx.sem(f"{tag}_xt_ready")

    def pads(self, dve, link):
        link(dve.memset(self.xn[:], 0.0))
        link(dve.memset(self.xn[:, :, E:E + 1], 1.0))

    def moments(self, dve, link, x, ready):
        st, xc, sq = self.st, self.xc, self.xn[:, :, 0:E]
        link(dve.tensor_reduce(st[:, 0], x, AX.X, ALU.add))
        link(dve.tensor_scalar(st[:, 0], st[:, 0], 1.0 / E, None, ALU.mult))
        link(dve.tensor_tensor(xc[:], x, over(st[:, 0], E), ALU.subtract))
        link(dve.tensor_tensor(sq, xc[:], xc[:], ALU.mult))
        link(dve.tensor_reduce(st[:, 1], sq, AX.X, ALU.add))
        dve.tensor_scalar(st[:, 2], st[:, 1], 1.0 / E, EPS, ALU.mult, ALU.add).then_inc(ready, 1)

    def vector(self, dve, link, x, n, scale=None):
        self.moments(dve, link, x, self.var_ready)
        dve.wait_ge(self.std_ready, n + 1)
        link(dve.reciprocal(self.st[:, 4], self.st[:, 3]))
        if scale is None:
            dve.tensor_tensor(self.xn[:, :, 0:E], self.xc[:], over(self.st[:, 4], E),
                              ALU.mult).then_inc(self.xn_ready, 1)
        else:
            link(dve.tensor_tensor(self.xc[:], self.xc[:], over(self.st[:, 4], E), ALU.mult))
            dve.tensor_tensor(self.xn[:, :, 0:E], self.xc[:],
                              scale[:].unsqueeze(1).to_broadcast([T, G, E]), ALU.mult
                              ).then_inc(self.xn_ready, 1)

    def tensor(self, pe, n, bank, ident):
        pe.wait_ge(self.xn_ready, n + 1)
        for s in range(G):
            mm = pe.transpose(bank[:, T * s:T * s + T], self.xn[:, s, :], ident[0:T, 0:T])
        mm.then_inc(self.turned, 1)

    def scalar(self, act, n, bank):
        act.wait_ge(self.var_ready, n + 1)
        act.activation(self.st[:, 3], self.st[:, 2], ACT.Sqrt).then_inc(self.std_ready, 1)
        act.wait_ge(self.turned, n + 1)
        act.activation(self.xt[:], bank[0:E + 1, 0:TG], ACT.Copy).then_inc(self.xt_ready, 1)


class Attention:

    def __init__(self, ctx, nc, tag, psum, gauss=False):
        def sb(name, shape):
            return ctx.enter_context(nc.sbuf_tensor(f"{tag}_{name}", shape, F32))

        def sem(name):
            return ctx.sem(f"{tag}_{name}")

        self.gauss = gauss
        self.qt, self.kt = sb("qt", [128, 4, TG]), sb("kt", [128, 4, TG])
        self.v = sb("v", [T, G, 512])
        self.sc = sb("sc", [T, 2, 2, 384])
        self.pt = sb("pt", [T, 2, 2, 384])
        self.ot = sb("ot", [128, 4, T])
        self.sums = sb("sums", [T, 2, HEADS])
        self.mask = sb("mask", [T, 384])
        if gauss:
            self.q2, self.k2, self.ones = sb("q2", [128, 4, TG]), sb("k2", [128, 4, TG]), sb("ones", [128, T])
            self.gamma = sb("gamma", [T, 2, 384])
        self.wo = sb("wo", [128, 4, E])
        self.S = [psum[2 * u:2 * u + 2] for u in range(2)]
        self.PT = psum[4:6]
        self.O, self.Y = psum[6], psum[7]
        self.s_done, self.sc_ready = sem("s_done"), sem("sc_ready")
        self.exp_done, self.p_ready = sem("exp_done"), sem("p_ready")
        self.pt_done, self.pt_ready = sem("pt_done"), sem("pt_ready")
        self.o_done, self.o_ready, self.y_done = sem("o_done"), sem("o_ready"), sem("y_done")
        self.links = 0 if gauss else G * (4 + 3)

    def pe_scores(self, pe, n, s):
        if s >= 2:
            pe.wait_ge(self.sc_ready, G * n + s - 1)
        c = slice(T * s, T * s + T)
        for h in range(HEADS):
            p = slice(64 * (h % 2), 64 * (h % 2) + 64)
            out = self.S[s % 2][h % 2][0:T, T * (h // 2):T * (h // 2) + T]
            if self.gauss:
                pe.matmul(out, self.kt[p, h // 2, c], self.qt[p, h // 2, c], start=True, stop=False)
                pe.matmul(out, self.k2[p, h // 2, c], self.ones[p, :], start=False, stop=False)
                mm = pe.matmul(out, self.ones[p, :], self.q2[p, h // 2, c], start=False, stop=True)
            else:
                mm = pe.matmul(out, self.qt[p, h // 2, c], self.kt[p, h // 2, c], start=True, stop=True)
        mm.then_inc(self.s_done, 1)

    def pe_turn(self, pe, n, s, ident):
        pe.wait_ge(self.p_ready, G * n + s + 1)
        for h in range(HEADS):
            mm = pe.transpose(self.PT[h % 2][0:T, T * (h // 2):T * (h // 2) + T],
                              self.sc[:, s % 2, h % 2, T * (h // 2):T * (h // 2) + T], ident[0:T, 0:T])
        mm.then_inc(self.pt_done, 1)

    def pe_values(self, pe, n, s):
        pe.wait_ge(self.exp_done if self.gauss else self.pt_ready, G * n + s + 1)
        src = (self.sc if self.gauss else self.pt)[:, s % 2]
        for h in range(HEADS):
            p = slice(64 * (h % 2), 64 * (h % 2) + 64)
            mm = pe.matmul(self.O[p, T * (h // 2):T * (h // 2) + T], self.v[:, s, 64 * h:64 * h + 64],
                           src[:, h % 2, T * (h // 2):T * (h // 2) + T], start=True, stop=True,
                           skip_group_check=True)
        mm.then_inc(self.o_done, 1)

    def pe_project(self, pe, n, s):
        pe.wait_ge(self.o_ready, G * n + s + 1)
        for j in range(4):
            mm = pe.matmul(self.Y[0:T, E * s:E * s + E], self.ot[:, j, :], self.wo[:, j, :],
                           start=(j == 0), stop=(j == 3))
        if s == G - 1:
            mm.then_inc(self.y_done, 1)

    def tensor(self, pe, n, ident):
        lag = 1 if self.gauss else 2
        for i in range(G + lag + 1):
            if i < G:
                self.pe_scores(pe, n, i)
            if i - lag - 1 >= 0:
                self.pe_project(pe, n, i - lag - 1)
            if 0 <= i - lag < G:
                self.pe_values(pe, n, i - lag)
            if not self.gauss and 0 <= i - 1 < G:
                self.pe_turn(pe, n, i - 1, ident)

    def scalar(self, act, n):
        lag = 1 if self.gauss else 2
        for s in range(G + lag):
            if s < G:
                act.wait_ge(self.sc_ready, G * n + s + 1)
                sc = self.sc[:, s % 2]
                act.activation(sc, sc, ACT.Exp, scale=-1.0 if self.gauss else 0.125).then_inc(self.exp_done, 1)
            if 0 <= s - lag < G:
                act.wait_ge(self.o_done, G * n + s - lag + 1)
                act.activation(self.ot[:].rearrange("p j t -> p (j t)"), self.O[:, 0:384],
                               ACT.Copy).then_inc(self.o_ready, 1)
            if not self.gauss and 0 <= s - 1 < G:
                act.wait_ge(self.pt_done, G * n + s)
                for b in range(2):
                    cp = act.activation(self.pt[:, (s - 1) % 2, b], self.PT[b][0:T, 0:384], ACT.Copy)
                cp.then_inc(self.pt_ready, 1)

    def dve_scores(self, dve, link, n, s):
        u = s % 2
        sc = self.sc[:, u]
        dve.wait_ge(self.s_done, G * n + s + 1)
        if s >= 2:
            dve.wait_ge(self.o_done if self.gauss else self.pt_done, G * n + s - 1)
        if self.gauss:
            dve.scalar_tensor_tensor(sc[:, 0], self.S[u][0][0:T, 0:384], 0.0, self.gamma[:, 0],
                                     ALU.max, ALU.mult)
            dve.scalar_tensor_tensor(sc[:, 1], self.S[u][1][0:T, 0:384], 0.0, self.gamma[:, 1],
                                     ALU.max, ALU.mult).then_inc(self.sc_ready, 1)
            return
        for b in range(2):
            link(dve.tensor_tensor(sc[:, b], self.S[u][b][0:T, 0:384], self.mask[:], ALU.add))
        by_head = sc.rearrange("p b (h k) -> p (b h) k", h=4)
        top = self.sums[:, 0]
        link(dve.tensor_reduce(top, by_head, AX.X, ALU.max))
        link(dve.tensor_scalar(top, top, NEG / 1e10, None, ALU.max))
        dve.tensor_tensor(by_head, by_head, over(top, T), ALU.subtract).then_inc(self.sc_ready, 1)
        dve.wait_ge(self.sc_ready, G * n + s + 1)

    def dve_normalise(self, dve, link, n, s):
        by_head = self.sc[:, s % 2].rearrange("p b (h k) -> p (b h) k", h=4)
        den = self.sums[:, 1]
        dve.wait_ge(self.exp_done, G * n + s + 1)
        link(dve.tensor_reduce(den, by_head, AX.X, ALU.add))
        link(dve.tensor_scalar(den, den, 1e-30, None, ALU.max))
        link(dve.reciprocal(den, den))
        dve.tensor_tensor(by_head, by_head, over(den, T), ALU.mult).then_inc(self.p_ready, 1)
        dve.wait_ge(self.p_ready, G * n + s + 1)

    def vector(self, dve, link, n):
        for s in range(G + 1):
            if s < G:
                self.dve_scores(dve, link, n, s)
            if s >= 1 and not self.gauss:
                self.dve_normalise(dve, link, n, s - 1)


def build_tokenizer(nc, d, H, act_out, f_out):
    NG = 16
    PIX = 4096
    NB = 8
    with Stage(nc) as ctx:
        def sb(name, shape):
            return ctx.enter_context(nc.sbuf_tensor(name, shape, F32))

        def ps(name, shape):
            return ctx.enter_context(nc.psum_tensor(name, shape, F32))

        sems = []

        def sem(name):
            sems.append(ctx.sem(name))
            return sems[-1]

        ROWS = 66
        RING = 4
        acts = nc.dram_tensor("acts_scratch", [NG, 128, ROWS, 64], F32).ap()
        modes = nc.dram_tensor("modes_scratch", [NG * 4, 32, 4, 128], F32).ap()

        ident = sb("ft_ident", [128, 128])
        lift_w = sb("ft_lift_w", [14, 128])
        lift_b = sb("ft_lift_b", [128, 1])
        conv_w = sb("ft_conv_w", [96, 3, 32])
        conv_b = sb("ft_conv_b", [128, 4])
        q1_w = sb("ft_q1_w", [128, 128])
        q1_b = sb("ft_q1_b", [128, 1])
        q2_w = sb("ft_q2_w", [128, 4])
        q2_b = sb("ft_q2_b", [4, 1])
        dft_w = sb("ft_dft_w", [128, 64])
        dft_h = sb("ft_dft_h", [128, 32])
        inv_h = sb("ft_inv_h", [128, 4, 16, 128])
        inv_w = sb("ft_inv_w", [128, 256])
        img = sb("ft_img", [96, RING, 4, 8, 64])
        anew = sb("ft_anew", [128, PIX])
        vtmp = sb("ft_vtmp", [128, 2, 512])
        xt = sb("ft_xt", [128, 2, 4, 128])
        y1 = sb("ft_y1", [128, 16, 2, 64])
        y1t = sb("ft_y1t", [128, 2, 4, 128])
        fout = sb("ft_fout", [128, 512])
        fall = sb("ft_fall", [128, 64, 128])
        wall = sb("ft_wall", [128, 64, 128])
        wq = y1[:].rearrange("p a b c -> p (a b c)").rearrange("p (u m o) -> p u m o", u=2, m=8)
        fq = y1t[:].rearrange("p a b c -> p (a b c)").rearrange("p (u m s) -> p u m s", u=2, m=8)
        og = sb("ft_og", [128, 4, 128])
        ot = sb("ft_ot", [128, 4, 128])
        zt = sb("ft_zt", [128, 16, 128])
        x5 = [img[0:14].rearrange("p a b c d -> p (a b c d)")[:, PIX * u:PIX * u + PIX] for u in range(2)]
        hout2 = wall[0:4].rearrange("p a b -> p (a b)")[:, 0:PIX]

        pa = [ps(f"ft_pa{k}", [128, 512]) for k in range(2)]
        pb = [ps(f"ft_pb{k}", [128, 4, 128]) for k in range(2)]
        pc = [ps(f"ft_pc{k}", [128, 16, 16, 2]) for k in range(2)]
        pf = ps("ft_pf", [128, 2, 16, 16])

        consts_in = sem("ft_consts_in")
        cw_in = sem("ft_cw_in")
        x_in = [sem(f"ft_x_in{u}") for u in range(2)]
        img_in = [sem(f"ft_img_in{u}") for u in range(RING)]
        border_out = sem("ft_border_out")
        pad_zero = sem("ft_pad_zero")
        acts_stored = sem("ft_acts_stored")
        modes_stored = sem("ft_modes_stored")
        f_in = sem("ft_f_in")
        w_in = sem("ft_w_in")
        w_neg = sem("ft_w_neg")
        wq_cp = sem("ft_wq_cp")
        fq_cp = sem("ft_fq_cp")
        wq_zero = sem("ft_wq_zero")
        pe_mix = sem("ft_pe_mix")
        ev_mix = sem("ft_ev_mix")
        og_cp = sem("ft_og_cp")
        pe_ot = sem("ft_pe_ot")
        ev_ot = sem("ft_ev_ot")
        pe_zt = sem("ft_pe_zt")
        ev_zt = sem("ft_ev_zt")
        pe_lift = sem("ft_pe_lift")
        ev_lift = sem("ft_ev_lift")
        pe_cv = sem("ft_pe_cv")
        ev_v = sem("ft_ev_v")
        ev_a = sem("ft_ev_a")
        pe_xt = sem("ft_pe_xt")
        ev_xt = sem("ft_ev_xt")
        pe_s1 = sem("ft_pe_s1")
        ev_s1 = sem("ft_ev_s1")
        pe_yt = sem("ft_pe_yt")
        ev_yt = sem("ft_ev_yt")
        pe_f = sem("ft_pe_f")
        ev_f = sem("ft_ev_f")
        pe_q1 = sem("ft_pe_q1")
        ev_q1 = sem("ft_ev_q1")
        ev_q1l = sem("ft_ev_q1l")
        pe_q2 = sem("ft_pe_q2")
        ev_q2 = sem("ft_ev_q2")
        h_in = sem("ft_h_in")
        txt_in = sem("ft_txt_in")
        wall_used = sem("ft_wall_used")

        start_at_base(nc, sems)
        block = ctx.block()


        @block.sync
        def _(sp):
            consts = [(ident[:], d["ident"]), (lift_w[:], d["lift_w"]), (lift_b[:], d["lift_b"]),
                      (conv_b[:], d["conv_b"]), (q1_w[:], d["q1_w"]), (q1_b[:], d["q1_b"]),
                      (q2_w[:], d["q2_w"]), (q2_b[:], d["q2_b"]), (dft_w[:], d["dft_w"]),
                      (dft_h[:], d["dft_h"]), (inv_h[:], d["inv_h"]), (inv_w[:], d["inv_w"])]
            for dst, src in consts:
                sp.dma_start(dst, src).then_inc(consts_in, 16)
            sp.dma_start(H[64:96, :, :], d["txt"]).then_inc(txt_in, 16)
            sp.wait_ge(pad_zero, BASE + 1)
            for row in (0, ROWS - 1):
                sp.dma_start(acts[:, :, row, :].rearrange("g p w -> p g w"),
                             zt[:].rearrange("p a b -> p (a b)")[:, 0:NG * 64].rearrange("p (g w) -> p g w", g=NG)
                             ).then_inc(border_out, 16)
            sp.wait_ge(border_out, BASE + 32)
            with sp.Fori(0, NG // 2) as i:
                for u in range(2):
                    g = 2 * i + u
                    sp.wait_ge(pe_lift, BASE + 16 * i)
                    sp.dma_start(x5[u][0:12], d["x"][bass.ds(g, 1), :, :]).then_inc(x_in[u], 16)
                    sp.dma_start(x5[u][12:14], d["grid"]).then_inc(x_in[u], 16)
            sp.wait_ge(pe_lift, BASE + 8 * NG)
            for l in range(4):
                sp.wait_ge(pe_cv, BASE + 128 * l)
                sp.dma_start(conv_w[:], d["conv_w"][bass.ds(l, 1)]).then_inc(cw_in, 16)
                sp.wait_ge(wq_cp, BASE + 32 * l)
                sp.wait_ge(w_neg, BASE + 2 * l)
                for mh in range(2):
                    for c in range(2):
                        for c2 in range(2):
                            src = d["wr"] if c == c2 else d["wi"]
                            p0 = 64 * mh + 32 * c
                            sp.dma_start(wall[p0:p0 + 32, 32 * c2:32 * c2 + 32, :],
                                         src[bass.ds(l, 1), :, :, 128 * mh:128 * mh + 128]).then_inc(w_in, 16)
                sp.wait_ge(f_out, 256 * l + 256)
                sp.wait_ge(og_cp, BASE + 16 * l)
                for k in range(4):
                    sp.dma_start(fall[32 * k:32 * k + 32, :, :],
                                 modes[:, :, 2 * (k % 2) + k // 2, :].rearrange("s i m -> i s m")
                                 ).then_inc(f_in, 16)
                sp.wait_ge(act_out, 256 * l + 256)
                with sp.Fori(0, NG) as g:
                    for b in range(NB):
                        sp.wait_ge(pe_cv, BASE - RING + 128 * l + 8 * g + b + 1)
                        for dy in range(3):
                            sp.dma_start(img[32 * dy:32 * dy + 32, b % RING],
                                         acts[bass.ds(g, 1), :, 8 * b + dy:8 * b + dy + 8, :].rearrange(
                                             "o (s c) h w -> (o c) s h w", s=4)).then_inc(img_in[b % RING], 16)
            sp.wait_ge(txt_in, BASE + 16)
            sp.wait_ge(h_in, BASE + 16 * 64)

        def stores(pool, n, g):
            pool.wait_ge(ev_a, BASE + 8 * n + 8)
            pool.dma_start(acts[bass.ds(g, 1), :, 1:65, :].rearrange("o p h w -> (o p) (h w)"),
                           anew[:]).then_inc(act_out, 16)
            pool.wait_ge(ev_f, BASE + n + 1)
            pool.dma_start(modes[bass.ds(4 * g, 4)].rearrange("s i c m -> (s i) (c m)"),
                           fout[:]).then_inc(f_out, 16)
            pool.wait_ge(act_out, 16 * n + 16)
            pool.sem_inc(acts_stored, 1)
            pool.wait_ge(f_out, 16 * n + 16)
            pool.sem_inc(modes_stored, 1)

        @block.gpsimd
        def _(pool):
            pool.memset(zt[:], 0.0).then_inc(pad_zero, 1)
            with pool.Fori(0, NG) as g:
                stores(pool, g, g)

            def mix_copies(l):
                pool.wait_ge(w_neg, BASE + 2 * l + 2)
                pool.wait_ge(pe_yt, BASE + 64 * l + 64)
                pool.memset(wq, 0.0).then_inc(wq_zero, 1)
                pool.wait_ge(wq_zero, BASE + l + 1)
                with pool.Fori(0, 8) as i:
                    for u in range(2):
                        q = 2 * i + u
                        pool.wait_ge(pe_mix, BASE + 16 * l + 2 * i)
                        for mh in range(2):
                            p = slice(64 * mh, 64 * mh + 64)
                            pool.tensor_copy(wq[p, u, :, p].rearrange("p m o -> p o m"),
                                             wall[p, :, bass.ds(8 * q, 8)]).then_inc(wq_cp, 1)

            for l in range(3):
                mix_copies(l)
                with pool.Fori(0, NG) as g:
                    stores(pool, 16 * l + g + 16, g)
            mix_copies(3)

        @block.scalar
        def _(act):
            act.wait_ge(consts_in, BASE + 12 * 16)

            def xt_copy(n, b):
                act.wait_ge(pe_xt, BASE + 8 * n + b + 1)
                if b >= 2:
                    act.wait_ge(pe_s1, BASE + 8 * n + b - 1)
                else:
                    act.wait_ge(pe_s1, BASE + 8 * n)
                act.activation(xt[:, b % 2], pb[(b + 1) % 2][:], ACT.Copy).then_inc(ev_xt, 1)

            with act.Fori(0, NG // 2) as i:
                for u in range(2):
                    n = 2 * i + u
                    for b in range(NB):
                        xt_copy(n, b)

            def conv_evac(n, m, b):
                act.wait_ge(pe_cv, BASE + 8 * m + b + 1)
                if b >= 2:
                    act.wait_ge(ev_a, BASE + 8 * n + b - 1)
                else:
                    act.wait_ge(ev_a, BASE + 8 * n)
                act.activation(vtmp[:, b % 2], pa[b % 2][:], ACT.Identity,
                               bias=conv_b_l).then_inc(ev_v, 1)

            for l in range(4):
                conv_b_l = conv_b[:, l:l + 1]
                act.wait_ge(w_in, BASE + 128 * (l + 1))
                for mh in range(2):
                    p0 = 64 * mh + 32
                    act.mul(wall[p0:p0 + 32, 0:32, :], wall[p0:p0 + 32, 0:32, :], -1.0).then_inc(w_neg, 1)
                with act.Fori(0, 8) as i:
                    for u in range(2):
                        q = 2 * i + u
                        act.wait_ge(pe_mix, BASE + 16 * l + q + 1)
                        act.activation(fall[:, :, bass.ds(8 * q, 8)].rearrange("p s m -> p m s"),
                                       pa[u][:].rearrange("p (m s) -> p m s", m=8),
                                       ACT.Copy).then_inc(ev_mix, 1)
                with act.Fori(0, NG // 2) as i:
                    for u in range(2):
                        g = 2 * i + u
                        m = 16 * l + g
                        n = m + 16
                        act.wait_ge(ev_mix, BASE + 16 * l + 16)
                        act.wait_ge(pe_ot, BASE + m)
                        act.activation(og[:], fall[:, bass.ds(4 * g, 4), :], ACT.Copy).then_inc(og_cp, 1)
                        if l < 3:
                            for b in range(NB):
                                conv_evac(n, m, b)
                                if b >= 1:
                                    xt_copy(n, b - 1)
                            xt_copy(n, NB - 1)
                        else:
                            for b in range(NB + 1):
                                if b < NB:
                                    conv_evac(n, m, b)
                                if b >= 1:
                                    k = 8 * g + b - 1
                                    act.wait_ge(pe_q1, BASE + k + 1)
                                    act.wait_ge(ev_q1l, BASE + k)
                                    act.activation(xt[:, 0].rearrange("p a b -> p (a b)"),
                                                   pb[1][:].rearrange("p a b -> p (a b)"), ACT.Identity,
                                                   bias=q1_b[:]).then_inc(ev_q1, 1)
                                    act.wait_ge(pe_q2, BASE + k + 1)
                                    if b == 1:
                                        act.wait_ge(h_in, BASE + 64 * g)
                                    act.activation(hout2[:, 512 * (b - 1):512 * b], 
                                                   pc[0][:].rearrange("p a b c -> p (a b c)")[0:4],
                                                   ACT.Identity, bias=q2_b[:]).then_inc(ev_q2, 1)
                            act.wait_ge(ev_q2, BASE + 8 * g + 8)
                            for s in range(4):
                                act.dma_start(H[0:64, bass.ds(4 * g + s, 1), :],
                                              hout2[s:s + 1, :].rearrange("p (h w) -> p h w", w=64)
                                              ).then_inc(h_in, 16)

            act.wait_ge(act_out, 16 * 64)
            act.wait_ge(f_out, 16 * 64)

        def q_leaky(dve, k):
            dve.wait_ge(ev_q1, BASE + k + 1)
            dve.wait_ge(pe_q2, BASE + k)
            t = xt[:, 0].rearrange("p a b -> p (a b)")
            dve.scalar_tensor_tensor(xt[:, 1].rearrange("p a b -> p (a b)"), t, 0.01, t,
                                     ALU.mult, ALU.max).then_inc(ev_q1l, 1)

        @block.vector
        def _(dve):
            dve.wait_ge(consts_in, BASE + 12 * 16)
            dve.wait_ge(pad_zero, BASE + 1)

            def s1_evac(n, k):
                dve.wait_ge(pe_s1, BASE + 8 * n + 2 * k + 2)
                if k == 0:
                    dve.wait_ge(pe_yt, BASE + 4 * n)
                dve.tensor_copy(y1[:, :, :, 16 * k:16 * k + 16].rearrange("p y c h -> p h y c"),
                                pc[k % 2][:]).then_inc(ev_s1, 1)

            def second_half(n):
                for q in range(4):
                    dve.wait_ge(pe_yt, BASE + 4 * n + q + 1)
                    if q >= 2:
                        dve.wait_ge(pe_f, BASE + 4 * n + q - 1)
                    else:
                        dve.wait_ge(pe_f, BASE + 4 * n)
                    dve.tensor_copy(y1t[:, q % 2], pb[(q + 1) % 2][:]).then_inc(ev_yt, 1)
                dve.wait_ge(pe_f, BASE + 4 * n + 4)
                dve.wait_ge(modes_stored, BASE + n)
                dve.tensor_copy(fout[:], pf[:].rearrange("p a b c -> p (a b c)")).then_inc(ev_f, 1)

            with dve.Fori(0, NG // 2) as i:
                for u in range(2):
                    n = 2 * i + u
                    dve.wait_ge(acts_stored, BASE + n)
                    dve.wait_ge(pe_xt, BASE + 8 * n)
                    for b in range(NB):
                        dve.wait_ge(pe_lift, BASE + 8 * n + b + 1)
                        dve.tensor_scalar(anew[:, 512 * b:512 * b + 512], pa[b % 2][:], lift_b[:], None, ALU.add).then_inc(ev_a, 1)
                        if b >= 2 and b % 2 == 1:
                            s1_evac(n, (b - 3) // 2)
                    s1_evac(n, 3)
                    second_half(n)

            for l in range(4):
                dve.wait_ge(f_in, BASE + 64 * (l + 1))
                dve.wait_ge(pe_f, BASE + 64 * (l + 1))
                with dve.Fori(0, 8) as i:
                    for u in range(2):
                        q = 2 * i + u
                        dve.wait_ge(pe_mix, BASE + 16 * l + 2 * i)
                        dve.tensor_copy(fq[:, u].rearrange("p m s -> p s m"),
                                        fall[:, :, bass.ds(8 * q, 8)]).then_inc(fq_cp, 1)
                dve.wait_ge(pe_mix, BASE + 16 * (l + 1))
                with dve.Fori(0, NG // 2) as i:
                    for u in range(2):
                        g = 2 * i + u
                        m = 16 * l + g
                        n = m + 16
                        dve.wait_ge(pe_ot, BASE + m + 1)
                        dve.wait_ge(pe_zt, BASE + 4 * m)
                        dve.tensor_copy(ot[:].rearrange("p c (s o) -> p s c o", s=4),
                                        pb[0][:].rearrange("p s (c o) -> p s c o", c=4)).then_inc(ev_ot, 1)
                        for q in range(4):
                            dve.wait_ge(pe_zt, BASE + 4 * m + q + 1)
                            if q == 0:
                                dve.wait_ge(pe_cv, BASE + 8 * m)
                                if l < 3:
                                    dve.wait_ge(pe_yt, BASE + 4 * n)
                            dve.tensor_copy(zt[:, 4 * q:4 * q + 4, :], pb[(q + 1) % 2][:]).then_inc(ev_zt, 1)
                        if l < 3:
                            dve.wait_ge(acts_stored, BASE + n)
                            dve.wait_ge(pe_xt, BASE + 8 * n)
                        else:
                            dve.wait_ge(acts_stored, BASE + 64)
                            dve.wait_ge(pe_q1, BASE + 8 * g)
                        for b in range(NB):
                            dve.wait_ge(ev_v, BASE + 8 * m + b + 1)
                            v = vtmp[:, b % 2]
                            dve.scalar_tensor_tensor(anew[:, 512 * b:512 * b + 512], v, 0.01, v,
                                                     ALU.mult, ALU.max).then_inc(ev_a, 1)
                            if l < 3:
                                if b >= 2 and b % 2 == 1:
                                    s1_evac(n, (b - 3) // 2)
                            elif b >= 1:
                                q_leaky(dve, 8 * g + b - 1)
                        if l < 3:
                            s1_evac(n, 3)
                            second_half(n)
                        else:
                            q_leaky(dve, 8 * g + 7)

        @block.tensor
        def _(pe):
            pe.wait_ge(consts_in, BASE + 12 * 16)

            def transposes(n, u, b, in_conv):
                pe.wait_ge(ev_a, BASE + 8 * n + b + 1)
                if b >= 2:
                    pe.wait_ge(ev_xt, BASE + 8 * n + b - 1)
                elif in_conv is None:
                    pe.wait_ge(ev_yt, BASE + 4 * n)
                else:
                    pe.wait_ge(ev_zt, BASE + 4 * in_conv + 3 + b)
                for k in range(4):
                    t = 4 * b + k
                    mm = pe.transpose(pb[(b + 1) % 2][:, k, :], anew[:, 128 * t:128 * t + 128], ident[:])
                mm.then_inc(pe_xt, 1)

            def along_w(n, b):
                pe.wait_ge(ev_xt, BASE + 8 * n + b + 1)
                k2 = b // 2
                if b % 2 == 0:
                    if k2 >= 2:
                        pe.wait_ge(ev_s1, BASE + 4 * n + k2 - 1)
                    else:
                        pe.wait_ge(ev_s1, BASE + 4 * n)
                for k in range(4):
                    r = 2 * (4 * (b % 2) + k)
                    mm = pe.matmul(pc[k2 % 2][:, r:r + 2].rearrange("p a b c -> p (a b c)"), xt[:, b % 2, k, :], dft_w[:], start=True, stop=True)
                mm.then_inc(pe_s1, 1)

            def along_h(n):
                pe.wait_ge(ev_s1, BASE + 4 * n + 4)

                def yt(q):
                    if q < 2:
                        pe.wait_ge(ev_xt, BASE + 8 * n + 7 + q)
                    else:
                        pe.wait_ge(ev_yt, BASE + 4 * n + q - 1)
                    for k in range(4):
                        mm = pe.transpose(pb[(q + 1) % 2][:, k, :],
                                          y1[:, 4 * q + k].rearrange("p c h -> p (c h)"), ident[:])
                    mm.then_inc(pe_yt, 1)

                def fm(q):
                    pe.wait_ge(ev_yt, BASE + 4 * n + q + 1)
                    if q == 0:
                        pe.wait_ge(ev_f, BASE + n)
                    for k in range(4):
                        mm = pe.matmul(pf[:, :, :, 4 * q + k], y1t[:, q % 2, k, :], dft_h[:],
                                       start=True, stop=True)
                    mm.then_inc(pe_f, 1)

                yt(0)
                for q in range(1, 4):
                    yt(q)
                    fm(q - 1)
                fm(3)

            with pe.Fori(0, NG // 2) as i:
                for u in range(2):
                    n = 2 * i + u
                    pe.wait_ge(x_in[u], BASE + 32 * i + 32)
                    for b in range(NB):
                        if b < 2:
                            pe.wait_ge(ev_a, BASE + 8 * n)
                        else:
                            pe.wait_ge(ev_a, BASE + 8 * n + b - 1)
                        pe.matmul(pa[b % 2][:], lift_w[:], x5[u][:, 512 * b:512 * b + 512],
                                  start=True, stop=True).then_inc(pe_lift, 1)
                        if b >= 1:
                            transposes(n, u, b - 1, None)
                        if b >= 2:
                            along_w(n, b - 2)
                    transposes(n, u, NB - 1, None)
                    along_w(n, NB - 2)
                    along_w(n, NB - 1)
                    along_h(n)

            for l in range(4):
                with pe.Fori(0, 8) as i:
                    for u in range(2):
                        q = 2 * i + u
                        if l == 0:
                            pe.wait_ge(ev_a, BASE + 8 * NG)
                        else:
                            pe.wait_ge(ev_v, BASE + 128 * l)
                        pe.wait_ge(ev_mix, BASE + 16 * l + 2 * i)
                        pe.wait_ge(wq_cp, BASE + 32 * l + 2 * q + 2)
                        pe.wait_ge(fq_cp, BASE + 16 * l + q + 1)
                        for j in range(8):
                            mm = pe.matmul(pa[u][:, 64 * j:64 * j + 64], wq[:, u, j, :], fq[:, u, j, :],
                                           start=True, stop=True)
                        mm.then_inc(pe_mix, 1)
                pe.wait_ge(cw_in, BASE + 16 * (l + 1))
                with pe.Fori(0, NG // 2) as i:
                    for u in range(2):
                        g = 2 * i + u
                        m = 16 * l + g
                        n = m + 16
                        pe.wait_ge(og_cp, BASE + m + 1)
                        if l < 3:
                            pe.wait_ge(ev_yt, BASE + 4 * n)
                        else:
                            pe.wait_ge(ev_yt, BASE + 4 * 64)
                            pe.wait_ge(ev_zt, BASE + 4 * m)
                        for s in range(4):
                            mm = pe.transpose(pb[0][:, s, :], og[:, s, :], ident[:])
                        mm.then_inc(pe_ot, 1)
                        pe.wait_ge(ev_ot, BASE + m + 1)
                        if l == 3:
                            pe.wait_ge(ev_q1, BASE + 8 * g)
                        for q in range(4):
                            if q >= 2:
                                pe.wait_ge(ev_zt, BASE + 4 * m + q - 1)
                            for k in range(4):
                                for t in range(4):
                                    mm = pe.matmul(pb[(q + 1) % 2][:, k, :], inv_h[:, t, 4 * q + k, :],
                                                   ot[:, t, :], start=(t == 0), stop=(t == 3))
                            mm.then_inc(pe_zt, 1)
                        pe.wait_ge(ev_mix, BASE + 16 * l + 16)
                        for b in range(NB + 1):
                            if b < NB:
                                if b >= 2:
                                    pe.wait_ge(ev_v, BASE + 8 * m + b - 1)
                                else:
                                    pe.wait_ge(ev_v, BASE + 8 * m)
                                acc = pa[b % 2]
                                pe.wait_ge(img_in[b % RING], BASE + 48 * (2 * m + b // RING + 1))
                                for dx, to, fr in ((1, slice(0, 64), slice(0, 64)), (0, slice(1, 64), slice(0, 63)),
                                                   (2, slice(0, 63), slice(1, 64))):
                                    for s in range(4):
                                        out = acc[32 * s:32 * s + 32, :].rearrange("p (h w) -> p h w", w=64)
                                        pe.matmul(out[:, :, to], conv_w[:, dx, :], img[:, b % RING, s, :, fr],
                                                  start=(dx == 1), stop=False, skip_group_check=True)
                                pe.wait_ge(ev_zt, BASE + 4 * m + (b // 2) + 1)
                                for k in range(2):
                                    mm = pe.matmul(acc[:, 256 * k:256 * k + 256], zt[:, 2 * b + k, :], inv_w[:],
                                                   start=False, stop=True, skip_group_check=True)
                                mm.then_inc(pe_cv, 1)
                            if l < 3:
                                if b >= 1:
                                    transposes(n, u, b - 1, m)
                                if b >= 2:
                                    along_w(n, b - 2)
                            elif b >= 1:
                                k = 8 * g + b - 1
                                pe.wait_ge(ev_a, BASE + 8 * n + b)
                                pe.wait_ge(ev_q1, BASE + k)
                                pe.wait_ge(ev_zt, BASE + 4 * m + 4)
                                pe.matmul(pb[1][:].rearrange("p a b -> p (a b)"), q1_w[:],
                                          anew[:, 512 * (b - 1):512 * b], start=True, stop=True
                                          ).then_inc(pe_q1, 1)
                                pe.wait_ge(ev_q1l, BASE + k + 1)
                                pe.wait_ge(ev_q2, BASE + k)
                                pe.matmul(pc[0][:].rearrange("p a b c -> p (a b c)")[0:4], q2_w[:],
                                          xt[:, 1].rearrange("p a b -> p (a b)"), start=True, stop=True
                                          ).then_inc(pe_q2, 1)
                        if l < 3:
                            along_w(n, NB - 1)
                            along_h(n)


def build_attention0(nc, d, H):
    with Stage(nc) as ctx:
        def sb(name, shape):
            return ctx.enter_context(nc.sbuf_tensor(f"a0_{name}", shape, F32))

        def sem(name):
            return ctx.sem(f"a0_{name}")

        psum = [ctx.enter_context(nc.psum_tensor(f"a0_ps{k}", [128, 512], F32)) for k in range(8)]
        norm = Norm(ctx, nc, "a0n")
        att = Attention(ctx, nc, "a0a", psum)
        ident, wqk, wv = sb("ident", [128, 128]), sb("wqk", [E + 1, 8, 128]), sb("wv", [E + 1, 512])
        bu = sb("bu", [T, E])
        consts_in, link_dve = sem("consts_in"), sem("link_dve")
        proj_done, proj_ready = sem("proj_done"), sem("proj_ready")
        block = ctx.block()
        per = Norm.LINKS + att.links + 2

        @block.sync
        def _(sp):
            for dst, src in ((ident[:], d["ident"]), (wqk[:], d["a0_wqk"]), (wv[:], d["a0_wv"]),
                             (bu[:], d["a0_bu"]), (att.wo[:], d["a0_wu"]), (att.mask[:], d["mask_strict"])):
                sp.dma_start(dst, src).then_inc(consts_in, 16)

        @block.tensor
        def _(pe):
            pe.wait_ge(consts_in, 6 * 16)
            with pe.Fori(0, NG) as n:
                norm.tensor(pe, n, att.Y, ident)
                pe.wait_ge(norm.xt_ready, n + 1)
                for j in range(12):
                    if j >= 4:
                        pe.wait_ge(proj_ready, 12 * n + j - 3)
                    if j < 8:
                        mm = pe.matmul(psum[j % 4][:, 0:TG], wqk[:, j, :], norm.xt[:], start=True, stop=True)
                    else:
                        s = j - 8
                        mm = pe.matmul(psum[j % 4][0:T, :], norm.xt[:, T * s:T * s + T], wv[:],
                                       start=True, stop=True)
                    mm.then_inc(proj_done, 1)
                pe.wait_ge(proj_ready, 12 * n + 12)
                att.tensor(pe, n, ident)

        @block.scalar
        def _(act):
            with act.Fori(0, NG) as n:
                norm.scalar(act, n, att.Y)
                for j in range(12):
                    act.wait_ge(proj_done, 12 * n + j + 1)
                    if j < 8:
                        dst = (att.qt, att.kt)[j // 4][:, j % 4, :]
                        act.activation(dst, psum[j % 4][:, 0:TG], ACT.Copy).then_inc(proj_ready, 1)
                    else:
                        act.activation(att.v[:, j - 8, :], psum[j % 4][0:T, :], ACT.Copy).then_inc(proj_ready, 1)
                att.scalar(act, n)

        @block.vector
        def _(dve):
            setup = Link(dve, link_dve, 0, 2)
            norm.pads(dve, setup)
            dve.wait_ge(consts_in, 6 * 16)
            with dve.Fori(0, NG) as n:
                link = Link(dve, link_dve, n, per, first=2)
                norm.vector(dve, link, group_of(H, n), n)
                att.vector(dve, link, n)
                h = group_of(H, n)
                dve.wait_ge(att.y_done, n + 1)
                link(dve.tensor_tensor(h, h, att.Y[0:T, 0:G * E].rearrange("p (s e) -> p s e", s=G), ALU.add))
                link(dve.tensor_tensor(h, h, bu[:].unsqueeze(1).to_broadcast([T, G, E]), ALU.add))
                link.done()


class Router:

    PAD, MARK = -1e30, -3e38

    def __init__(self, ctx, nc, tag, experts):
        def sb(name, shape):
            return ctx.enter_context(nc.sbuf_tensor(f"{tag}_{name}", shape, F32))

        def sem(name):
            return ctx.sem(f"{tag}_{name}")

        self.x, self.w = experts, experts + 8
        self.val = sb("val", [T, G, self.w])
        self.mark = sb("mark", [T, G, self.w])
        self.top8 = sb("top8", [T, G, 8])
        self.find = sb("find", [T, G, 8])
        self.ex = sb("ex", [T, G, experts])
        self.small = sb("small", [T, 2, G])
        self.spare = sb("spare", [T, 3])
        self.comb = sb("comb", [T, G, 128])
        self.combt = sb("combt", [128, TG])
        self.exp_in, self.exp_out = sem("exp_in"), sem("exp_out")
        self.logits_done = sem("logits_done")
        self.comb_ready, self.comb_turned, self.combt_ready = sem("comb_ready"), sem("comb_turned"), sem("combt_ready")

    def pads(self, dve, link):
        link(dve.memset(self.val[:], self.PAD))
        link(dve.memset(self.find[:], self.PAD))
        link(dve.memset(self.comb[:], 0.0))

    def softmax(self, dve, link, src, count, dst):
        link(dve.tensor_reduce(self.small[:, 0], src, AX.X, ALU.max))
        dve.tensor_tensor(self.ex[:], src, over(self.small[:, 0], self.x), ALU.subtract).then_inc(self.exp_in, 1)
        dve.wait_ge(self.exp_out, count)
        link(dve.tensor_reduce(self.small[:, 1], self.ex[:], AX.X, ALU.add))
        link(dve.reciprocal(self.small[:, 1], self.small[:, 1]))
        link(dve.tensor_tensor(dst, self.ex[:], over(self.small[:, 1], self.x), ALU.mult))

    def exponential(self, act, count):
        act.wait_ge(self.exp_in, count)
        act.activation(self.ex[:], self.ex[:], ACT.Exp).then_inc(self.exp_out, 1)

    def choose(self, dve, link, k):
        dve.memset(self.spare[:, 0:1], 0.0)
        for s in range(G):
            last = dve.max(self.top8[:, s], self.val[:, s])
        link(last)
        link(dve.tensor_copy(self.find[:, :, 0:k], self.top8[:, :, 0:k]))
        dve.memset(self.spare[:, 1:2], 0.0)
        for s in range(G):
            last = dve.match_replace(self.mark[:, s], self.find[:, s], self.val[:, s], self.MARK)
        link(last)
        link(dve.tensor_scalar(self.mark[:], self.mark[:], self.MARK / 2, None, ALU.is_lt))

    def share(self, dve, link, count):
        link(dve.tensor_copy(self.small[:, 0], self.top8[:, :, 0]))
        dve.tensor_tensor(self.ex[:], self.val[:, :, 0:self.x], over(self.small[:, 0], self.x),
                          ALU.subtract).then_inc(self.exp_in, 1)
        dve.wait_ge(self.exp_out, count)
        link(dve.tensor_tensor(self.ex[:], self.ex[:], self.mark[:, :, 0:self.x], ALU.mult))
        link(dve.tensor_reduce(self.small[:, 1], self.ex[:], AX.X, ALU.add))
        link(dve.reciprocal(self.small[:, 1], self.small[:, 1]))
        dve.tensor_tensor(self.comb[:, :, 0:self.x], self.ex[:], over(self.small[:, 1], self.x),
                          ALU.mult).then_inc(self.comb_ready, 1)

    def logits(self, pe, bank, xt, gate):
        for s in range(G):
            mm = pe.matmul(bank[0:T, 16 * s:16 * s + self.x], xt[:, T * s:T * s + T], gate[:],
                           start=True, stop=True)
        mm.then_inc(self.logits_done, 1)

    def turn(self, pe, n, bank, ident):
        pe.wait_ge(self.comb_ready, n + 1)
        for s in range(G):
            mm = pe.transpose(bank[:, T * s:T * s + T], self.comb[:, s, :], ident[0:T, 0:T])
        mm.then_inc(self.comb_turned, 1)

    def turned(self, act, n, bank):
        act.wait_ge(self.comb_turned, n + 1)
        act.activation(self.combt[:], bank[:, 0:TG], ACT.Copy).then_inc(self.combt_ready, 1)


def build_routed_mlp(nc, d, H, tag, experts, capacity):
    BLOCKS = 16
    with Stage(nc) as ctx:
        def sb(name, shape):
            return ctx.enter_context(nc.sbuf_tensor(f"{tag}_{name}", shape, F32))

        def sem(name):
            return ctx.sem(f"{tag}_{name}")

        psum = [ctx.enter_context(nc.psum_tensor(f"{tag}_ps{k}", [128, 512], F32)) for k in range(8)]
        misc, Y, HB, CB, POS = psum[0], psum[1], psum[2:4], psum[4:6], psum[6]
        norm = Norm(ctx, nc, f"{tag}n")
        route = Router(ctx, nc, f"{tag}r", experts)
        ident = sb("ident", [128, 128])
        gate, w1, w2 = sb("gate", [E + 1, experts]), sb("w1", [E + 1, BLOCKS, 128]), sb("w2", [128, BLOCKS, E])
        b2, pick = sb("b2", [experts, E]), sb("pick", [experts, BLOCKS, 128])
        relu, hw = sb("relu", [128, 2, TG]), sb("hw", [128, 2, TG])
        y = sb("y", [T, G, E])
        consts = [(ident, "ident"), (gate, f"{tag}_gate"), (w1, f"{tag}_w1"), (w2, f"{tag}_w2"),
                  (b2, f"{tag}_b2"), (pick, f"{tag}_pick")]
        if capacity is None:
            norm2 = Norm(ctx, nc, f"{tag}m")
            gamma, beta = sb("gamma", [T, E]), sb("beta", [T, E])
            consts += [(gamma, f"{tag}_gamma"), (beta, f"{tag}_beta")]
            per = 2 * Norm.LINKS + 1 + 4 + 4 + 5
        else:
            upto, ones = sb("upto", [T, T]), sb("ones", [T, T])
            before = sb("before", [T, G + 1, experts])
            kept = sb("kept", [T, G, experts])
            fin, fix = sb("fin", [T, G, E]), sb("fix", [T, G, E])
            consts += [(upto, "upto"), (ones, "ones")]
            chosen, placed = sem("chosen"), sem("placed")
            per = Norm.LINKS + 4 + 4 + 3 + 3 + 7
        consts_in, link_dve = sem("consts_in"), sem("link_dve")
        h_done, r_ready, c_done, hw_ready, y_part, y_done = (
            sem("h_done"), sem("r_ready"), sem("c_done"), sem("hw_ready"), sem("y_part"), sem("y_done"))
        block = ctx.block()

        @block.sync
        def _(sp):
            for dst, name in consts:
                sp.dma_start(dst[:], d[name]).then_inc(consts_in, 16)

        @block.tensor
        def _(pe):
            pe.wait_ge(consts_in, 16 * len(consts))

            def hidden(n, e):
                if e >= 2:
                    pe.wait_ge(r_ready, BLOCKS * n + e - 1)
                pe.matmul(HB[e % 2][:, 0:TG], w1[:, e, :], norm.xt[:], start=True, stop=True).then_inc(h_done, 1)
                if e == 0:
                    pe.wait_ge(route.combt_ready, n + 1)
                if e >= 2:
                    pe.wait_ge(hw_ready, BLOCKS * n + e - 1)
                pe.matmul(CB[e % 2][:, 0:TG], pick[:, e, :], route.combt[0:experts, :],
                          start=True, stop=True).then_inc(c_done, 1)

            def output(n, e):
                pe.wait_ge(hw_ready, BLOCKS * n + e + 1)
                for s in range(G):
                    mm = pe.matmul(Y[0:T, E * s:E * s + E], hw[:, e % 2, T * s:T * s + T], w2[:, e, :],
                                   start=(e == 0 and s == 0), stop=False, skip_group_check=True)
                mm.then_inc(y_part, 1)

            with pe.Fori(0, NG) as n:
                norm.tensor(pe, n, misc, ident)
                pe.wait_ge(norm.xt_ready, n + 1)
                route.logits(pe, misc, norm.xt, gate)
                if capacity is not None:
                    pe.wait_ge(chosen, n + 1)
                    for s in range(G):
                        out = POS[0:T, 16 * s:16 * s + experts]
                        pe.matmul(out, ones[:], before[:, s, :], start=True, stop=False)
                        mm = pe.matmul(out, upto[:], route.mark[:, s, 0:experts], start=False, stop=True)
                    mm.then_inc(placed, 1)
                route.turn(pe, n, misc, ident)
                for e in range(BLOCKS + 1):
                    if e < BLOCKS:
                        hidden(n, e)
                    if e >= 1:
                        output(n, e - 1)
                for s in range(G):
                    mm = pe.matmul(Y[0:T, E * s:E * s + E], route.combt[0:experts, T * s:T * s + T], b2[:],
                                   start=False, stop=True, skip_group_check=True)
                mm.then_inc(y_done, 1)

        @block.scalar
        def _(act):
            with act.Fori(0, NG) as n:
                norm.scalar(act, n, misc)
                route.exponential(act, n + 1)
                route.turned(act, n, misc)
                for e in range(BLOCKS):
                    act.wait_ge(h_done, BLOCKS * n + e + 1)
                    if e >= 2:
                        act.wait_ge(hw_ready, BLOCKS * n + e - 1)
                    act.activation(relu[:, e % 2], HB[e % 2][:, 0:TG], ACT.Relu).then_inc(r_ready, 1)
                if capacity is None:
                    act.wait_ge(norm2.var_ready, n + 1)
                    act.activation(norm2.st[:, 3], norm2.st[:, 2], ACT.Sqrt).then_inc(norm2.std_ready, 1)

        @block.vector
        def _(dve):
            first = 5 + (0 if capacity is None else 1)
            setup = Link(dve, link_dve, 0, first)
            norm.pads(dve, setup)
            route.pads(dve, setup)
            if capacity is not None:
                setup(dve.memset(before[:], 0.0))
            setup.done()
            dve.wait_ge(consts_in, 16 * len(consts))
            with dve.Fori(0, NG) as n:
                link = Link(dve, link_dve, n, per, first)
                h = group_of(H, n)
                norm.vector(dve, link, h, n)
                dve.wait_ge(route.logits_done, n + 1)
                logits = misc[0:T, 0:16 * G].rearrange("p (s x) -> p s x", s=G)[:, :, 0:experts]
                if capacity is None:
                    link(dve.tensor_copy(route.val[:, :, 0:experts], logits))
                    route.choose(dve, link, 2)
                    route.share(dve, link, n + 1)
                else:
                    route.softmax(dve, link, logits, n + 1, route.val[:, :, 0:experts])
                    route.choose(dve, link, 1)
                    mark = route.mark[:, :, 0:experts]
                    for s in range(G):
                        ins = dve.tensor_tensor(before[:, s + 1], before[:, s], mark[:, s], ALU.add)
                        if s < G - 1:
                            link(ins)
                    ins.then_inc(chosen, 1)
                    dve.wait_ge(placed, n + 1)
                    dve.wait_ge(chosen, n + 1)
                    link(dve.tensor_copy(before[:, 0], before[:, G]))
                    pos = POS[0:T, 0:16 * G].rearrange("p (s x) -> p s x", s=G)[:, :, 0:experts]
                    link(dve.tensor_scalar(kept[:], pos, float(capacity), None, ALU.is_le))
                    link(dve.tensor_tensor(kept[:], kept[:], mark, ALU.mult))
                    dve.tensor_tensor(route.comb[:, :, 0:experts], kept[:], route.val[:, :, 0:experts],
                                      ALU.mult).then_inc(route.comb_ready, 1)
                for e in range(BLOCKS):
                    dve.wait_ge(r_ready, BLOCKS * n + e + 1)
                    dve.wait_ge(c_done, BLOCKS * n + e + 1)
                    if e >= 2:
                        dve.wait_ge(y_part, BLOCKS * n + e - 1)
                    dve.tensor_tensor(hw[:, e % 2], relu[:, e % 2], CB[e % 2][:, 0:TG], ALU.mult).then_inc(hw_ready, 1)
                dve.wait_ge(y_done, n + 1)
                moe = Y[0:T, 0:G * E].rearrange("p (s e) -> p s e", s=G)
                if capacity is None:
                    link(dve.tensor_tensor(y[:], norm.xn[:, :, 0:E], moe, ALU.add))
                    norm2.moments(dve, link, y[:], norm2.var_ready)
                    dve.wait_ge(norm2.std_ready, n + 1)
                    link(dve.reciprocal(norm2.st[:, 4], norm2.st[:, 3]))
                    link(dve.tensor_tensor(y[:], norm2.xc[:], over(norm2.st[:, 4], E), ALU.mult))
                    link(dve.tensor_tensor(y[:], y[:], gamma[:].unsqueeze(1).to_broadcast([T, G, E]), ALU.mult))
                    link(dve.tensor_tensor(y[:], y[:], beta[:].unsqueeze(1).to_broadcast([T, G, E]), ALU.add))
                else:
                    link(dve.tensor_copy(y[:], moe))
                    link(dve.tensor_scalar(fix[:], y[:], -1e4, 1e4, ALU.max, ALU.min))
                    link(dve.tensor_tensor(fin[:], y[:], y[:], ALU.is_equal))
                    link(dve.tensor_tensor(fix[:], fix[:], fin[:], ALU.mult))
                    link(dve.tensor_scalar(fin[:], y[:], 0.0, 0.0, ALU.mult, ALU.is_equal))
                    dve.memset(route.spare[:, 2:3], 0.0)
                    link(dve.copy_predicated(fix[:], fin[:].bitcast(mybir.dt.int32), y[:]))
                out = y if capacity is None else fix
                link(dve.tensor_tensor(h, h, out[:], ALU.add))
                link.done()


def build_mlp0(nc, d, H):
    build_routed_mlp(nc, d, H, "f0", 16, None)


def build_mlp1(nc, d, H):
    tokens = S * T
    build_routed_mlp(nc, d, H, "f1", 8, -(-tokens * 5 // (4 * 8)))


def build_linear_attention(nc, d, H):
    with Stage(nc) as ctx:
        def sb(name, shape):
            return ctx.enter_context(nc.sbuf_tensor(f"l1_{name}", shape, F32))

        def sem(name):
            return ctx.sem(f"l1_{name}")

        psum = [ctx.enter_context(nc.psum_tensor(f"l1_ps{k}", [128, 512], F32)) for k in range(6)]
        misc, QK, VB, EB, LB, OB = psum
        norm = Norm(ctx, nc, "l1n")
        ident = sb("ident", [128, 128])
        wq, wk, wv = sb("wq", [E + 1, E]), sb("wk", [E + 1, E]), sb("wv", [E + 1, E])
        gamma, beta = sb("gamma", [E, 1]), sb("beta", [E, 1])
        qall = sb("qall", [E, NG, TG])
        lam, cen = sb("lam", [E, S, E]), sb("cen", [E, S, E])
        ek, etok, vtok = sb("ek", [E, G, T]), sb("etok", [T, G, E]), sb("vtok", [T, G, E])
        top, den = sb("top", [E, G]), sb("den", [E, G])
        bn = sb("bn", [E, 8])
        qg = sb("qg", [E, TG])
        consts = [(ident, "ident"), (wq, "l1_wq"), (wk, "l1_wk"), (wv, "l1_wv"), (gamma, "l1_gamma"),
                  (beta, "l1_beta")]
        consts_in, link_dve = sem("consts_in"), sem("link_dve")
        k_done, q_done, q_ready, v_done, v_ready = (
            sem("k_done"), sem("q_done"), sem("q_ready"), sem("v_done"), sem("v_ready"))
        e_in, e_out, e_turned, etok_ready, lam_done = (
            sem("e_in"), sem("e_out"), sem("e_turned"), sem("etok_ready"), sem("lam_done"))
        h_done = sem("h_done")
        bvar_ready, bstd_ready, bn_ready, qg_ready, o_done = (
            sem("bvar_ready"), sem("bstd_ready"), sem("bn_ready"), sem("qg_ready"), sem("o_done"))
        start_at_base(nc, [h_done, o_done])
        block = ctx.block()
        per = Norm.LINKS + 1 + 1 + 1 + 1
        bn_links = 9

        @block.sync
        def _(sp):
            for dst, name in consts:
                sp.dma_start(dst[:], d[name]).then_inc(consts_in, 16)

        @block.tensor
        def _(pe):
            pe.wait_ge(consts_in, 16 * len(consts))
            with pe.Fori(0, NG) as n:
                norm.tensor(pe, n, misc, ident)
                pe.wait_ge(norm.xt_ready, n + 1)
                for s in range(G):
                    mm = pe.matmul(VB[0:T, E * s:E * s + E], norm.xt[:, T * s:T * s + T], wv[:], start=True, stop=True)
                mm.then_inc(v_done, 1)
                pe.matmul(QK[0:E, 0:TG], wk[:], norm.xt[:], start=True, stop=True).then_inc(k_done, 1)
                pe.wait_ge(e_out, n + 1)
                pe.matmul(LB[0:E, 0:TG], wq[:], norm.xt[:], start=True, stop=True).then_inc(q_done, 1)
                for s in range(G):
                    mm = pe.transpose(EB[0:T, E * s:E * s + E], ek[:, s, :], ident[0:E, 0:E])
                mm.then_inc(e_turned, 1)
                pe.wait_ge(etok_ready, n + 1)
                pe.wait_ge(v_ready, n + 1)
                pe.wait_ge(q_ready, n + 1)
                for s in range(G):
                    mm = pe.matmul(LB[0:E, E * s:E * s + E], etok[:, s, :], vtok[:, s, :], start=True, stop=True)
                mm.then_inc(lam_done, 1)
            with pe.Fori(0, NG) as n:
                pe.wait_ge(bn_ready, 1)
                pe.wait_ge(qg_ready, n + 1)
                pe.wait_ge(h_done, BASE + n)
                for s in range(G):
                    mm = pe.matmul(OB[0:T, E * s:E * s + E], qg[:, T * s:T * s + T],
                                   lam[:, bass.ds(G * n + s, 1), :], start=True, stop=True)
                mm.then_inc(o_done, 1)

        @block.scalar
        def _(act):
            with act.Fori(0, NG) as n:
                norm.scalar(act, n, misc)
                act.wait_ge(v_done, n + 1)
                act.activation(vtok[:], VB[0:T, 0:G * E].rearrange("p (s e) -> p s e", s=G), ACT.Copy).then_inc(v_ready, 1)
                act.wait_ge(e_in, n + 1)
                act.activation(ek[:], ek[:], ACT.Exp).then_inc(e_out, 1)
                act.wait_ge(q_done, n + 1)
                act.activation(qall[:, bass.ds(n, 1), :].rearrange("p o t -> p (o t)"), LB[0:E, 0:TG], ACT.Copy).then_inc(q_ready, 1)
                act.wait_ge(e_turned, n + 1)
                act.activation(etok[:], EB[0:T, 0:G * E].rearrange("p (s e) -> p s e", s=G), ACT.Copy).then_inc(etok_ready, 1)
            act.wait_ge(bvar_ready, 1)
            act.activation(bn[:, 3:4], bn[:, 2:3], ACT.Sqrt).then_inc(bstd_ready, 1)
            with act.Fori(0, NG) as n:
                act.wait_ge(o_done, BASE + n)
                act.wait_ge(q_ready, NG)
                act.activation(qg[:], qall[:, bass.ds(n, 1), :].rearrange("p o t -> p (o t)"), ACT.Copy).then_inc(qg_ready, 1)

        @block.vector
        def _(dve):
            setup = Link(dve, link_dve, 0, 2)
            norm.pads(dve, setup)
            dve.wait_ge(consts_in, 16 * len(consts))
            with dve.Fori(0, NG) as n:
                link = Link(dve, link_dve, n, per, 2)
                norm.vector(dve, link, group_of(H, n), n)
                keys = QK[0:E, 0:TG].rearrange("p (s t) -> p s t", s=G)
                dve.wait_ge(k_done, n + 1)
                link(dve.tensor_reduce(top[:], keys, AX.X, ALU.max))
                dve.tensor_tensor(ek[:], keys, over(top[:], T), ALU.subtract).then_inc(e_in, 1)
                dve.wait_ge(e_out, n + 1)
                link(dve.tensor_reduce(den[:], ek[:], AX.X, ALU.add))
                link(dve.reciprocal(den[:], den[:]))
                dve.wait_ge(lam_done, n + 1)
                link(dve.tensor_tensor(lam[:, bass.ds(G * n, G), :],
                                       LB[0:E, 0:G * E].rearrange("p (s e) -> p s e", s=G),
                                       over(den[:], E), ALU.mult))
                link.done()
            link = Link(dve, link_dve, NG, per, 2)
            size = 1.0 / (S * E)
            flat = lam[:].rearrange("p s e -> p (s e)")
            cflat = cen[:].rearrange("p s e -> p (s e)")
            link(dve.tensor_reduce(bn[:, 0:1], flat, AX.X, ALU.add))
            link(dve.tensor_scalar(bn[:, 0:1], bn[:, 0:1], size, None, ALU.mult))
            link(dve.tensor_scalar(flat, flat, bn[:, 0:1], None, ALU.subtract))
            link(dve.tensor_tensor(cflat, flat, flat, ALU.mult))
            link(dve.tensor_reduce(bn[:, 1:2], cflat, AX.X, ALU.add))
            dve.tensor_scalar(bn[:, 2:3], bn[:, 1:2], size, EPS, ALU.mult, ALU.add).then_inc(bvar_ready, 1)
            dve.wait_ge(bstd_ready, 1)
            link(dve.reciprocal(bn[:, 4:5], bn[:, 3:4]))
            link(dve.tensor_tensor(bn[:, 5:6], bn[:, 4:5], gamma[:], ALU.mult))
            dve.tensor_scalar(flat, flat, bn[:, 5:6], beta[:], ALU.mult, ALU.add).then_inc(bn_ready, 1)
            with dve.Fori(0, NG) as n:
                h = group_of(H, n)
                dve.wait_ge(o_done, BASE + n + 1)
                dve.tensor_tensor(h, h, OB[0:T, 0:G * E].rearrange("p (s e) -> p s e", s=G), ALU.add).then_inc(h_done, 1)
                dve.wait_ge(h_done, BASE + n + 1)


def build_gauss_attention(nc, d, H):
    with Stage(nc) as ctx:
        def sb(name, shape):
            return ctx.enter_context(nc.sbuf_tensor(f"a2_{name}", shape, F32))

        def sem(name):
            return ctx.sem(f"a2_{name}")

        psum = [ctx.enter_context(nc.psum_tensor(f"a2_ps{k}", [128, 512], F32)) for k in range(8)]
        norm = Norm(ctx, nc, "a2n")
        att = Attention(ctx, nc, "a2a", psum, gauss=True)
        ident, wqk, wv = sb("ident", [128, 128]), sb("wqk", [E + 1, 8, 128]), sb("wv", [E + 1, 512])
        scale = sb("scale", [T, E])
        consts = [(ident, "ident"), (wqk, "a2_wqk"), (wv, "a2_wv"), (scale, "a2_scale"),
                  (att.wo, "a2_wo"), (att.gamma, "a2_gamma"), (att.ones, "ones128")]
        consts_in, link_dve = sem("consts_in"), sem("link_dve")
        proj_done, proj_ready = sem("proj_done"), sem("proj_ready")
        block = ctx.block()
        per = Norm.LINKS + 1 + att.links + 1

        @block.sync
        def _(sp):
            for dst, name in consts:
                sp.dma_start(dst[:], d[name]).then_inc(consts_in, 16)

        @block.tensor
        def _(pe):
            pe.wait_ge(consts_in, 16 * len(consts))
            with pe.Fori(0, NG) as n:
                norm.tensor(pe, n, att.Y, ident)
                pe.wait_ge(norm.xt_ready, n + 1)
                for j in range(12):
                    if j >= 4:
                        pe.wait_ge(proj_ready, 12 * n + j - 3)
                    if j < 8:
                        mm = pe.matmul(psum[j % 4][:, 0:TG], wqk[:, j, :], norm.xt[:], start=True, stop=True)
                    else:
                        s = j - 8
                        mm = pe.matmul(psum[j % 4][0:T, :], norm.xt[:, T * s:T * s + T], wv[:],
                                       start=True, stop=True)
                    mm.then_inc(proj_done, 1)
                pe.wait_ge(proj_ready, 12 * n + 12)
                att.tensor(pe, n, ident)

        @block.scalar
        def _(act):
            with act.Fori(0, NG) as n:
                norm.scalar(act, n, att.Y)
                for j in range(12):
                    act.wait_ge(proj_done, 12 * n + j + 1)
                    bank = psum[j % 4]
                    if j < 4:
                        act.activation(att.q2[:, j, :], bank[:, 0:TG], ACT.Square)
                        act.activation(att.qt[:, j, :], bank[:, 0:TG], ACT.Copy).then_inc(proj_ready, 1)
                    elif j < 8:
                        act.activation(att.k2[:, j - 4, :], bank[:, 0:TG], ACT.Square)
                        act.activation(att.kt[:, j - 4, :], bank[:, 0:TG], ACT.Copy, scale=-2.0).then_inc(proj_ready, 1)
                    else:
                        act.activation(att.v[:, j - 8, :], bank[0:T, :], ACT.Copy).then_inc(proj_ready, 1)
                att.scalar(act, n)

        @block.vector
        def _(dve):
            setup = Link(dve, link_dve, 0, 2)
            norm.pads(dve, setup)
            dve.wait_ge(consts_in, 16 * len(consts))
            with dve.Fori(0, NG) as n:
                link = Link(dve, link_dve, n, per, first=2)
                norm.vector(dve, link, group_of(H, n), n, scale)
                att.vector(dve, link, n)
                h = group_of(H, n)
                dve.wait_ge(att.y_done, n + 1)
                link(dve.tensor_tensor(h, h, att.Y[0:T, 0:G * E].rearrange("p (s e) -> p s e", s=G), ALU.add))
                link.done()


def build_mlp2(nc, d, H):
    UNITS, X = 5, 4
    with Stage(nc) as ctx:
        def sb(name, shape):
            return ctx.enter_context(nc.sbuf_tensor(f"f2_{name}", shape, F32))

        def sem(name):
            return ctx.sem(f"f2_{name}")

        psum = [ctx.enter_context(nc.psum_tensor(f"f2_ps{k}", [128, 512], F32)) for k in range(8)]
        misc, Y, H1, H2, CB = psum[0], psum[1], psum[2:4], psum[4:6], psum[6:8]
        norm = Norm(ctx, nc, "f2n")
        route = Router(ctx, nc, "f2r", X)
        ident, gate = sb("ident", [128, 128]), sb("gate", [E + 1, X])
        w1, w2, b2 = sb("w1", [E + 1, UNITS, 128]), sb("w2", [128, UNITS, 128]), sb("b2", [128, UNITS])
        w3, b3, pick = sb("w3", [128, UNITS, E]), sb("b3", [UNITS, E]), sb("pick", [UNITS, UNITS, 128])
        r1, r2, hw = sb("r1", [128, 2, TG]), sb("r2", [128, 2, TG]), sb("hw", [128, 2, TG])
        consts = [(ident, "ident"), (gate, "f2_gate"), (w1, "f2_w1"), (w2, "f2_w2"), (b2, "f2_b2"),
                  (w3, "f2_w3"), (b3, "f2_b3"), (pick, "f2_pick")]
        consts_in, link_dve = sem("consts_in"), sem("link_dve")
        h1_done, r1_ready, h2_done, r2_ready = sem("h1_done"), sem("r1_ready"), sem("h2_done"), sem("r2_ready")
        c_done, hw_ready, y_part, y_done = sem("c_done"), sem("hw_ready"), sem("y_part"), sem("y_done")
        block = ctx.block()
        per = Norm.LINKS + 4 + 4 + 4 + 1
        first = 6

        @block.sync
        def _(sp):
            for dst, name in consts:
                sp.dma_start(dst[:], d[name]).then_inc(consts_in, 16)

        @block.tensor
        def _(pe):
            pe.wait_ge(consts_in, 16 * len(consts))
            with pe.Fori(0, NG) as n:
                norm.tensor(pe, n, misc, ident)
                pe.wait_ge(norm.xt_ready, n + 1)
                route.logits(pe, misc, norm.xt, gate)
                route.turn(pe, n, misc, ident)
                for e in range(UNITS + 2):
                    base = UNITS * n
                    if e < UNITS:
                        if e >= 2:
                            pe.wait_ge(r1_ready, base + e - 1)
                        pe.matmul(H1[e % 2][:, 0:TG], w1[:, e, :], norm.xt[:], start=True, stop=True).then_inc(h1_done, 1)
                    if 1 <= e <= UNITS:
                        k = e - 1
                        pe.wait_ge(r1_ready, base + k + 1)
                        if k >= 2:
                            pe.wait_ge(r2_ready, base + k - 1)
                            pe.wait_ge(hw_ready, base + k - 1)
                        pe.matmul(H2[k % 2][:, 0:TG], w2[:, k, :], r1[:, k % 2], start=True, stop=True).then_inc(h2_done, 1)
                        if k == 0:
                            pe.wait_ge(route.combt_ready, n + 1)
                        pe.matmul(CB[k % 2][:, 0:TG], pick[:, k, :], route.combt[0:UNITS, :],
                                  start=True, stop=True).then_inc(c_done, 1)
                    if e >= 2:
                        k = e - 2
                        pe.wait_ge(hw_ready, base + k + 1)
                        for s in range(G):
                            mm = pe.matmul(Y[0:T, E * s:E * s + E], hw[:, k % 2, T * s:T * s + T], w3[:, k, :],
                                           start=(k == 0 and s == 0), stop=False, skip_group_check=True)
                        mm.then_inc(y_part, 1)
                for s in range(G):
                    mm = pe.matmul(Y[0:T, E * s:E * s + E], route.combt[0:UNITS, T * s:T * s + T], b3[:],
                                   start=False, stop=True, skip_group_check=True)
                mm.then_inc(y_done, 1)

        @block.scalar
        def _(act):
            act.wait_ge(consts_in, 16 * len(consts))
            with act.Fori(0, NG) as n:
                norm.scalar(act, n, misc)
                route.exponential(act, 2 * n + 1)
                route.exponential(act, 2 * n + 2)
                route.turned(act, n, misc)
                for e in range(UNITS + 1):
                    base = UNITS * n
                    if e < UNITS:
                        act.wait_ge(h1_done, base + e + 1)
                        if e >= 2:
                            act.wait_ge(h2_done, base + e - 1)
                        act.activation(r1[:, e % 2], H1[e % 2][:, 0:TG], ACT.Relu).then_inc(r1_ready, 1)
                    if e >= 1:
                        k = e - 1
                        act.wait_ge(h2_done, base + k + 1)
                        if k >= 2:
                            act.wait_ge(hw_ready, base + k - 1)
                        act.activation(r2[:, k % 2], H2[k % 2][:, 0:TG], ACT.Relu, bias=b2[:, k:k + 1]).then_inc(r2_ready, 1)

        @block.vector
        def _(dve):
            setup = Link(dve, link_dve, 0, first)
            norm.pads(dve, setup)
            route.pads(dve, setup)
            setup(dve.memset(route.comb[:, :, X:X + 1], 1.0))
            setup.done()
            dve.wait_ge(consts_in, 16 * len(consts))
            with dve.Fori(0, NG) as n:
                link = Link(dve, link_dve, n, per, first)
                h = group_of(H, n)
                norm.vector(dve, link, h, n)
                dve.wait_ge(route.logits_done, n + 1)
                logits = misc[0:T, 0:16 * G].rearrange("p (s x) -> p s x", s=G)[:, :, 0:X]
                route.softmax(dve, link, logits, 2 * n + 1, route.val[:, :, 0:X])
                route.choose(dve, link, 2)
                route.share(dve, link, 2 * n + 2)
                for e in range(UNITS):
                    dve.wait_ge(r2_ready, UNITS * n + e + 1)
                    dve.wait_ge(c_done, UNITS * n + e + 1)
                    if e >= 2:
                        dve.wait_ge(y_part, UNITS * n + e - 1)
                    dve.tensor_tensor(hw[:, e % 2], r2[:, e % 2], CB[e % 2][:, 0:TG], ALU.mult).then_inc(hw_ready, 1)
                dve.wait_ge(y_done, n + 1)
                link(dve.tensor_tensor(h, h, Y[0:T, 0:G * E].rearrange("p (s e) -> p s e", s=G), ALU.add))
                link.done()


def build_diff_attention(nc, d, H):
    CH = 16
    NC = T // CH
    PER = 2 * NC
    with Stage(nc) as ctx:
        def sb(name, shape):
            return ctx.enter_context(nc.sbuf_tensor(f"a3_{name}", shape, F32))

        def sem(name):
            return ctx.sem(f"a3_{name}")

        psum = [ctx.enter_context(nc.psum_tensor(f"a3_ps{k}", [128, 512], F32)) for k in range(8)]
        misc, QP, KP, VB, A, PT = psum[0], psum[1], psum[2], psum[3], psum[4:6], psum[6:8]
        norm = Norm(ctx, nc, "a3n")
        ident = sb("ident", [128, 128])
        wq, wk, wv = sb("wq", [E, E]), sb("wk", [E, E]), sb("wv", [E, E])
        wm, bm = sb("wm", [128, 4]), sb("bm", [T, 1])
        qp, kp, vt = sb("qp", [128, 2, T]), sb("kp", [128, 2, T]), sb("vt", [T, G, E])
        diff = sb("diff", [128, 2, CH, T])
        sc = sb("sc", [T, 2, 4, T])
        pt = sb("pt", [T, 2, 4, T])
        sums = sb("sums", [T, 2, 2, 4])
        consts = [(ident, "ident"), (wq, "a3_wq"), (wk, "a3_wk"), (wv, "a3_wv"), (wm, "a3_wm"), (bm, "a3_bm")]
        consts_in, link_dve = sem("consts_in"), sem("link_dve")
        q_done, k_done, v_done, qk_ready, v_ready = sem("q_done"), sem("k_done"), sem("v_done"), sem("qk_ready"), sem("v_ready")
        sub_done, relu_done, chunk_done = sem("sub_done"), sem("relu_done"), sem("chunk_done")
        sc_ready, exp_done, p_ready, pt_done, pt_ready, o_done = (
            sem("sc_ready"), sem("exp_done"), sem("p_ready"), sem("pt_done"), sem("pt_ready"), sem("o_done"))
        block = ctx.block()
        per = Norm.LINKS + 2 * 2 + 2 * 2 + 1

        @block.sync
        def _(sp):
            for dst, name in consts:
                sp.dma_start(dst[:], d[name]).then_inc(consts_in, 16)

        @block.tensor
        def _(pe):
            pe.wait_ge(consts_in, 16 * len(consts))
            with pe.Fori(0, NG) as n:
                norm.tensor(pe, n, misc, ident)
                pe.wait_ge(norm.xt_ready, n + 1)
                x = norm.xt
                for s in range(G):
                    mm = pe.matmul(VB[0:T, E * s:E * s + E], x[0:E, T * s:T * s + T], wv[:], start=True, stop=True)
                mm.then_inc(v_done, 1)
                for bank, w, done in ((QP, wq, q_done), (KP, wk, k_done)):
                    for s in range(G):
                        p = slice(64 * (s % 2), 64 * (s % 2) + 64)
                        mm = pe.matmul(bank[p, T * (s // 2):T * (s // 2) + T], w[:], x[0:E, T * s:T * s + T],
                                       start=True, stop=True, skip_group_check=True)
                    mm.then_inc(done, 1)
                for pair in range(2):
                    for c in range(NC):
                        pe.wait_ge(relu_done, PER * n + NC * pair + c + 1)
                        for k in range(CH):
                            key = CH * c + k
                            mm = pe.matmul(A[pair][0:T, 4 * key:4 * key + 4], diff[:, c % 2, k, :], wm[:],
                                           start=True, stop=True)
                        mm.then_inc(chunk_done, 1)
                for pair in range(2):
                    pe.wait_ge(p_ready, 2 * n + pair + 1)
                    if pair == 0:
                        pe.wait_ge(v_ready, n + 1)
                    for k in range(4):
                        mm = pe.transpose(PT[pair][0:T, T * k:T * k + T], sc[:, pair, k, :], ident[0:T, 0:T])
                    mm.then_inc(pt_done, 1)
                for pair in range(2):
                    pe.wait_ge(pt_ready, 2 * n + pair + 1)
                    for k in range(4):
                        s, g = 2 * pair + k // 2, k % 2
                        out = misc[0:T, E * s:E * s + E].rearrange("p (e g) -> p g e", g=2)[:, g, :]
                        mm = pe.matmul(out, pt[:, pair, k, :], vt[:, s, 32 * g:32 * g + 32], start=True, stop=True)
                mm.then_inc(o_done, 1)

        @block.scalar
        def _(act):
            with act.Fori(0, NG) as n:
                norm.scalar(act, n, misc)
                act.wait_ge(q_done, n + 1)
                act.activation(qp[:].rearrange("p a t -> p (a t)"), QP[:, 0:2 * T], ACT.Copy)
                act.wait_ge(k_done, n + 1)
                act.activation(kp[:].rearrange("p a t -> p (a t)"), KP[:, 0:2 * T], ACT.Copy).then_inc(qk_ready, 1)
                act.activation(vt[:].rearrange("p s e -> p (s e)"), VB[0:T, 0:G * E], ACT.Copy).then_inc(v_ready, 1)
                for c in range(PER):
                    act.wait_ge(sub_done, PER * n + c + 1)
                    act.activation(diff[:, c % 2], diff[:, c % 2], ACT.Relu).then_inc(relu_done, 1)
                for pair in range(2):
                    act.wait_ge(sc_ready, 2 * n + pair + 1)
                    act.activation(sc[:, pair], sc[:, pair], ACT.Exp).then_inc(exp_done, 1)
                for pair in range(2):
                    act.wait_ge(pt_done, 2 * n + pair + 1)
                    act.activation(pt[:, pair].rearrange("p k t -> p (k t)"), PT[pair][0:T, 0:4 * T],
                                   ACT.Copy).then_inc(pt_ready, 1)

        @block.vector
        def _(dve):
            setup = Link(dve, link_dve, 0, 2)
            norm.pads(dve, setup)
            dve.wait_ge(consts_in, 16 * len(consts))
            with dve.Fori(0, NG) as n:
                link = Link(dve, link_dve, n, per, first=2)
                h = group_of(H, n)
                norm.vector(dve, link, h, n)
                dve.wait_ge(qk_ready, n + 1)
                for pair in range(2):
                    for c in range(NC):
                        k = NC * pair + c
                        if k >= 2:
                            dve.wait_ge(chunk_done, PER * n + k - 1)
                        q = qp[:, pair].unsqueeze(1).to_broadcast([128, CH, T])
                        dve.tensor_tensor(diff[:, k % 2], q, over(kp[:, pair, CH * c:CH * c + CH], T),
                                          ALU.subtract).then_inc(sub_done, 1)
                for pair in range(2):
                    dve.wait_ge(chunk_done, PER * n + NC * (pair + 1))
                    dst = sc[:, pair]
                    src = A[pair][0:T, 0:4 * T].rearrange("p (k c) -> p c k", c=4)
                    link(dve.tensor_scalar(dst, src, bm[:], 0.0, ALU.add, ALU.max))
                    link(dve.tensor_reduce(sums[:, pair, 0], dst, AX.X, ALU.max))
                    dve.tensor_tensor(dst, dst, over(sums[:, pair, 0], T), ALU.subtract).then_inc(sc_ready, 1)
                for pair in range(2):
                    dst, den = sc[:, pair], sums[:, pair, 1]
                    dve.wait_ge(exp_done, 2 * n + pair + 1)
                    link(dve.tensor_reduce(den, dst, AX.X, ALU.add))
                    link(dve.reciprocal(den, den))
                    dve.tensor_tensor(dst, dst, over(den, T), ALU.mult).then_inc(p_ready, 1)
                    dve.wait_ge(p_ready, 2 * n + pair + 1)
                dve.wait_ge(o_done, n + 1)
                link(dve.tensor_tensor(h, h, misc[0:T, 0:G * E].rearrange("p (s e) -> p s e", s=G), ALU.add))
                link.done()


def build_product_keys(nc, d, H):
    TOP, HALF = 16, 64
    NT = HALF * HALF // 128
    SHIFT = -40.0
    counts = [TOP // (a + 1) for a in range(TOP // 2)]
    starts = [sum(counts[:a]) for a in range(TOP // 2)]
    NCAND = sum(counts) + TOP // 2
    with Stage(nc) as ctx:
        def sb(name, shape, dtype=F32):
            return ctx.enter_context(nc.sbuf_tensor(f"pk_{name}", shape, dtype))

        def sem(name):
            return ctx.sem(f"pk_{name}")

        psum = [ctx.enter_context(nc.psum_tensor(f"pk_ps{k}", [128, 512], F32)) for k in range(8)]
        SC, KV, KT, misc = psum[0:4], psum[4:6], psum[6], psum[7]
        QUERY, SCORES, RANK, RANK_END, TURN, PER_TILE = 0, (1, 4), 7, 52, (55, 59), 2
        norm = Norm(ctx, nc, "pkn")
        att = Attention(ctx, nc, "pka", psum)
        ident = sb("ident", [128, 128])
        wpk, wq, kbd = sb("wpk", [E, 4, 128]), sb("wq", [E, 4, 128]), sb("kbd", [128, 4, 256])
        sel = sb("sel", [128, NT, 128], BF16)
        piece = sb("piece", [128, 2, 3, TG], BF16)
        rest, idle = sb("rest", [128, TG]), sb("idle", [128, 2])
        selw = sb("selw", [128, 512])
        qpk = sb("qpk", [128, 4, TG])
        qs = sb("qs", [128, 4, T])
        sim = sb("sim", [T, HEADS, 2, HALF])
        left = sb("left", [T, HEADS, 2, HALF])
        t16 = sb("t16", [T, HEADS, 2, TOP])
        cand, cleft, c16 = sb("cand", [T, HEADS, NCAND]), sb("cleft", [T, HEADS, NCAND]), sb("c16", [T, HEADS, TOP])
        size = sb("size", [T, HEADS, 2, 2])
        thr, spare = sb("thr", [T, 4, HEADS]), sb("spare", [T, 6])
        cexp = sb("cexp", [T, HEADS, TOP])
        rsum = sb("rsum", [T, HEADS])
        rden, next_rden = sb("rden", [T, G, HEADS]), sb("next_rden", [T, G, HEADS])
        shift = sb("shift", [128, 1])
        st, next_st, next_qt = sb("st", [128, HEADS, TG]), sb("next_st", [128, HEADS, TG]), sb("next_qt", [128, 4, TG])
        table = sb("table", [128, 2, NT, 128])
        ex, wt = sb("ex", [128, 4, TG]), sb("wt", [128, 4, TG])
        kvs = sb("kvs", [128, TG])
        ktok = sb("ktok", [T, G, 512])
        consts = [(ident, "ident"), (wpk, "pk_wpk"), (wq, "pk_wq"), (kbd, "pk_kbd"),
                  (att.wo, "pk_wo"), (att.mask, "mask_causal")]
        consts_in, link_dve = sem("consts_in"), sem("link_dve")
        proj_done, proj_ready = sem("proj_done"), sem("proj_ready")
        sim_done, sim_ready, simt_ready, st_done, st_ready = (
            sem("sim_done"), sem("sim_ready"), sem("simt_ready"), sem("st_done"), sem("st_ready"))
        sel_in, sel_ready = sem("sel_in"), sem("sel_ready")
        piece_ready, link_pool, carried = sem("piece_ready"), sem("link_pool"), sem("carried")
        qs_ready, link_rank, link_att = sem("qs_ready"), sem("link_rank"), sem("link_att")
        den_in, den_out, rden_ready = sem("den_in"), sem("den_out"), sem("rden_ready")
        table_in = [sem(f"table_in{u}") for u in range(2)]
        sc_done, ex_ready, wt_ready, kv_step = sem("sc_done"), sem("ex_ready"), sem("wt_ready"), sem("kv_step")
        kvs_ready, kvt_done, kvn_ready = sem("kvs_ready"), sem("kvt_done"), sem("kvn_ready")
        kt_done, kt_ready = sem("kt_done"), sem("kt_ready")
        start_at_base(nc, [kvs_ready, carried])
        block = ctx.block()
        RANK_LINKS = 3 + 1 + 3 + 4 + 3

        @block.sync
        def _(sp):
            for dst, name in consts:
                sp.dma_start(dst[:], d[name]).then_inc(consts_in, 16)

            for k in range(NT * 128 // 512):
                if k >= 1:
                    sp.wait_ge(sel_ready, k)
                sp.dma_start(selw[:], d["pk_sel"][:, 4 * k:4 * k + 4, :].rearrange("p t k -> p (t k)")).then_inc(sel_in, 16)

            def load(h):
                sp.dma_start(table[:, h % 2], d["pk_table"][h]).then_inc(table_in[h % 2], 16)

            def next_pair(n, pair):
                for u in range(2):
                    sp.wait_ge(kv_step, 256 * n + 64 * pair + 32 * (u + 1))
                    load((2 * pair + 2 + u) % HEADS)

            load(0)
            load(1)
            with sp.Fori(0, NG - 1) as n:
                for pair in range(4):
                    next_pair(n, pair)
            for pair in range(3):
                next_pair(NG - 1, pair)

        @block.gpsimd
        def _(pool):
            for k in range(NT * 128 // 512):
                pool.wait_ge(sel_in, 16 * (k + 1))
                pool.tensor_copy(sel[:, 4 * k:4 * k + 4, :].rearrange("p t k -> p (t k)"), selw[:]).then_inc(sel_ready, 1)
            pool.memset(idle[:], 0.0).then_inc(link_pool, 1)
            pool.wait_ge(link_pool, 1)

            def carry(m):
                pool.wait_ge(st_ready, 2 * G * m + 2 * G)
                pool.wait_ge(rden_ready, G * m + G)
                take_wait()
                pool.tensor_copy(st[:], next_st[:])
                pool.tensor_copy(rden[:], next_rden[:])
                pool.tensor_copy(att.qt[:], next_qt[:]).then_inc(carried, 1)
                pool.wait_ge(carried, BASE + m + 1)

            def take_wait():
                pool.tensor_tensor(idle[:, 0:1], idle[:, 1:2], idle[:, 1:2], ALU.add)

            def pieces(n):
                link = Link(pool, link_pool, n, 4 * HEADS, first=1)
                for h in range(HEADS):
                    u, now = h % 2, st[:, h, :]
                    pool.wait_ge(kvs_ready, BASE + HEADS * n + h - 1)
                    take_wait()
                    link(pool.tensor_copy(piece[:, u, 0], now))
                    link(pool.tensor_tensor(rest[:], now, piece[:, u, 0], ALU.subtract))
                    take_wait()
                    link(pool.tensor_copy(piece[:, u, 1], rest[:]))
                    link(pool.tensor_tensor(piece[:, u, 2], rest[:], piece[:, u, 1], ALU.subtract))
                    pool.sem_inc(piece_ready, 1)

            carry(0)
            with pool.Fori(0, NG - 1) as n:
                pieces(n)
                pool.wait_ge(att.s_done, G * n + G)
                carry(n + 1)
            pieces(NG - 1)

        @block.tensor
        def _(pe):
            pe.wait_ge(consts_in, 16 * len(consts))
            pe.wait_ge(sel_ready, NT * 128 // 512)

            def sample_steps(k):
                pe.wait_ge(qs_ready, k + 1)
                for p in range(2):
                    if p == 1:
                        pe.wait_ge(sim_ready, 2 * k + 1)
                    for t in range(2):
                        mm = pe.matmul(misc[0:T, 256 * t:256 * t + 256], qs[:, 2 * p + t, :], kbd[:, 2 * p + t, :],
                                       start=True, stop=True)
                    mm.then_inc(sim_done, 1)
                    yield
                for p in range(2):
                    if p == 0:
                        pe.wait_ge(simt_ready, k + 1)
                    else:
                        pe.wait_ge(st_ready, 2 * k + 1)
                    for h in range(4):
                        mm = pe.transpose(misc[:, T * h:T * h + T],
                                          sim[:, 4 * p + h].rearrange("p a b -> p (a b)"), ident[0:T, 0:T])
                    mm.then_inc(st_done, 1)
                    yield

            def project(m):
                norm.tensor(pe, m, misc, ident)
                pe.wait_ge(norm.xt_ready, m + 1)
                for j in range(8):
                    if j >= 4:
                        pe.wait_ge(proj_ready, 8 * m + j - 3)
                    w = (wpk, wq)[j // 4]
                    pe.matmul(psum[j % 4][:, 0:TG], w[:, j % 4, :], norm.xt[0:E, :], start=True,
                              stop=True).then_inc(proj_done, 1)

            def head_table(n, hh, u, steps):
                base = 256 * n + 64 * hh + 32 * u
                pe.wait_ge(piece_ready, HEADS * n + 2 * hh + u + 1)
                pe.wait_ge(table_in[u], 64 * n + 16 * hh + 16)
                for t in range(NT + 2):
                    if t < NT:
                        if t >= 4:
                            pe.wait_ge(wt_ready, base + t - 3)
                        for q in range(3):
                            mm = pe.matmul(SC[t % 4][:, 0:TG], sel[:, t, :], piece[:, u, q], start=(q == 0),
                                           stop=(q == 2))
                        mm.then_inc(sc_done, 1)
                    if t >= 2:
                        k = t - 2
                        pe.wait_ge(wt_ready, base + k + 1)
                        mm = pe.matmul(KV[u][:, 0:TG], table[:, u, k, :], wt[:, k % 4], start=(k == 0),
                                       stop=(k == NT - 1))
                        mm.then_inc(kv_step, 1)
                    if u == 1 and t == 8:
                        turn_kv(n, hh, 0)
                    if NT * u + t in SCORES + TURN and t < NT:
                        next(steps, None)

            def turn_kv(n, hh, u):
                pe.wait_ge(kvs_ready, BASE + HEADS * n + 2 * hh + u + 1)
                if u == 1:
                    pe.wait_ge(kvn_ready, HEADS * n + 2 * hh + 1)
                for s in range(G):
                    mm = pe.transpose(KT[0:T, 128 * s:128 * s + 128], kvs[:, T * s:T * s + T], ident[:])
                mm.then_inc(kvt_done, 1)

            def heads_and_attention(n, ahead):
                with pe.Fori(0, HEADS // 2) as hh:
                    pe.wait_ge(proj_ready, 8 * n + (16 if ahead else 8))
                    steps = sample_steps(G * n + G + hh) if ahead else iter(())
                    for u in range(2):
                        head_table(n, hh, u, steps)
                    turn_kv(n, hh, 1)
                    pe.wait_ge(kvn_ready, HEADS * n + 2 * hh + 2)
                for s in range(G):
                    if s >= 1:
                        pe.wait_ge(kt_ready, G * n + s)
                    for j in range(4):
                        mm = pe.transpose(KT[:, T * j:T * j + T], ktok[:, s, 128 * j:128 * j + 128], ident[0:T, 0:T])
                    mm.then_inc(kt_done, 1)
                pe.wait_ge(kt_ready, G * n + G)
                pe.wait_ge(carried, BASE + n + 1)
                att.tensor(pe, n, ident)

            project(0)
            with pe.Fori(0, G) as s:
                for _ in sample_steps(s):
                    pass
            pe.wait_ge(st_ready, 2 * G)
            with pe.Fori(0, NG - 1) as n:
                project(n + 1)
                heads_and_attention(n, True)
            heads_and_attention(NG - 1, False)

        @block.scalar
        def _(act):
            def project(m):
                norm.scalar(act, m, misc)
                act.wait_ge(carried, BASE + m)
                for j in range(8):
                    act.wait_ge(proj_done, 8 * m + j + 1)
                    dst = (qpk, next_qt)[j // 4]
                    act.activation(dst[:, j % 4, :], psum[j % 4][:, 0:TG], ACT.Copy).then_inc(proj_ready, 1)

            def sample_steps(m, s):
                k = G * m + s
                act.wait_ge(proj_ready, 8 * m + 8)
                act.activation(qs[:], qpk[:, :, bass.ds(T * s, T)], ACT.Copy).then_inc(qs_ready, 1)
                yield
                for p in range(2):
                    act.wait_ge(sim_done, 2 * k + p + 1)
                    act.activation(sim[:, :, p, :], misc[0:T, :].rearrange("q (h k) -> q h k", h=HEADS),
                                   ACT.Copy).then_inc(sim_ready, 1)
                    yield
                act.wait_ge(den_in, k + 1)
                act.activation(cexp[:], c16[:], ACT.Exp, bias=shift[0:T]).then_inc(den_out, 1)
                yield
                for b in range(2):
                    act.wait_ge(st_done, 2 * k + b + 1)
                    act.activation(next_st[:, 4 * b:4 * b + 4, bass.ds(T * s, T)],
                                   misc[:, 0:4 * T].rearrange("p (h t) -> p h t", h=4), ACT.Copy
                                   ).then_inc(st_ready, 1)
                    yield

            def heads_and_attention(n, ahead):
                with act.Fori(0, HEADS // 2) as hh:
                    steps = sample_steps(n + 1, hh) if ahead else iter(())
                    for u in range(2):
                        base = 256 * n + 64 * hh + 32 * u
                        for t in range(NT):
                            act.wait_ge(sc_done, base + t + 1)
                            if t >= 4:
                                act.wait_ge(wt_ready, base + t - 3)
                            act.activation(ex[:, t % 4], SC[t % 4][:, 0:TG], ACT.Exp,
                                           bias=shift[:]).then_inc(ex_ready, 1)
                            if NT * u + t - 1 in (QUERY - 1, ) + SCORES + (RANK_END, ) + TURN:
                                next(steps, None)
                        act.wait_ge(kv_step, base + NT)
                        act.activation(kvs[:], KV[u][:, 0:TG], ACT.Copy).then_inc(kvs_ready, 1)
                for s in range(G):
                    act.wait_ge(kt_done, G * n + s + 1)
                    act.activation(att.kt[:, :, T * s:T * s + T], KT[:, 0:4 * T].rearrange("p (j t) -> p j t", j=4),
                                   ACT.Copy).then_inc(kt_ready, 1)
                att.scalar(act, n)

            project(0)
            with act.Fori(0, G) as s:
                for _ in sample_steps(0, s):
                    pass
            with act.Fori(0, NG - 1) as n:
                project(n + 1)
                heads_and_attention(n, True)
            heads_and_attention(NG - 1, False)

        @block.vector
        def _(dve):
            setup = Link(dve, link_dve, 0, 3)
            norm.pads(dve, setup)
            setup(dve.memset(shift[:], SHIFT))
            dve.wait_ge(consts_in, 16 * len(consts))

            def top16(link, k, rows):
                dve.memset(spare[:, k:k + 1], 0.0)
                for i, (v, _, best) in enumerate(rows):
                    last = dve.max(best[:, 0:8], v)
                    if i % PER_TILE == 1 and i < len(rows) - 1:
                        yield
                link.mark(last)
                yield
                link.wait()
                dve.memset(spare[:, k + 1:k + 2], 0.0)
                for i, (v, rest, best) in enumerate(rows):
                    last = dve.match_replace(rest, best[:, 0:8], v, -3e38)
                    if i % PER_TILE == 1 and i < len(rows) - 1:
                        yield
                link.mark(last)
                yield
                link.wait()
                dve.memset(spare[:, k + 2:k + 3], 0.0)
                for i, (_, rest, best) in enumerate(rows):
                    last = dve.max(best[:, 8:16], rest)
                    if i % PER_TILE == 1 and i < len(rows) - 1:
                        yield
                link.mark(last)
                yield
                link.wait()

            def threshold_steps(m, s):
                k = G * m + s
                link = Link(dve, link_rank, k, RANK_LINKS)
                dve.wait_ge(sim_ready, 2 * k + 2)
                yield from top16(link, 0, [(sim[:, h, p], left[:, h, p], t16[:, h, p]) for h in range(HEADS)
                                           for p in range(2)])
                for a, (at, c) in enumerate(zip(starts, counts)):
                    dve.tensor_tensor(cand[:, :, at:at + c], t16[:, :, 1, 0:c],
                                      t16[:, :, 0, a:a + 1].to_broadcast([T, HEADS, c]), ALU.add)
                    if a % PER_TILE == 1:
                        yield
                at = sum(counts)
                link.mark(dve.tensor_tensor(cand[:, :, at:NCAND], t16[:, :, 0, TOP // 2:TOP],
                                            t16[:, :, 1, 0:1].to_broadcast([T, HEADS, TOP // 2]), ALU.add))
                yield
                link.wait()
                yield from top16(link, 3, [(cand[:, h], cleft[:, h], c16[:, h]) for h in range(HEADS)])
                ends = t16[:].rearrange("t h p k -> t (h p) k")[:, :, 0:TOP:TOP - 1]
                link.mark(dve.scalar_tensor_tensor(size[:].rearrange("t h p x -> t (h p) x"), ends, -1.0, ends,
                                                   ALU.mult, ALU.max))
                yield
                link.wait()
                link.mark(dve.tensor_reduce(thr[:, 0], size[:], AX.XY, ALU.add))
                yield
                link.wait()
                dve.tensor_scalar(thr[:, 2], c16[:, :, 0], -87.0, None, ALU.add)
                link.mark(dve.scalar_tensor_tensor(thr[:, 1], thr[:, 0], -1e-6, c16[:, :, TOP - 1], ALU.mult, ALU.add))
                yield
                link.wait()
                link.mark(dve.tensor_tensor(thr[:, 3], thr[:, 1], thr[:, 2], ALU.max))
                yield
                link.wait()
                dve.tensor_tensor(sim[:, :, 0, :], sim[:, :, 0, :], over(thr[:, 3], HALF),
                                  ALU.subtract).then_inc(simt_ready, 1)
                dve.tensor_tensor(c16[:], c16[:], over(thr[:, 3], TOP), ALU.subtract).then_inc(den_in, 1)
                yield
                yield
                yield
                dve.wait_ge(simt_ready, k + 1)
                dve.wait_ge(den_out, k + 1)
                link.mark(dve.scalar_tensor_tensor(cexp[:], c16[:], 0.0, cexp[:], ALU.is_ge, ALU.mult))
                yield
                link.wait()
                link.mark(dve.tensor_reduce(rsum[:], cexp[:], AX.X, ALU.add))
                yield
                link.wait()
                link.mark(dve.reciprocal(rsum[:], rsum[:]))
                yield
                link.wait()
                dve.tensor_copy(next_rden[:, bass.ds(s, 1), :].rearrange("t o h -> t (o h)"), rsum[:]
                                ).then_inc(rden_ready, 1)
                yield
                dve.wait_ge(rden_ready, k + 1)

            def keys_values(n, hh, u):
                dve.wait_ge(kvt_done, HEADS * n + 2 * hh + u + 1)
                dve.wait_ge(carried, BASE + n + 1)
                r = rden[:, :, bass.ds(2 * hh + u, 1)].to_broadcast([T, G, E])
                kv = KT[0:T, :].rearrange("p (s f) -> p s f", s=G)
                c = bass.ds(128 * hh + 64 * u, E)
                dve.tensor_tensor(ktok[:, :, c], kv[:, :, 0:E], r, ALU.mult)
                dve.tensor_tensor(att.v[:, :, c], kv[:, :, E:2 * E], r, ALU.mult).then_inc(kvn_ready, 1)

            def heads_and_attention(n, ahead):
                with dve.Fori(0, HEADS // 2) as hh:
                    steps = threshold_steps(n + 1, hh) if ahead else iter(())
                    for u in range(2):
                        base = 256 * n + 64 * hh + 32 * u
                        for t in range(NT):
                            dve.wait_ge(ex_ready, base + t + 1)
                            if t >= 4:
                                dve.wait_ge(kv_step, base + t - 3)
                            dve.scalar_tensor_tensor(wt[:, t % 4], SC[t % 4][:, 0:TG], 0.0, ex[:, t % 4],
                                                     ALU.is_ge, ALU.mult).then_inc(wt_ready, 1)
                            if u == 1 and t == 10:
                                keys_values(n, hh, 0)
                            if NT * u + t >= RANK:
                                next(steps, None)
                    for _ in steps:
                        assert False, "steps left at the end of the pair of heads"
                    keys_values(n, hh, 1)
                link = Link(dve, link_att, n, att.links + 1)
                att.vector(dve, link, n)
                h = group_of(H, n)
                dve.wait_ge(att.y_done, n + 1)
                link(dve.tensor_tensor(h, h, att.Y[0:T, 0:G * E].rearrange("p (s e) -> p s e", s=G), ALU.add))
                link.done()

            def normalise(m):
                link = Link(dve, link_dve, m, Norm.LINKS, 3)
                norm.vector(dve, link, group_of(H, m), m)
                link.done()

            normalise(0)
            with dve.Fori(0, G) as s:
                for _ in threshold_steps(0, s):
                    pass
            with dve.Fori(0, NG - 1) as n:
                normalise(n + 1)
                heads_and_attention(n, True)
            heads_and_attention(NG - 1, False)


def early_fusion_kernel(nc, d, out):
    with ExitStack() as ctx:
        H = ctx.enter_context(nc.sbuf_tensor("H", [96, 64, 64], F32))
        act_out = ctx.enter_context(nc.semaphore("ft_act_out"))
        f_out = ctx.enter_context(nc.semaphore("ft_f_out"))
        build_tokenizer(nc, d, H, act_out, f_out)
        for stage in (build_attention0, build_mlp0, build_linear_attention, build_mlp1, build_gauss_attention,
                      build_mlp2, build_diff_attention, build_product_keys,):
            stage(nc, d, H)
        store_tokens(nc, H, out)


def store_tokens(nc, H, out):
    with ExitStack() as ctx:
        stored = ctx.enter_context(nc.semaphore("stored"))
        block = ctx.enter_context(nc.Block())

        @block.sync
        def _(sp):
            sp.dma_start(out.rearrange("s t e -> t s e"), H[:]).then_inc(stored, 16)
            sp.wait_ge(stored, 16)


def lay_out(inputs):
    d, a = constants(inputs)
    return d


def constants(inputs):
    import numpy as np

    a = {k: np.asarray(v) for k, v in inputs.items()}
    f = np.float32
    d = {"ident": np.eye(128, dtype=f)}
    d["x"] = np.ascontiguousarray(a["x"].reshape(16, 4, 4096, 3).transpose(0, 1, 3, 2)).reshape(16, 12, 4096)
    d["grid"] = np.ascontiguousarray(a["L0_tok_input_grid"].reshape(4096, 2).transpose(1, 0))
    d["txt"] = np.ascontiguousarray(a["txt"].transpose(1, 0, 2))
    lift = np.zeros((14, 128), f)
    for s in range(4):
        lift[3 * s:3 * s + 3, 32 * s:32 * s + 32] = a["L0_tok_P_w"][2:5]
        lift[12:14, 32 * s:32 * s + 32] = a["L0_tok_P_w"][0:2]
    d["lift_w"] = lift
    d["lift_b"] = np.tile(a["L0_tok_P_b"], 4).reshape(128, 1)
    q1 = np.zeros((4, 32, 4, 32), f)
    q2 = np.zeros((4, 32, 4), f)
    for s in range(4):
        q1[s, :, s, :] = a["L0_tok_Q1_w"]
        q2[s, :, s] = a["L0_tok_Q2_w"][:, 0]
    d["conv_w"] = np.ascontiguousarray(a["L0_tok_conv_w"].transpose(0, 3, 2, 4, 1)).reshape(4, 96, 3, 32)
    d["conv_b"] = np.ascontiguousarray(np.tile(a["L0_tok_conv_b"], (1, 4)).transpose(1, 0))
    d["q1_w"] = q1.reshape(128, 128)
    d["q1_b"] = np.tile(a["L0_tok_Q1_b"], 4).reshape(128, 1)
    d["q2_w"] = q2.reshape(128, 4)
    d["q2_b"] = np.tile(a["L0_tok_Q2_b"], 4).reshape(4, 1)
    d["wr"] = a["L0_tok_spec_wr"].reshape(4, 32, 32, 256)
    d["wi"] = a["L0_tok_spec_wi"].reshape(4, 32, 32, 256)

    ang = 2 * np.pi * np.arange(64)[:, None] * np.arange(16)[None, :] / 64
    co, si = np.cos(ang), np.sin(ang)
    dw = np.zeros((2, 64, 2, 16, 2))
    for h in range(2):
        dw[h, :, h, :, 0] = co
        dw[h, :, h, :, 1] = -si
    d["dft_w"] = dw.reshape(128, 64).astype(f)
    dh = np.zeros((2, 64, 2, 16))
    dh[0, :, 0], dh[1, :, 0], dh[0, :, 1], dh[1, :, 1] = co, si, -si, co
    d["dft_h"] = dh.reshape(128, 32).astype(f)
    ih = np.zeros((8, 16, 2, 2, 16, 4, 16, 2))
    for mh in range(2):
        for y in range(16):
            cc = co[:, 8 * mh:8 * mh + 8].T.reshape(8, 16, 4)
            ss = si[:, 8 * mh:8 * mh + 8].T.reshape(8, 16, 4)
            ih[:, y, mh, 0, :, :, y, 0], ih[:, y, mh, 1, :, :, y, 0] = cc, -ss
            ih[:, y, mh, 0, :, :, y, 1], ih[:, y, mh, 1, :, :, y, 1] = ss, cc
    d["inv_h"] = ih.reshape(128, 4, 16, 128).astype(f)
    iw = np.zeros((4, 16, 2, 4, 64))
    weight = np.where(np.arange(16) == 0, 1.0, 2.0)[:, None] / 4096
    for h in range(4):
        iw[h, :, 0, h, :] = co.T * weight
        iw[h, :, 1, h, :] = -si.T * weight
    d["inv_w"] = iw.reshape(128, 256).astype(f)
    def with_bias(w, b):
        return np.concatenate([w, b.reshape(1, -1)], axis=0)

    def rows(x, n=96):
        return np.ascontiguousarray(np.broadcast_to(x, (n,) + x.shape))

    i, j = np.arange(96)[:, None], np.arange(96)[None, :]
    d["mask_strict"] = np.tile(np.where(j >= i, f(NEG), f(0)), (1, 4))
    d["mask_causal"] = np.tile(np.where(j > i, f(NEG), f(0)), (1, 4))

    d["a0_wqk"] = np.concatenate([with_bias(a["L0_attn_Wq"], a["L0_attn_bq"]),
                                  with_bias(a["L0_attn_Wk"], a["L0_attn_bk"])], axis=1).reshape(65, 8, 128)
    d["a0_wv"] = with_bias(a["L0_attn_Wv"], a["L0_attn_bv"])
    d["a0_wu"] = np.ascontiguousarray(a["L0_attn_Wu"].reshape(4, 128, 64).transpose(1, 0, 2))
    d["a0_bu"] = rows(a["L0_attn_bu"])
    d["upto"] = np.triu(np.ones((96, 96), f))
    d["ones"] = np.ones((96, 96), f)

    def routed(tag, gate_w, gate_b, w1, b1, w2, b2):
        x, _, fl = w1.shape
        n = fl // 128
        d[tag + "_gate"] = with_bias(gate_w, gate_b)
        both = np.concatenate([w1, b1.reshape(x, 1, fl)], axis=1)
        d[tag + "_w1"] = np.ascontiguousarray(both.transpose(1, 0, 2)).reshape(65, x * n, 128)
        d[tag + "_w2"] = np.ascontiguousarray(w2.reshape(x * n, 128, 64).transpose(1, 0, 2))
        d[tag + "_b2"] = b2
        d[tag + "_pick"] = np.repeat(np.repeat(np.eye(x, dtype=f), n, axis=1)[:, :, None], 128, axis=2)

    routed("f0", *[a["L0_ffn_" + k] for k in ("gate_w", "gate_b", "w1", "b1", "w2", "b2")])
    d["f0_gamma"], d["f0_beta"] = rows(a["L0_ffn_gamma"]), rows(a["L0_ffn_beta"])
    routed("f1", *[a["L1_ffn_" + k] for k in ("gate_w", "gate_b", "w1", "b1", "w2", "b2")])

    d["l1_wq"] = with_bias(a["L1_attn_W_qk"][0], a["L1_attn_b_qk"][0])
    d["l1_wk"] = with_bias(a["L1_attn_W_qk"][1], a["L1_attn_b_qk"][1])
    d["l1_wv"] = with_bias(a["L1_attn_W_v"], a["L1_attn_b_v"])
    d["l1_gamma"] = a["L1_attn_gamma"].reshape(64, 1)
    d["l1_beta"] = a["L1_attn_beta"].reshape(64, 1)
    zero = np.zeros((512,), f)
    heads = lambda w: np.ascontiguousarray(w.transpose(1, 0, 2)).reshape(64, 512)
    d["a2_wqk"] = np.concatenate([with_bias(heads(a["L2_attn_W_q"]), zero),
                                  with_bias(heads(a["L2_attn_W_k"]), zero)], axis=1).reshape(65, 8, 128)
    d["a2_wv"] = with_bias(heads(a["L2_attn_W_v"]), zero)
    d["a2_wo"] = np.ascontiguousarray(a["L2_attn_W_o"].transpose(1, 0).reshape(4, 128, 64).transpose(1, 0, 2))
    d["a2_scale"] = rows(a["L2_attn_ln_scale"])
    by_parity = a["L2_attn_gamma"].reshape(4, 2).transpose(1, 0)
    d["a2_gamma"] = rows(np.repeat(by_parity[:, :, None], 96, axis=2).reshape(2, 384))
    d["ones128"] = np.ones((128, 96), f)

    d["f2_gate"] = with_bias(a["L2_ffn_gW"], a["L2_ffn_gb"])
    w1, w2, w3 = np.zeros((65, 5, 128), f), np.zeros((128, 5, 128), f), np.zeros((128, 5, 64), f)
    b2, b3, pick = np.zeros((128, 5), f), np.zeros((5, 64), f), np.zeros((5, 5, 128), f)
    w1[:, 0, 0:64] = with_bias(a["L2_ffn_sW1"], a["L2_ffn_sb1"])
    w2[0:64, 0, :], b2[:, 0], w3[:, 0] = a["L2_ffn_sW2"], a["L2_ffn_sb2"], a["L2_ffn_sW3"]
    b3[4], pick[4, 0] = a["L2_ffn_sb3"], 1
    for x in range(4):
        w1[:, x + 1, :] = with_bias(a["L2_ffn_eW1"][x], a["L2_ffn_eb1"][x])
        w2[:, x + 1, 0:64], b2[0:64, x + 1] = a["L2_ffn_eW2"][x], a["L2_ffn_eb2"][x]
        w3[0:64, x + 1], b3[x], pick[x, x + 1] = a["L2_ffn_eW3"][x], a["L2_ffn_eb3"][x], 1
    d["f2_w1"], d["f2_w2"], d["f2_w3"], d["f2_b2"], d["f2_b3"], d["f2_pick"] = w1, w2, w3, b2, b3, pick

    d["a3_wq"] = np.ascontiguousarray(a["L3_attn_Wq"].transpose(1, 0))
    d["a3_wk"] = np.ascontiguousarray(a["L3_attn_Wk"].transpose(1, 0))
    d["a3_wv"] = np.ascontiguousarray(a["L3_attn_Wv"].reshape(32, 2, 64).transpose(2, 1, 0)).reshape(64, 64)
    wm = np.zeros((4, 32, 4), f)
    for k in range(4):
        wm[k, :, k] = a["L3_attn_w_mlp"]
    d["a3_wm"] = wm.reshape(128, 4)
    d["a3_bm"] = rows(a["L3_attn_b_mlp"])
    d["pk_wpk"] = a["L3_ffn_Wq_pk"].reshape(64, 4, 128)
    d["pk_wq"] = a["L3_ffn_Wq"].reshape(64, 4, 128)
    keys = a["L3_ffn_pk_keys"]
    kbd = np.zeros((4, 32, 4, 4, 64), f)
    for t in range(4):
        for k in range(4):
            kbd[k, :, t, k, :] = keys[t // 2, :, 4 * (t % 2) + k, :].transpose(1, 0)
    d["pk_kbd"] = kbd.reshape(128, 4, 256)
    sel = np.zeros((2, 64, 32, 2, 64), f)
    for i in range(64):
        sel[0, i, :, :, i] = 1
        sel[1, i, i // 2, i % 2, :] = 1
    d["pk_sel"] = sel.reshape(128, 32, 128)
    both = np.concatenate([a["L3_ffn_keys_table"], a["L3_ffn_values_table"]], axis=1)
    d["pk_table"] = np.ascontiguousarray(both.reshape(8, 32, 128, 128).transpose(0, 2, 1, 3))
    d["pk_wo"] = np.ascontiguousarray(a["L3_ffn_Wo"].reshape(4, 128, 64).transpose(1, 0, 2))
    return d, a


def kernel(**inputs):
    import numpy as _np
    import concourse.bacc as _bacc
    from concourse import mybir as _mybir
    from concourse.bass_utils import run_bass_kernel_spmd as _run

    nc = _bacc.Bacc("TRN2", target_bir_lowering=False, num_devices=1)
    laid = lay_out(inputs)
    arrays, d = {}, {}
    for name, a in laid.items():
        a = _np.ascontiguousarray(a)
        arrays[f"in_{name}_dram"] = a
        d[name] = nc.dram_tensor(f"in_{name}_dram", a.shape, _mybir.dt.from_np(a.dtype), kind="ExternalInput").ap()
    out = nc.dram_tensor("out_0_dram", (64, 96, 64), _mybir.dt.float32, kind="ExternalOutput").ap()
    early_fusion_kernel(nc, d, out)
    r = _run(nc, [arrays], core_ids=[0])
    return r.results[0]["out_0_dram"]
```

```python
from contextlib import ExitStack

import concourse.bass as bass
from concourse import mybir

F32 = mybir.dt.float32
BF16 = mybir.dt.bfloat16
ALU = mybir.AluOpType
ACT = mybir.ActivationFunctionType
AX = mybir.AxisListType


T, S, E, G = 96, 64, 64, 4
NG = S // G
TG = T * G
EPS = 1e-5
HEADS = 8
NEG = -1e30


class Stage(ExitStack):

    def __init__(self, nc):
        super().__init__()
        self.nc, self.sems = nc, []

    def sem(self, name):
        self.sems.append(self.enter_context(self.nc.semaphore(name)))
        return self.sems[-1]

    def block(self):
        self.callback(self.clear)
        return self.enter_context(self.nc.Block())

    def clear(self):
        with self.nc.Block() as block:

            @block.sync
            def _(sp):
                for s in self.sems:
                    sp.sem_clear(s)


BASE = 4


def start_at_base(nc, sems):
    with nc.Block() as block:

        @block.sync
        def _(sp):
            for s in sems:
                sp.sem_inc(s, BASE)


class Link:

    def __init__(self, eng, sem, n, per, first=0):
        self.eng, self.sem, self.n, self.per, self.k, self.first = eng, sem, n, per, 0, first

    def __call__(self, ins):
        self.mark(ins)
        self.wait()

    def mark(self, ins):
        ins.then_inc(self.sem, 1)
        self.k += 1

    def wait(self):
        self.eng.wait_ge(self.sem, self.per * self.n + self.first + self.k)

    def done(self):
        assert self.k == self.per, f"{self.k} links, not {self.per}"


def group_of(H, g):
    return H[:, bass.ds(G * g, G), :]


def over(x, n):
    return x.unsqueeze(2).to_broadcast([x.shape[0], x.shape[1], n])


class Norm:

    LINKS = 6

    def __init__(self, ctx, nc, tag):
        self.st = ctx.enter_context(nc.sbuf_tensor(f"{tag}_st", [T, 5, G], F32))
        self.xc = ctx.enter_context(nc.sbuf_tensor(f"{tag}_xc", [T, G, E], F32))
        self.xn = ctx.enter_context(nc.sbuf_tensor(f"{tag}_xn", [T, G, 128], F32))
        self.xt = ctx.enter_context(nc.sbuf_tensor(f"{tag}_xt", [E + 1, TG], F32))
        self.var_ready = ctx.sem(f"{tag}_var_ready")
        self.std_ready = ctx.sem(f"{tag}_std_ready")
        self.xn_ready = ctx.sem(f"{tag}_xn_ready")
        self.turned = ctx.sem(f"{tag}_turned")
        self.xt_ready = ctx.sem(f"{tag}_xt_ready")

    def pads(self, dve, link):
        link(dve.memset(self.xn[:], 0.0))
        link(dve.memset(self.xn[:, :, E:E + 1], 1.0))

    def moments(self, dve, link, x, ready):
        st, xc, sq = self.st, self.xc, self.xn[:, :, 0:E]
        link(dve.tensor_reduce(st[:, 0], x, AX.X, ALU.add))
        link(dve.tensor_scalar(st[:, 0], st[:, 0], 1.0 / E, None, ALU.mult))
        link(dve.tensor_tensor(xc[:], x, over(st[:, 0], E), ALU.subtract))
        link(dve.tensor_tensor(sq, xc[:], xc[:], ALU.mult))
        link(dve.tensor_reduce(st[:, 1], sq, AX.X, ALU.add))
        dve.tensor_scalar(st[:, 2], st[:, 1], 1.0 / E, EPS, ALU.mult, ALU.add).then_inc(ready, 1)

    def steps(self, dve, link, x, n):
        st, xc, sq = self.st, self.xc, self.xn[:, :, 0:E]
        link(dve.tensor_reduce(st[:, 0], x, AX.X, ALU.add))
        link(dve.tensor_scalar(st[:, 0], st[:, 0], 1.0 / E, None, ALU.mult))
        link(dve.tensor_tensor(xc[:], x, over(st[:, 0], E), ALU.subtract))
        yield
        link(dve.tensor_tensor(sq, xc[:], xc[:], ALU.mult))
        link(dve.tensor_reduce(st[:, 1], sq, AX.X, ALU.add))
        dve.tensor_scalar(st[:, 2], st[:, 1], 1.0 / E, EPS, ALU.mult, ALU.add).then_inc(self.var_ready, 1)
        yield
        dve.wait_ge(self.std_ready, n + 1)
        link(dve.reciprocal(st[:, 4], st[:, 3]))
        dve.tensor_tensor(self.xn[:, :, 0:E], xc[:], over(st[:, 4], E), ALU.mult).then_inc(self.xn_ready, 1)
        yield

    def vector(self, dve, link, x, n, scale=None):
        self.moments(dve, link, x, self.var_ready)
        dve.wait_ge(self.std_ready, n + 1)
        link(dve.reciprocal(self.st[:, 4], self.st[:, 3]))
        if scale is None:
            dve.tensor_tensor(self.xn[:, :, 0:E], self.xc[:], over(self.st[:, 4], E),
                              ALU.mult).then_inc(self.xn_ready, 1)
        else:
            link(dve.tensor_tensor(self.xc[:], self.xc[:], over(self.st[:, 4], E), ALU.mult))
            dve.tensor_tensor(self.xn[:, :, 0:E], self.xc[:],
                              scale[:].unsqueeze(1).to_broadcast([T, G, E]), ALU.mult
                              ).then_inc(self.xn_ready, 1)

    def tensor(self, pe, n, bank, ident):
        pe.wait_ge(self.xn_ready, n + 1)
        for s in range(G):
            mm = pe.transpose(bank[:, T * s:T * s + T], self.xn[:, s, :], ident[0:T, 0:T])
        mm.then_inc(self.turned, 1)

    def scalar(self, act, n, bank):
        self.deviation(act, n)
        self.copy_turned(act, n, bank)

    def deviation(self, act, n):
        act.wait_ge(self.var_ready, n + 1)
        act.activation(self.st[:, 3], self.st[:, 2], ACT.Sqrt).then_inc(self.std_ready, 1)

    def copy_turned(self, act, n, bank):
        act.wait_ge(self.turned, n + 1)
        act.activation(self.xt[:], bank[0:E + 1, 0:TG], ACT.Copy).then_inc(self.xt_ready, 1)


class Attention:

    def __init__(self, ctx, nc, tag, psum, gauss=False):
        def sb(name, shape):
            return ctx.enter_context(nc.sbuf_tensor(f"{tag}_{name}", shape, F32))

        def sem(name):
            return ctx.sem(f"{tag}_{name}")

        self.gauss = gauss
        self.qt, self.kt = sb("qt", [128, 4, TG]), sb("kt", [128, 4, TG])
        self.v = sb("v", [T, G, 512])
        self.sc = sb("sc", [T, 2, 2, 384])
        self.pt = sb("pt", [T, 2, 2, 384])
        self.ot = sb("ot", [128, 4, T])
        self.sums = sb("sums", [T, 2, HEADS])
        self.mask = sb("mask", [T, 384])
        if gauss:
            self.q2, self.k2, self.ones = sb("q2", [128, 4, TG]), sb("k2", [128, 4, TG]), sb("ones", [128, T])
            self.gamma = sb("gamma", [T, 2, 384])
        self.wo = sb("wo", [128, 4, E])
        self.S = [psum[2 * u:2 * u + 2] for u in range(2)]
        self.PT = psum[4:6]
        self.O, self.Y = psum[6], psum[7]
        self.s_done, self.sc_ready = sem("s_done"), sem("sc_ready")
        self.exp_done, self.p_ready = sem("exp_done"), sem("p_ready")
        self.pt_done, self.pt_ready = sem("pt_done"), sem("pt_ready")
        self.o_done, self.o_ready, self.y_done = sem("o_done"), sem("o_ready"), sem("y_done")
        self.links = 0 if gauss else G * (4 + 3)

    def pe_scores(self, pe, n, s):
        if s >= 2:
            pe.wait_ge(self.sc_ready, G * n + s - 1)
        c = slice(T * s, T * s + T)
        for h in range(HEADS):
            p = slice(64 * (h % 2), 64 * (h % 2) + 64)
            out = self.S[s % 2][h % 2][0:T, T * (h // 2):T * (h // 2) + T]
            if self.gauss:
                pe.matmul(out, self.kt[p, h // 2, c], self.qt[p, h // 2, c], start=True, stop=False)
                pe.matmul(out, self.k2[p, h // 2, c], self.ones[p, :], start=False, stop=False)
                mm = pe.matmul(out, self.ones[p, :], self.q2[p, h // 2, c], start=False, stop=True)
            else:
                mm = pe.matmul(out, self.qt[p, h // 2, c], self.kt[p, h // 2, c], start=True, stop=True)
        mm.then_inc(self.s_done, 1)

    def pe_turn(self, pe, n, s, ident):
        pe.wait_ge(self.p_ready, G * n + s + 1)
        for h in range(HEADS):
            mm = pe.transpose(self.PT[h % 2][0:T, T * (h // 2):T * (h // 2) + T],
                              self.sc[:, s % 2, h % 2, T * (h // 2):T * (h // 2) + T], ident[0:T, 0:T])
        mm.then_inc(self.pt_done, 1)

    def pe_values(self, pe, n, s):
        pe.wait_ge(self.exp_done if self.gauss else self.pt_ready, G * n + s + 1)
        src = (self.sc if self.gauss else self.pt)[:, s % 2]
        for h in range(HEADS):
            p = slice(64 * (h % 2), 64 * (h % 2) + 64)
            mm = pe.matmul(self.O[p, T * (h // 2):T * (h // 2) + T], self.v[:, s, 64 * h:64 * h + 64],
                           src[:, h % 2, T * (h // 2):T * (h // 2) + T], start=True, stop=True,
                           skip_group_check=True)
        mm.then_inc(self.o_done, 1)

    def pe_project(self, pe, n, s):
        pe.wait_ge(self.o_ready, G * n + s + 1)
        for j in range(4):
            mm = pe.matmul(self.Y[0:T, E * s:E * s + E], self.ot[:, j, :], self.wo[:, j, :],
                           start=(j == 0), stop=(j == 3))
        if s == G - 1:
            mm.then_inc(self.y_done, 1)

    def tensor(self, pe, n, ident):
        lag = 1 if self.gauss else 2
        for i in range(G + lag + 1):
            if i < G:
                self.pe_scores(pe, n, i)
            if i - lag - 1 >= 0:
                self.pe_project(pe, n, i - lag - 1)
            if 0 <= i - lag < G:
                self.pe_values(pe, n, i - lag)
            if not self.gauss and 0 <= i - 1 < G:
                self.pe_turn(pe, n, i - 1, ident)

    def scalar(self, act, n):
        lag = 1 if self.gauss else 2
        for s in range(G + lag):
            if s < G:
                act.wait_ge(self.sc_ready, G * n + s + 1)
                sc = self.sc[:, s % 2]
                act.activation(sc, sc, ACT.Exp, scale=-1.0 if self.gauss else 0.125).then_inc(self.exp_done, 1)
            if 0 <= s - lag < G:
                act.wait_ge(self.o_done, G * n + s - lag + 1)
                act.activation(self.ot[:].rearrange("p j t -> p (j t)"), self.O[:, 0:384],
                               ACT.Copy).then_inc(self.o_ready, 1)
            if not self.gauss and 0 <= s - 1 < G:
                act.wait_ge(self.pt_done, G * n + s)
                for b in range(2):
                    cp = act.activation(self.pt[:, (s - 1) % 2, b], self.PT[b][0:T, 0:384], ACT.Copy)
                cp.then_inc(self.pt_ready, 1)

    def dve_scores(self, dve, link, n, s):
        u = s % 2
        sc = self.sc[:, u]
        dve.wait_ge(self.s_done, G * n + s + 1)
        if s >= 2:
            dve.wait_ge(self.o_done if self.gauss else self.pt_done, G * n + s - 1)
        if self.gauss:
            dve.scalar_tensor_tensor(sc[:, 0], self.S[u][0][0:T, 0:384], 0.0, self.gamma[:, 0],
                                     ALU.max, ALU.mult)
            dve.scalar_tensor_tensor(sc[:, 1], self.S[u][1][0:T, 0:384], 0.0, self.gamma[:, 1],
                                     ALU.max, ALU.mult).then_inc(self.sc_ready, 1)
            return
        for b in range(2):
            link(dve.tensor_tensor(sc[:, b], self.S[u][b][0:T, 0:384], self.mask[:], ALU.add))
        by_head = sc.rearrange("p b (h k) -> p (b h) k", h=4)
        top = self.sums[:, 0]
        link(dve.tensor_reduce(top, by_head, AX.X, ALU.max))
        link(dve.tensor_scalar(top, top, NEG / 1e10, None, ALU.max))
        dve.tensor_tensor(by_head, by_head, over(top, T), ALU.subtract).then_inc(self.sc_ready, 1)
        dve.wait_ge(self.sc_ready, G * n + s + 1)

    def dve_normalise(self, dve, link, n, s):
        by_head = self.sc[:, s % 2].rearrange("p b (h k) -> p (b h) k", h=4)
        den = self.sums[:, 1]
        dve.wait_ge(self.exp_done, G * n + s + 1)
        link(dve.tensor_reduce(den, by_head, AX.X, ALU.add))
        link(dve.tensor_scalar(den, den, 1e-30, None, ALU.max))
        link(dve.reciprocal(den, den))
        dve.tensor_tensor(by_head, by_head, over(den, T), ALU.mult).then_inc(self.p_ready, 1)
        dve.wait_ge(self.p_ready, G * n + s + 1)

    def vector(self, dve, link, n):
        for s in range(G + 1):
            if s < G:
                self.dve_scores(dve, link, n, s)
            if s >= 1 and not self.gauss:
                self.dve_normalise(dve, link, n, s - 1)


def build_tokenizer(nc, d, H, act_out, f_out):
    NG = 16
    PIX = 4096
    NB = 8
    with Stage(nc) as ctx:
        def sb(name, shape):
            return ctx.enter_context(nc.sbuf_tensor(name, shape, F32))

        def ps(name, shape):
            return ctx.enter_context(nc.psum_tensor(name, shape, F32))

        sems = []

        def sem(name):
            sems.append(ctx.sem(name))
            return sems[-1]

        ROWS = 66
        RING = 4
        acts = nc.dram_tensor("acts_scratch", [NG, 128, ROWS, 64], F32).ap()
        modes = nc.dram_tensor("modes_scratch", [NG * 4, 32, 4, 128], F32).ap()

        ident = sb("ft_ident", [128, 128])
        lift_w = sb("ft_lift_w", [14, 128])
        lift_b = sb("ft_lift_b", [128, 1])
        conv_w = sb("ft_conv_w", [96, 3, 32])
        conv_b = sb("ft_conv_b", [128, 4])
        q1_w = sb("ft_q1_w", [128, 128])
        q1_b = sb("ft_q1_b", [128, 1])
        q2_w = sb("ft_q2_w", [128, 4])
        q2_b = sb("ft_q2_b", [4, 1])
        dft_w = sb("ft_dft_w", [128, 64])
        dft_h = sb("ft_dft_h", [128, 32])
        inv_h = sb("ft_inv_h", [128, 4, 16, 128])
        inv_w = sb("ft_inv_w", [128, 256])
        img = sb("ft_img", [96, RING, 4, 8, 64])
        anew = sb("ft_anew", [128, PIX])
        vtmp = sb("ft_vtmp", [128, 2, 512])
        xt = sb("ft_xt", [128, 2, 4, 128])
        y1 = sb("ft_y1", [128, 16, 2, 64])
        y1t = sb("ft_y1t", [128, 2, 4, 128])
        fout = sb("ft_fout", [128, 512])
        fall = sb("ft_fall", [128, 64, 128])
        wall = sb("ft_wall", [128, 64, 128])
        wq = y1[:].rearrange("p a b c -> p (a b c)").rearrange("p (u m o) -> p u m o", u=2, m=8)
        fq = y1t[:].rearrange("p a b c -> p (a b c)").rearrange("p (u m s) -> p u m s", u=2, m=8)
        og = sb("ft_og", [128, 4, 128])
        ot = sb("ft_ot", [128, 4, 128])
        zt = sb("ft_zt", [128, 16, 128])
        x5 = [img[0:14].rearrange("p a b c d -> p (a b c d)")[:, PIX * u:PIX * u + PIX] for u in range(2)]
        hout2 = wall[0:4].rearrange("p a b -> p (a b)")[:, 0:PIX]

        pa = [ps(f"ft_pa{k}", [128, 512]) for k in range(2)]
        pb = [ps(f"ft_pb{k}", [128, 4, 128]) for k in range(2)]
        pc = [ps(f"ft_pc{k}", [128, 16, 16, 2]) for k in range(2)]
        pf = ps("ft_pf", [128, 2, 16, 16])

        consts_in = sem("ft_consts_in")
        cw_in = sem("ft_cw_in")
        x_in = [sem(f"ft_x_in{u}") for u in range(2)]
        img_in = [sem(f"ft_img_in{u}") for u in range(RING)]
        border_out = sem("ft_border_out")
        pad_zero = sem("ft_pad_zero")
        acts_stored = sem("ft_acts_stored")
        modes_stored = sem("ft_modes_stored")
        f_in = sem("ft_f_in")
        w_in = sem("ft_w_in")
        w_neg = sem("ft_w_neg")
        wq_cp = sem("ft_wq_cp")
        fq_cp = sem("ft_fq_cp")
        wq_zero = sem("ft_wq_zero")
        pe_mix = sem("ft_pe_mix")
        ev_mix = sem("ft_ev_mix")
        og_cp = sem("ft_og_cp")
        pe_ot = sem("ft_pe_ot")
        ev_ot = sem("ft_ev_ot")
        pe_zt = sem("ft_pe_zt")
        ev_zt = sem("ft_ev_zt")
        pe_lift = sem("ft_pe_lift")
        ev_lift = sem("ft_ev_lift")
        pe_cv = sem("ft_pe_cv")
        ev_v = sem("ft_ev_v")
        ev_a = sem("ft_ev_a")
        pe_xt = sem("ft_pe_xt")
        ev_xt = sem("ft_ev_xt")
        pe_s1 = sem("ft_pe_s1")
        ev_s1 = sem("ft_ev_s1")
        pe_yt = sem("ft_pe_yt")
        ev_yt = sem("ft_ev_yt")
        pe_f = sem("ft_pe_f")
        ev_f = sem("ft_ev_f")
        pe_q1 = sem("ft_pe_q1")
        ev_q1 = sem("ft_ev_q1")
        ev_q1l = sem("ft_ev_q1l")
        pe_q2 = sem("ft_pe_q2")
        ev_q2 = sem("ft_ev_q2")
        h_in = sem("ft_h_in")
        txt_in = sem("ft_txt_in")
        wall_used = sem("ft_wall_used")

        start_at_base(nc, sems)
        block = ctx.block()


        @block.sync
        def _(sp):
            consts = [(ident[:], d["ident"]), (lift_w[:], d["lift_w"]), (lift_b[:], d["lift_b"]),
                      (conv_b[:], d["conv_b"]), (q1_w[:], d["q1_w"]), (q1_b[:], d["q1_b"]),
                      (q2_w[:], d["q2_w"]), (q2_b[:], d["q2_b"]), (dft_w[:], d["dft_w"]),
                      (dft_h[:], d["dft_h"]), (inv_h[:], d["inv_h"]), (inv_w[:], d["inv_w"])]
            for dst, src in consts:
                sp.dma_start(dst, src).then_inc(consts_in, 16)
            sp.dma_start(H[64:96, :, :], d["txt"]).then_inc(txt_in, 16)
            sp.wait_ge(pad_zero, BASE + 1)
            for row in (0, ROWS - 1):
                sp.dma_start(acts[:, :, row, :].rearrange("g p w -> p g w"),
                             zt[:].rearrange("p a b -> p (a b)")[:, 0:NG * 64].rearrange("p (g w) -> p g w", g=NG)
                             ).then_inc(border_out, 16)
            sp.wait_ge(border_out, BASE + 32)
            with sp.Fori(0, NG // 2) as i:
                for u in range(2):
                    g = 2 * i + u
                    sp.wait_ge(pe_lift, BASE + 16 * i)
                    sp.dma_start(x5[u][0:12], d["x"][bass.ds(g, 1), :, :]).then_inc(x_in[u], 16)
                    sp.dma_start(x5[u][12:14], d["grid"]).then_inc(x_in[u], 16)
            sp.wait_ge(pe_lift, BASE + 8 * NG)
            for l in range(4):
                sp.wait_ge(pe_cv, BASE + 128 * l)
                sp.dma_start(conv_w[:], d["conv_w"][bass.ds(l, 1)]).then_inc(cw_in, 16)
                sp.wait_ge(wq_cp, BASE + 16 * l)
                sp.wait_ge(fq_cp, BASE + 16 * l)
                sp.wait_ge(w_neg, BASE + 2 * l)
                for mh in range(2):
                    for c in range(2):
                        for c2 in range(2):
                            src = d["wr"] if c == c2 else d["wi"]
                            p0 = 64 * mh + 32 * c
                            sp.dma_start(wall[p0:p0 + 32, 32 * c2:32 * c2 + 32, :],
                                         src[bass.ds(l, 1), :, :, 128 * mh:128 * mh + 128]).then_inc(w_in, 16)
                sp.wait_ge(f_out, 256 * l + 256)
                sp.wait_ge(og_cp, BASE + 16 * l)
                for k in range(4):
                    sp.dma_start(fall[32 * k:32 * k + 32, :, :],
                                 modes[:, :, 2 * (k % 2) + k // 2, :].rearrange("s i m -> i s m")
                                 ).then_inc(f_in, 16)
                sp.wait_ge(act_out, 256 * l + 256)
                with sp.Fori(0, NG) as g:
                    for b in range(NB):
                        sp.wait_ge(pe_cv, BASE - RING + 128 * l + 8 * g + b + 1)
                        for dy in range(3):
                            sp.dma_start(img[32 * dy:32 * dy + 32, b % RING],
                                         acts[bass.ds(g, 1), :, 8 * b + dy:8 * b + dy + 8, :].rearrange(
                                             "o (s c) h w -> (o c) s h w", s=4)).then_inc(img_in[b % RING], 16)
            sp.wait_ge(txt_in, BASE + 16)
            sp.wait_ge(h_in, BASE + 16 * 64)

        def stores(pool, n, g):
            pool.wait_ge(ev_a, BASE + 8 * n + 8)
            pool.dma_start(acts[bass.ds(g, 1), :, 1:65, :].rearrange("o p h w -> (o p) (h w)"),
                           anew[:]).then_inc(act_out, 16)
            pool.wait_ge(ev_f, BASE + n + 1)
            pool.dma_start(modes[bass.ds(4 * g, 4)].rearrange("s i c m -> (s i) (c m)"),
                           fout[:]).then_inc(f_out, 16)
            pool.wait_ge(act_out, 16 * n + 16)
            pool.sem_inc(acts_stored, 1)
            pool.wait_ge(f_out, 16 * n + 16)
            pool.sem_inc(modes_stored, 1)

        @block.gpsimd
        def _(pool):
            pool.memset(zt[:], 0.0).then_inc(pad_zero, 1)
            with pool.Fori(0, NG) as g:
                stores(pool, g, g)

            def mix_copies(l):
                pool.wait_ge(w_neg, BASE + 2 * l + 2)
                pool.wait_ge(pe_yt, BASE + 64 * l + 64)
                pool.memset(wq, 0.0).then_inc(wq_zero, 1)
                pool.wait_ge(wq_zero, BASE + l + 1)
                with pool.Fori(0, 8) as i:
                    for u in range(2):
                        q = 2 * i + u
                        pool.wait_ge(pe_mix, BASE + 16 * l + 2 * i)
                        pool.tensor_copy(wq[0:64, u, :, 0:64].rearrange("p m o -> p o m"),
                                         wall[0:64, :, bass.ds(8 * q, 8)]).then_inc(wq_cp, 1)

            for l in range(3):
                mix_copies(l)
                with pool.Fori(0, NG) as g:
                    stores(pool, 16 * l + g + 16, g)
            mix_copies(3)

        @block.scalar
        def _(act):
            act.wait_ge(consts_in, BASE + 12 * 16)

            def xt_copy(n, b):
                act.wait_ge(pe_xt, BASE + 8 * n + b + 1)
                if b >= 2:
                    act.wait_ge(pe_s1, BASE + 8 * n + b - 1)
                else:
                    act.wait_ge(pe_s1, BASE + 8 * n)
                act.activation(xt[:, b % 2], pb[(b + 1) % 2][:], ACT.Copy).then_inc(ev_xt, 1)

            with act.Fori(0, NG // 2) as i:
                for u in range(2):
                    n = 2 * i + u
                    for b in range(NB):
                        xt_copy(n, b)

            def conv_evac(n, m, b):
                act.wait_ge(pe_cv, BASE + 8 * m + b + 1)
                if b >= 2:
                    act.wait_ge(ev_a, BASE + 8 * n + b - 1)
                else:
                    act.wait_ge(ev_a, BASE + 8 * n)
                act.activation(vtmp[:, b % 2], pa[b % 2][:], ACT.Identity,
                               bias=conv_b_l).then_inc(ev_v, 1)

            for l in range(4):
                conv_b_l = conv_b[:, l:l + 1]
                act.wait_ge(w_in, BASE + 128 * (l + 1))
                for mh in range(2):
                    p0 = 64 * mh + 32
                    act.mul(wall[p0:p0 + 32, 0:32, :], wall[p0:p0 + 32, 0:32, :], -1.0).then_inc(w_neg, 1)
                with act.Fori(0, 8) as i:
                    for u in range(2):
                        q = 2 * i + u
                        act.wait_ge(pe_mix, BASE + 16 * l + q + 1)
                        act.activation(fall[:, :, bass.ds(8 * q, 8)].rearrange("p s m -> p m s"),
                                       pa[u][:].rearrange("p (m s) -> p m s", m=8),
                                       ACT.Copy).then_inc(ev_mix, 1)
                with act.Fori(0, NG // 2) as i:
                    for u in range(2):
                        g = 2 * i + u
                        m = 16 * l + g
                        n = m + 16
                        act.wait_ge(ev_mix, BASE + 16 * l + 16)
                        act.wait_ge(pe_ot, BASE + m)
                        act.activation(og[:], fall[:, bass.ds(4 * g, 4), :], ACT.Copy).then_inc(og_cp, 1)
                        if l < 3:
                            for b in range(NB):
                                conv_evac(n, m, b)
                                if b >= 1:
                                    xt_copy(n, b - 1)
                            xt_copy(n, NB - 1)
                        else:
                            for b in range(NB + 2):
                                if b < NB:
                                    conv_evac(n, m, b)
                                if 1 <= b <= NB:
                                    k = 8 * g + b - 1
                                    act.wait_ge(pe_q1, BASE + k + 1)
                                    act.wait_ge(ev_q1l, BASE + k)
                                    act.activation(xt[:, 0].rearrange("p a b -> p (a b)"),
                                                   pb[1][:].rearrange("p a b -> p (a b)"), ACT.Identity,
                                                   bias=q1_b[:]).then_inc(ev_q1, 1)
                                if b >= 2:
                                    act.wait_ge(pe_q2, BASE + 8 * g + b - 1)
                                    if b == 2:
                                        act.wait_ge(h_in, BASE + 64 * g)
                                    act.activation(hout2[:, 512 * (b - 2):512 * (b - 1)],
                                                   pc[0][:].rearrange("p a b c -> p (a b c)")[0:4],
                                                   ACT.Identity, bias=q2_b[:]).then_inc(ev_q2, 1)
                            act.wait_ge(ev_q2, BASE + 8 * g + 8)
                            for s in range(4):
                                act.dma_start(H[0:64, bass.ds(4 * g + s, 1), :],
                                              hout2[s:s + 1, :].rearrange("p (h w) -> p h w", w=64)
                                              ).then_inc(h_in, 16)

            act.wait_ge(act_out, 16 * 64)
            act.wait_ge(f_out, 16 * 64)

        def q_leaky(dve, k):
            dve.wait_ge(ev_q1, BASE + k + 1)
            dve.wait_ge(pe_q2, BASE + k)
            t = xt[:, 0].rearrange("p a b -> p (a b)")
            dve.scalar_tensor_tensor(xt[:, 1].rearrange("p a b -> p (a b)"), t, 0.01, t,
                                     ALU.mult, ALU.max).then_inc(ev_q1l, 1)

        @block.vector
        def _(dve):
            dve.wait_ge(consts_in, BASE + 12 * 16)
            dve.wait_ge(pad_zero, BASE + 1)

            def s1_evac(n, k):
                dve.wait_ge(pe_s1, BASE + 8 * n + 2 * k + 2)
                if k == 0:
                    dve.wait_ge(pe_yt, BASE + 4 * n)
                dve.tensor_copy(y1[:, :, :, 16 * k:16 * k + 16].rearrange("p y c h -> p h y c"),
                                pc[k % 2][:]).then_inc(ev_s1, 1)

            def second_half(n):
                for q in range(4):
                    dve.wait_ge(pe_yt, BASE + 4 * n + q + 1)
                    if q >= 2:
                        dve.wait_ge(pe_f, BASE + 4 * n + q - 1)
                    else:
                        dve.wait_ge(pe_f, BASE + 4 * n)
                    dve.tensor_copy(y1t[:, q % 2], pb[(q + 1) % 2][:]).then_inc(ev_yt, 1)
                dve.wait_ge(pe_f, BASE + 4 * n + 4)
                dve.wait_ge(modes_stored, BASE + n)
                dve.tensor_copy(fout[:], pf[:].rearrange("p a b c -> p (a b c)")).then_inc(ev_f, 1)

            with dve.Fori(0, NG // 2) as i:
                for u in range(2):
                    n = 2 * i + u
                    dve.wait_ge(acts_stored, BASE + n)
                    dve.wait_ge(pe_xt, BASE + 8 * n)
                    for b in range(NB):
                        dve.wait_ge(pe_lift, BASE + 8 * n + b + 1)
                        dve.tensor_scalar(anew[:, 512 * b:512 * b + 512], pa[b % 2][:], lift_b[:], None, ALU.add).then_inc(ev_a, 1)
                        if b >= 2 and b % 2 == 1:
                            s1_evac(n, (b - 3) // 2)
                    s1_evac(n, 3)
                    second_half(n)

            for l in range(4):
                dve.wait_ge(f_in, BASE + 64 * (l + 1))
                dve.wait_ge(pe_f, BASE + 64 * (l + 1))
                with dve.Fori(0, 8) as i:
                    for u in range(2):
                        q = 2 * i + u
                        dve.wait_ge(wq_zero, BASE + l + 1)
                        dve.wait_ge(w_neg, BASE + 2 * l + 2)
                        dve.wait_ge(pe_mix, BASE + 16 * l + 2 * i)
                        dve.tensor_copy(wq[64:128, u, :, 64:128].rearrange("p m o -> p o m"),
                                        wall[64:128, :, bass.ds(8 * q, 8)])
                        dve.tensor_copy(fq[:, u].rearrange("p m s -> p s m"),
                                        fall[:, :, bass.ds(8 * q, 8)]).then_inc(fq_cp, 1)
                dve.wait_ge(pe_mix, BASE + 16 * (l + 1))
                with dve.Fori(0, NG // 2) as i:
                    for u in range(2):
                        g = 2 * i + u
                        m = 16 * l + g
                        n = m + 16
                        dve.wait_ge(pe_ot, BASE + m + 1)
                        dve.wait_ge(pe_zt, BASE + 4 * m)
                        dve.tensor_copy(ot[:].rearrange("p c (s o) -> p s c o", s=4),
                                        pb[0][:].rearrange("p s (c o) -> p s c o", c=4)).then_inc(ev_ot, 1)
                        for q in range(4):
                            dve.wait_ge(pe_zt, BASE + 4 * m + q + 1)
                            if q == 0:
                                dve.wait_ge(pe_cv, BASE + 8 * m)
                                if l < 3:
                                    dve.wait_ge(pe_yt, BASE + 4 * n)
                            dve.tensor_copy(zt[:, 4 * q:4 * q + 4, :], pb[(q + 1) % 2][:]).then_inc(ev_zt, 1)
                        if l < 3:
                            dve.wait_ge(acts_stored, BASE + n)
                            dve.wait_ge(pe_xt, BASE + 8 * n)
                        else:
                            dve.wait_ge(acts_stored, BASE + 64)
                            dve.wait_ge(pe_q1, BASE + 8 * g)
                        for b in range(NB):
                            dve.wait_ge(ev_v, BASE + 8 * m + b + 1)
                            v = vtmp[:, b % 2]
                            dve.scalar_tensor_tensor(anew[:, 512 * b:512 * b + 512], v, 0.01, v,
                                                     ALU.mult, ALU.max).then_inc(ev_a, 1)
                            if l < 3:
                                if b >= 2 and b % 2 == 1:
                                    s1_evac(n, (b - 3) // 2)
                            elif b >= 1:
                                q_leaky(dve, 8 * g + b - 1)
                        if l < 3:
                            s1_evac(n, 3)
                            second_half(n)
                        else:
                            q_leaky(dve, 8 * g + 7)

        @block.tensor
        def _(pe):
            pe.wait_ge(consts_in, BASE + 12 * 16)

            def transposes(n, u, b, in_conv):
                pe.wait_ge(ev_a, BASE + 8 * n + b + 1)
                if b >= 2:
                    pe.wait_ge(ev_xt, BASE + 8 * n + b - 1)
                elif in_conv is None:
                    pe.wait_ge(ev_yt, BASE + 4 * n)
                else:
                    pe.wait_ge(ev_zt, BASE + 4 * in_conv + 3 + b)
                for k in range(4):
                    t = 4 * b + k
                    mm = pe.transpose(pb[(b + 1) % 2][:, k, :], anew[:, 128 * t:128 * t + 128], ident[:])
                mm.then_inc(pe_xt, 1)

            def along_w(n, b):
                pe.wait_ge(ev_xt, BASE + 8 * n + b + 1)
                k2 = b // 2
                if b % 2 == 0:
                    if k2 >= 2:
                        pe.wait_ge(ev_s1, BASE + 4 * n + k2 - 1)
                    else:
                        pe.wait_ge(ev_s1, BASE + 4 * n)
                for k in range(4):
                    r = 2 * (4 * (b % 2) + k)
                    mm = pe.matmul(pc[k2 % 2][:, r:r + 2].rearrange("p a b c -> p (a b c)"), xt[:, b % 2, k, :], dft_w[:], start=True, stop=True)
                mm.then_inc(pe_s1, 1)

            def along_h(n):
                pe.wait_ge(ev_s1, BASE + 4 * n + 4)

                def yt(q):
                    if q < 2:
                        pe.wait_ge(ev_xt, BASE + 8 * n + 7 + q)
                    else:
                        pe.wait_ge(ev_yt, BASE + 4 * n + q - 1)
                    for k in range(4):
                        mm = pe.transpose(pb[(q + 1) % 2][:, k, :],
                                          y1[:, 4 * q + k].rearrange("p c h -> p (c h)"), ident[:])
                    mm.then_inc(pe_yt, 1)

                def fm(q):
                    pe.wait_ge(ev_yt, BASE + 4 * n + q + 1)
                    if q == 0:
                        pe.wait_ge(ev_f, BASE + n)
                    for k in range(4):
                        mm = pe.matmul(pf[:, :, :, 4 * q + k], y1t[:, q % 2, k, :], dft_h[:],
                                       start=True, stop=True)
                    mm.then_inc(pe_f, 1)

                yt(0)
                for q in range(1, 4):
                    yt(q)
                    fm(q - 1)
                fm(3)

            with pe.Fori(0, NG // 2) as i:
                for u in range(2):
                    n = 2 * i + u
                    pe.wait_ge(x_in[u], BASE + 32 * i + 32)
                    for b in range(NB):
                        if b < 2:
                            pe.wait_ge(ev_a, BASE + 8 * n)
                        else:
                            pe.wait_ge(ev_a, BASE + 8 * n + b - 1)
                        pe.matmul(pa[b % 2][:], lift_w[:], x5[u][:, 512 * b:512 * b + 512],
                                  start=True, stop=True).then_inc(pe_lift, 1)
                        if b >= 1:
                            transposes(n, u, b - 1, None)
                        if b >= 2:
                            along_w(n, b - 2)
                    transposes(n, u, NB - 1, None)
                    along_w(n, NB - 2)
                    along_w(n, NB - 1)
                    along_h(n)

            def taps(m, b):
                if b == 0:
                    pe.wait_ge(ev_mix, BASE + 16 * (l + 1))
                if b >= 2:
                    pe.wait_ge(ev_v, BASE + 8 * m + b - 1)
                else:
                    pe.wait_ge(ev_v, BASE + 8 * m)
                pe.wait_ge(img_in[b % RING], BASE + 48 * (2 * m + b // RING + 1))
                for dx, to, fr in ((1, slice(0, 64), slice(0, 64)), (0, slice(1, 64), slice(0, 63)),
                                   (2, slice(0, 63), slice(1, 64))):
                    for s in range(4):
                        out = pa[b % 2][32 * s:32 * s + 32, :].rearrange("p (h w) -> p h w", w=64)
                        pe.matmul(out[:, :, to], conv_w[:, dx, :], img[:, b % RING, s, :, fr],
                                  start=(dx == 1), stop=False, skip_group_check=True)

            for l in range(4):
                with pe.Fori(0, 8) as i:
                    for u in range(2):
                        q = 2 * i + u
                        if l == 0:
                            pe.wait_ge(ev_a, BASE + 8 * NG)
                        else:
                            pe.wait_ge(ev_v, BASE + 128 * l)
                        pe.wait_ge(ev_mix, BASE + 16 * l + 2 * i)
                        pe.wait_ge(wq_cp, BASE + 16 * l + q + 1)
                        pe.wait_ge(fq_cp, BASE + 16 * l + q + 1)
                        for j in range(8):
                            mm = pe.matmul(pa[u][:, 64 * j:64 * j + 64], wq[:, u, j, :], fq[:, u, j, :],
                                           start=True, stop=True)
                        mm.then_inc(pe_mix, 1)
                pe.wait_ge(cw_in, BASE + 16 * (l + 1))
                with pe.Fori(0, NG // 2) as i:
                    for u in range(2):
                        g = 2 * i + u
                        m = 16 * l + g
                        n = m + 16
                        pe.wait_ge(og_cp, BASE + m + 1)
                        if l < 3:
                            pe.wait_ge(ev_yt, BASE + 4 * n)
                        else:
                            pe.wait_ge(ev_yt, BASE + 4 * 64)
                            pe.wait_ge(ev_zt, BASE + 4 * m)
                        for s in range(4):
                            mm = pe.transpose(pb[0][:, s, :], og[:, s, :], ident[:])
                        mm.then_inc(pe_ot, 1)
                        taps(m, 0)
                        pe.wait_ge(ev_ot, BASE + m + 1)
                        if l == 3:
                            pe.wait_ge(ev_q1, BASE + 8 * g)
                        for q in range(4):
                            if q >= 2:
                                pe.wait_ge(ev_zt, BASE + 4 * m + q - 1)
                            for k in range(4):
                                for t in range(4):
                                    mm = pe.matmul(pb[(q + 1) % 2][:, k, :], inv_h[:, t, 4 * q + k, :],
                                                   ot[:, t, :], start=(t == 0), stop=(t == 3))
                            mm.then_inc(pe_zt, 1)
                        for b in range(NB + 1 if l < 3 else NB + 2):
                            if b < NB:
                                acc = pa[b % 2]
                                if b >= 1:
                                    taps(m, b)
                                pe.wait_ge(ev_zt, BASE + 4 * m + (b // 2) + 1)
                                for k in range(2):
                                    mm = pe.matmul(acc[:, 256 * k:256 * k + 256], zt[:, 2 * b + k, :], inv_w[:],
                                                   start=False, stop=True, skip_group_check=True)
                                mm.then_inc(pe_cv, 1)
                            if l < 3:
                                if b >= 1:
                                    transposes(n, u, b - 1, m)
                                if b >= 2:
                                    along_w(n, b - 2)
                            else:
                                if 1 <= b <= NB:
                                    k = 8 * g + b - 1
                                    pe.wait_ge(ev_a, BASE + 8 * n + b)
                                    pe.wait_ge(ev_q1, BASE + k)
                                    pe.wait_ge(ev_zt, BASE + 4 * m + 4)
                                    pe.matmul(pb[1][:].rearrange("p a b -> p (a b)"), q1_w[:],
                                              anew[:, 512 * (b - 1):512 * b], start=True, stop=True
                                              ).then_inc(pe_q1, 1)
                                if b >= 2:
                                    k = 8 * g + b - 2
                                    pe.wait_ge(ev_q1l, BASE + k + 1)
                                    pe.wait_ge(ev_q2, BASE + k)
                                    pe.matmul(pc[0][:].rearrange("p a b c -> p (a b c)")[0:4], q2_w[:],
                                              xt[:, 1].rearrange("p a b -> p (a b)"), start=True, stop=True
                                              ).then_inc(pe_q2, 1)
                        if l < 3:
                            along_w(n, NB - 1)
                            along_h(n)


def build_attention0(nc, d, H):
    with Stage(nc) as ctx:
        def sb(name, shape):
            return ctx.enter_context(nc.sbuf_tensor(f"a0_{name}", shape, F32))

        def sem(name):
            return ctx.sem(f"a0_{name}")

        psum = [ctx.enter_context(nc.psum_tensor(f"a0_ps{k}", [128, 512], F32)) for k in range(8)]
        norm = Norm(ctx, nc, "a0n")
        att = Attention(ctx, nc, "a0a", psum)
        ident, wqk, wv = sb("ident", [128, 128]), sb("wqk", [E + 1, 8, 128]), sb("wv", [E + 1, 512])
        bu = sb("bu", [T, E])
        TURN = psum[4]
        consts_in, link_dve, link_norm = sem("consts_in"), sem("link_dve"), sem("link_norm")
        proj_done, proj_ready = sem("proj_done"), sem("proj_ready")
        block = ctx.block()
        per = att.links + 2

        @block.sync
        def _(sp):
            for dst, src in ((ident[:], d["ident"]), (wqk[:], d["a0_wqk"]), (wv[:], d["a0_wv"]),
                             (bu[:], d["a0_bu"]), (att.wo[:], d["a0_wu"]), (att.mask[:], d["mask_strict"])):
                sp.dma_start(dst, src).then_inc(consts_in, 16)

        @block.tensor
        def _(pe):
            pe.wait_ge(consts_in, 6 * 16)
            with pe.Fori(0, NG) as n:
                norm.tensor(pe, n, TURN, ident)
                pe.wait_ge(norm.xt_ready, n + 1)
                for j in range(12):
                    if j >= 4:
                        pe.wait_ge(proj_ready, 12 * n + j - 3)
                    if j < 8:
                        mm = pe.matmul(psum[j % 4][:, 0:TG], wqk[:, j, :], norm.xt[:], start=True, stop=True)
                    else:
                        s = j - 8
                        mm = pe.matmul(psum[j % 4][0:T, :], norm.xt[:, T * s:T * s + T], wv[:],
                                       start=True, stop=True)
                    mm.then_inc(proj_done, 1)
                pe.wait_ge(proj_ready, 12 * n + 12)
                att.tensor(pe, n, ident)

        @block.scalar
        def _(act):
            def group(n, last):
                norm.copy_turned(act, n, TURN)
                for j in range(12):
                    act.wait_ge(proj_done, 12 * n + j + 1)
                    if j < 8:
                        dst = (att.qt, att.kt)[j // 4][:, j % 4, :]
                        act.activation(dst, psum[j % 4][:, 0:TG], ACT.Copy).then_inc(proj_ready, 1)
                    else:
                        act.activation(att.v[:, j - 8, :], psum[j % 4][0:T, :], ACT.Copy).then_inc(proj_ready, 1)
                if not last:
                    norm.deviation(act, n + 1)
                att.scalar(act, n)

            norm.deviation(act, 0)
            with act.Fori(0, NG - 1) as n:
                group(n, False)
            group(NG - 1, True)

        @block.vector
        def _(dve):
            setup = Link(dve, link_dve, 0, 2)
            norm.pads(dve, setup)
            dve.wait_ge(consts_in, 6 * 16)

            def normalise(m):
                norm.vector(dve, Link(dve, link_norm, m, Norm.LINKS), group_of(H, m), m)

            def group(n, last):
                link = Link(dve, link_dve, n, per, first=2)
                if not last:
                    dve.wait_ge(norm.turned, n + 1)
                    normalise(n + 1)
                att.vector(dve, link, n)
                h = group_of(H, n)
                dve.wait_ge(att.y_done, n + 1)
                link(dve.tensor_tensor(h, h, att.Y[0:T, 0:G * E].rearrange("p (s e) -> p s e", s=G), ALU.add))
                link(dve.tensor_tensor(h, h, bu[:].unsqueeze(1).to_broadcast([T, G, E]), ALU.add))
                link.done()

            normalise(0)
            with dve.Fori(0, NG - 1) as n:
                group(n, False)
            group(NG - 1, True)


class Router:

    PAD, MARK = -1e30, -3e38

    def __init__(self, ctx, nc, tag, experts):
        def sb(name, shape):
            return ctx.enter_context(nc.sbuf_tensor(f"{tag}_{name}", shape, F32))

        def sem(name):
            return ctx.sem(f"{tag}_{name}")

        self.x, self.w = experts, experts + 8
        self.val = sb("val", [T, G, self.w])
        self.mark = sb("mark", [T, G, self.w])
        self.top8 = sb("top8", [T, G, 8])
        self.find = sb("find", [T, G, 8])
        self.ex = sb("ex", [T, G, experts])
        self.small = sb("small", [T, 2, G])
        self.spare = sb("spare", [T, 3])
        self.comb = sb("comb", [T, G, 128])
        self.combt = sb("combt", [128, TG])
        self.exp_in, self.exp_out = sem("exp_in"), sem("exp_out")
        self.logits_done = sem("logits_done")
        self.comb_ready, self.comb_turned, self.combt_ready = sem("comb_ready"), sem("comb_turned"), sem("combt_ready")

    def pads(self, dve, link):
        link(dve.memset(self.val[:], self.PAD))
        link(dve.memset(self.find[:], self.PAD))
        link(dve.memset(self.comb[:], 0.0))

    def softmax_steps(self, dve, link, src, count, dst):
        link(dve.tensor_reduce(self.small[:, 0], src, AX.X, ALU.max))
        dve.tensor_tensor(self.ex[:], src, over(self.small[:, 0], self.x), ALU.subtract).then_inc(self.exp_in, 1)
        yield
        dve.wait_ge(self.exp_out, count)
        link(dve.tensor_reduce(self.small[:, 1], self.ex[:], AX.X, ALU.add))
        link(dve.reciprocal(self.small[:, 1], self.small[:, 1]))
        link(dve.tensor_tensor(dst, self.ex[:], over(self.small[:, 1], self.x), ALU.mult))

    def exponential(self, act, count):
        act.wait_ge(self.exp_in, count)
        act.activation(self.ex[:], self.ex[:], ACT.Exp).then_inc(self.exp_out, 1)

    def choose_steps(self, dve, link, k):
        dve.memset(self.spare[:, 0:1], 0.0)
        for s in range(G):
            last = dve.max(self.top8[:, s], self.val[:, s])
        link(last)
        link(dve.tensor_copy(self.find[:, :, 0:k], self.top8[:, :, 0:k]))
        yield
        dve.memset(self.spare[:, 1:2], 0.0)
        for s in range(G):
            last = dve.match_replace(self.mark[:, s], self.find[:, s], self.val[:, s], self.MARK)
        link(last)
        link(dve.tensor_scalar(self.mark[:], self.mark[:], self.MARK / 2, None, ALU.is_lt))

    def share_steps(self, dve, link, count, ready):
        link(dve.tensor_copy(self.small[:, 0], self.top8[:, :, 0]))
        dve.tensor_tensor(self.ex[:], self.val[:, :, 0:self.x], over(self.small[:, 0], self.x),
                          ALU.subtract).then_inc(self.exp_in, 1)
        yield
        dve.wait_ge(self.exp_out, count)
        link(dve.tensor_tensor(self.ex[:], self.ex[:], self.mark[:, :, 0:self.x], ALU.mult))
        link(dve.tensor_reduce(self.small[:, 1], self.ex[:], AX.X, ALU.add))
        link(dve.reciprocal(self.small[:, 1], self.small[:, 1]))
        dve.tensor_tensor(self.comb[:, :, 0:self.x], self.ex[:], over(self.small[:, 1], self.x),
                          ALU.mult).then_inc(ready, 1)

    def logits(self, pe, bank, xt, gate):
        for s in range(G):
            mm = pe.matmul(bank[0:T, 16 * s:16 * s + self.x], xt[:, T * s:T * s + T], gate[:],
                           start=True, stop=True)
        mm.then_inc(self.logits_done, 1)

    def turn(self, pe, n, bank, ident):
        pe.wait_ge(self.comb_ready, n + 1)
        for s in range(G):
            mm = pe.transpose(bank[:, T * s:T * s + T], self.comb[:, s, :], ident[0:T, 0:T])
        mm.then_inc(self.comb_turned, 1)

    def turned(self, act, n, bank, bf16=None):
        act.wait_ge(self.comb_turned, n + 1)
        if bf16 is not None:
            act.activation(bf16[:], bank[:, 0:TG], ACT.Copy)
        act.activation(self.combt[:], bank[:, 0:TG], ACT.Copy).then_inc(self.combt_ready, 1)


def build_routed_mlp(nc, d, H, tag, experts, capacity):
    BLOCKS = 16
    with Stage(nc) as ctx:
        def sb(name, shape):
            return ctx.enter_context(nc.sbuf_tensor(f"{tag}_{name}", shape, F32))

        def sem(name):
            return ctx.sem(f"{tag}_{name}")

        psum = [ctx.enter_context(nc.psum_tensor(f"{tag}_ps{k}", [128, 512], F32)) for k in range(8)]
        misc, Y, HB, CB, POS = psum[0], psum[1], psum[2:4], psum[4:6], psum[6]
        norm = Norm(ctx, nc, f"{tag}n")
        route = Router(ctx, nc, f"{tag}r", experts)
        ident = sb("ident", [128, 128])
        gate, w1, w2 = sb("gate", [E + 1, experts]), sb("w1", [E + 1, BLOCKS, 128]), sb("w2", [128, BLOCKS, E])
        b2, pick = sb("b2", [experts, E]), sb("pick", [128, BLOCKS, 128])
        PIECES = 32
        pick16 = ctx.enter_context(nc.sbuf_tensor(f"{tag}_pick16", [128, BLOCKS, 128], BF16))
        combt16 = ctx.enter_context(nc.sbuf_tensor(f"{tag}_combt16", [128, TG], BF16))
        piece = ctx.enter_context(nc.sbuf_tensor(f"{tag}_piece", [T, G, 3, experts], BF16))
        rest = sb("rest", [T, G, experts])
        weights_ready, pick_ready = sem("weights_ready"), sem("pick_ready")
        relu, hw = sb("relu", [128, 2, TG]), sb("hw", [128, 2, TG])
        xt, y = sb("xt", [E + 1, TG]), sb("y", [T, G, E])
        if capacity is None:
            pe_at, act_at, dve_at = (5, 7, 14), (2, 6, 10), (0, 1, 3, 8, 9, 12)
        else:
            pe_at, act_at, dve_at = (5, 7, 12, 14), (2, 6, 9), (0, 1, 3, 8, 10, 11, 13)
        consts = [(ident, "ident"), (gate, f"{tag}_gate"), (w1, f"{tag}_w1"), (w2, f"{tag}_w2"),
                  (b2, f"{tag}_b2"), (pick, f"{tag}_pick")]
        if capacity is None:
            norm2 = Norm(ctx, nc, f"{tag}m")
            gamma, beta = sb("gamma", [T, E]), sb("beta", [T, E])
            consts += [(gamma, f"{tag}_gamma"), (beta, f"{tag}_beta")]
            xkeep = sb("xkeep", [T, G, E])
            per_front, per = Norm.LINKS + 1 + 4 + 4 + 4, Norm.LINKS + 1 + 5
        else:
            upto, ones = sb("upto", [T, T]), sb("ones", [T, T])
            before = sb("before", [T, G + 1, experts])
            kept = sb("kept", [T, G, experts])
            fin, fix = sb("fin", [T, G, E]), sb("fix", [T, G, E])
            consts += [(upto, "upto"), (ones, "ones")]
            chosen, placed = sem("chosen"), sem("placed")
            per_front, per = Norm.LINKS + 4 + 4 + 3 + 3 + 4, 7
        consts_in, link_dve, link_front, xt_carried = (
            sem("consts_in"), sem("link_dve"), sem("link_front"), sem("xt_carried"))
        h_done, r_ready, c_done, hw_ready, y_part, y_done = (
            sem("h_done"), sem("r_ready"), sem("c_done"), sem("hw_ready"), sem("y_part"), sem("y_done"))
        block = ctx.block()

        @block.sync
        def _(sp):
            for dst, name in consts:
                sp.dma_start(dst[:], d[name]).then_inc(consts_in, 16)

        @block.tensor
        def _(pe):
            pe.wait_ge(consts_in, 16 * len(consts))
            pe.wait_ge(pick_ready, 1)

            def hidden(n, e):
                if e >= 2:
                    pe.wait_ge(r_ready, BLOCKS * n + e - 1)
                pe.matmul(HB[e % 2][:, 0:TG], w1[:, e, :], xt[:], start=True, stop=True).then_inc(h_done, 1)
                if e == 0:
                    pe.wait_ge(route.combt_ready, n + 1)
                if e >= 2:
                    pe.wait_ge(hw_ready, BLOCKS * n + e - 1)
                pe.matmul(CB[e % 2][:, 0:TG], pick16[:, e, :], combt16[:],
                          start=True, stop=True).then_inc(c_done, 1)

            def output(n, e):
                pe.wait_ge(hw_ready, BLOCKS * n + e + 1)
                for s in range(G):
                    mm = pe.matmul(Y[0:T, E * s:E * s + E], hw[:, e % 2, T * s:T * s + T], w2[:, e, :],
                                   start=(e == 0 and s == 0), stop=False, skip_group_check=True)
                mm.then_inc(y_part, 1)

            def front(m):
                norm.tensor(pe, m, misc, ident)
                yield
                pe.wait_ge(norm.xt_ready, m + 1)
                route.logits(pe, misc, norm.xt, gate)
                yield
                if capacity is not None:
                    pe.wait_ge(chosen, m + 1)
                    for s in range(G):
                        out = POS[0:T, 16 * s:16 * s + experts]
                        pe.matmul(out, ones[:], before[:, s, :], start=True, stop=False)
                        mm = pe.matmul(out, upto[:], route.mark[:, s, 0:experts], start=False, stop=True)
                    mm.then_inc(placed, 1)
                    yield
                route.turn(pe, m, misc, ident)
                yield

            def blocks(n, steps):
                pe.wait_ge(xt_carried, n + 1)
                for e in range(BLOCKS + 1):
                    if e < BLOCKS:
                        hidden(n, e)
                    if e >= 1:
                        output(n, e - 1)
                    if e in pe_at:
                        next(steps, None)
                for s in range(G):
                    mm = pe.matmul(Y[0:T, E * s:E * s + E], route.combt[0:experts, T * s:T * s + T], b2[:],
                                   start=False, stop=True, skip_group_check=True)
                mm.then_inc(y_done, 1)

            for _ in front(0):
                pass
            with pe.Fori(0, NG - 1) as n:
                blocks(n, front(n + 1))
            blocks(NG - 1, iter(()))

        @block.scalar
        def _(act):
            def front(m):
                norm.deviation(act, m)
                yield
                norm.copy_turned(act, m, misc)
                yield
                route.exponential(act, m + 1)
                yield

            def carry(m):
                act.wait_ge(norm.xt_ready, m + 1)
                act.activation(xt[:], norm.xt[:], ACT.Copy).then_inc(xt_carried, 1)

            def blocks(n, steps):
                for e in range(BLOCKS):
                    act.wait_ge(h_done, BLOCKS * n + e + 1)
                    if e >= 2:
                        act.wait_ge(hw_ready, BLOCKS * n + e - 1)
                    act.activation(relu[:, e % 2], HB[e % 2][:, 0:TG], ACT.Relu).then_inc(r_ready, 1)
                    if e in act_at:
                        next(steps, None)

            def finish(n):
                if capacity is None:
                    act.wait_ge(norm2.var_ready, n + 1)
                    act.activation(norm2.st[:, 3], norm2.st[:, 2], ACT.Sqrt).then_inc(norm2.std_ready, 1)

            act.wait_ge(consts_in, 16 * len(consts))
            act.activation(pick16[:], pick[:], ACT.Copy).then_inc(pick_ready, 1)
            for _ in front(0):
                pass
            carry(0)
            route.turned(act, 0, misc, combt16)
            with act.Fori(0, NG - 1) as n:
                blocks(n, front(n + 1))
                carry(n + 1)
                act.wait_ge(y_done, n + 1)
                route.turned(act, n + 1, misc, combt16)
                finish(n)
            blocks(NG - 1, iter(()))
            finish(NG - 1)

        @block.vector
        def _(dve):
            first = 5 + (0 if capacity is None else 1)
            setup = Link(dve, link_dve, 0, first)
            norm.pads(dve, setup)
            route.pads(dve, setup)
            if capacity is not None:
                setup(dve.memset(before[:], 0.0))
            setup.done()
            dve.wait_ge(consts_in, 16 * len(consts))
            def front(m):
                link = Link(dve, link_front, m, per_front)
                yield from norm.steps(dve, link, group_of(H, m), m)
                dve.wait_ge(route.logits_done, m + 1)
                logits = misc[0:T, 0:16 * G].rearrange("p (s x) -> p s x", s=G)[:, :, 0:experts]
                if capacity is None:
                    link(dve.tensor_copy(route.val[:, :, 0:experts], logits))
                    yield from route.choose_steps(dve, link, 2)
                    yield from route.share_steps(dve, link, m + 1, weights_ready)
                else:
                    yield from route.softmax_steps(dve, link, logits, m + 1, route.val[:, :, 0:experts])
                    yield from route.choose_steps(dve, link, 1)
                    mark = route.mark[:, :, 0:experts]
                    for s in range(G):
                        ins = dve.tensor_tensor(before[:, s + 1], before[:, s], mark[:, s], ALU.add)
                        if s < G - 1:
                            link(ins)
                    ins.then_inc(chosen, 1)
                    yield
                    dve.wait_ge(placed, m + 1)
                    dve.wait_ge(chosen, m + 1)
                    link(dve.tensor_copy(before[:, 0], before[:, G]))
                    pos = POS[0:T, 0:16 * G].rearrange("p (s x) -> p s x", s=G)[:, :, 0:experts]
                    link(dve.tensor_scalar(kept[:], pos, float(capacity), None, ALU.is_le))
                    link(dve.tensor_tensor(kept[:], kept[:], mark, ALU.mult))
                    dve.tensor_tensor(route.comb[:, :, 0:experts], kept[:], route.val[:, :, 0:experts],
                                      ALU.mult).then_inc(weights_ready, 1)
                dve.wait_ge(weights_ready, m + 1)
                comb = route.comb[:, :, 0:experts]
                link(dve.tensor_copy(piece[:, :, 0], comb))
                link(dve.tensor_tensor(rest[:], comb, piece[:, :, 0], ALU.subtract))
                link(dve.tensor_copy(piece[:, :, 1], rest[:]))
                link(dve.tensor_tensor(piece[:, :, 2], rest[:], piece[:, :, 1], ALU.subtract))
                dve.tensor_copy(route.comb[:, :, PIECES:PIECES + 3 * experts],
                                piece[:].rearrange("t s k x -> t s (k x)")).then_inc(route.comb_ready, 1)
                link.done()
                yield

            def blocks(n, steps):
                link = Link(dve, link_dve, n, per, first)
                h = group_of(H, n)
                if capacity is None:
                    dve.wait_ge(norm.xn_ready, n + 1)
                    link(dve.tensor_copy(xkeep[:], norm.xn[:, :, 0:E]))
                for e in range(BLOCKS):
                    dve.wait_ge(r_ready, BLOCKS * n + e + 1)
                    dve.wait_ge(c_done, BLOCKS * n + e + 1)
                    if e >= 2:
                        dve.wait_ge(y_part, BLOCKS * n + e - 1)
                    dve.tensor_tensor(hw[:, e % 2], relu[:, e % 2], CB[e % 2][:, 0:TG], ALU.mult).then_inc(hw_ready, 1)
                    if e in dve_at:
                        next(steps, None)
                for _ in steps:
                    assert False, "steps left after the blocks"
                dve.wait_ge(y_done, n + 1)
                moe = Y[0:T, 0:G * E].rearrange("p (s e) -> p s e", s=G)
                if capacity is None:
                    link(dve.tensor_tensor(y[:], xkeep[:], moe, ALU.add))
                    norm2.moments(dve, link, y[:], norm2.var_ready)
                    dve.wait_ge(norm2.std_ready, n + 1)
                    link(dve.reciprocal(norm2.st[:, 4], norm2.st[:, 3]))
                    link(dve.tensor_tensor(y[:], norm2.xc[:], over(norm2.st[:, 4], E), ALU.mult))
                    link(dve.tensor_tensor(y[:], y[:], gamma[:].unsqueeze(1).to_broadcast([T, G, E]), ALU.mult))
                    link(dve.tensor_tensor(y[:], y[:], beta[:].unsqueeze(1).to_broadcast([T, G, E]), ALU.add))
                else:
                    link(dve.tensor_copy(y[:], moe))
                    link(dve.tensor_scalar(fix[:], y[:], -1e4, 1e4, ALU.max, ALU.min))
                    link(dve.tensor_tensor(fin[:], y[:], y[:], ALU.is_equal))
                    link(dve.tensor_tensor(fix[:], fix[:], fin[:], ALU.mult))
                    link(dve.tensor_scalar(fin[:], y[:], 0.0, 0.0, ALU.mult, ALU.is_equal))
                    dve.memset(route.spare[:, 2:3], 0.0)
                    link(dve.copy_predicated(fix[:], fin[:].bitcast(mybir.dt.int32), y[:]))
                out = y if capacity is None else fix
                link(dve.tensor_tensor(h, h, out[:], ALU.add))
                link.done()

            for _ in front(0):
                pass
            with dve.Fori(0, NG - 1) as n:
                blocks(n, front(n + 1))
            blocks(NG - 1, iter(()))


def build_mlp0(nc, d, H):
    build_routed_mlp(nc, d, H, "f0", 16, None)


def build_mlp1(nc, d, H):
    tokens = S * T
    build_routed_mlp(nc, d, H, "f1", 8, -(-tokens * 5 // (4 * 8)))


def build_linear_attention(nc, d, H):
    with Stage(nc) as ctx:
        def sb(name, shape):
            return ctx.enter_context(nc.sbuf_tensor(f"l1_{name}", shape, F32))

        def sem(name):
            return ctx.sem(f"l1_{name}")

        psum = [ctx.enter_context(nc.psum_tensor(f"l1_ps{k}", [128, 512], F32)) for k in range(6)]
        misc, QK, VB, EB, LB, OB = psum
        norm = Norm(ctx, nc, "l1n")
        ident = sb("ident", [128, 128])
        wq, wk, wv = sb("wq", [E + 1, E]), sb("wk", [E + 1, E]), sb("wv", [E + 1, E])
        gamma, beta = sb("gamma", [E, 1]), sb("beta", [E, 1])
        qall = sb("qall", [E, NG, TG])
        lam, cen = sb("lam", [E, S, E]), sb("cen", [E, S, E])
        ek, etok, vtok = sb("ek", [E, G, T]), sb("etok", [T, G, E]), sb("vtok", [T, G, E])
        top, den = sb("top", [E, G]), sb("den", [E, G])
        bn = sb("bn", [E, 8])
        qg = sb("qg", [E, TG])
        consts = [(ident, "ident"), (wq, "l1_wq"), (wk, "l1_wk"), (wv, "l1_wv"), (gamma, "l1_gamma"),
                  (beta, "l1_beta")]
        consts_in, link_dve, link_norm = sem("consts_in"), sem("link_dve"), sem("link_norm")
        k_done, q_done, q_ready, v_done, v_ready = (
            sem("k_done"), sem("q_done"), sem("q_ready"), sem("v_done"), sem("v_ready"))
        e_in, e_out, e_turned, etok_ready, lam_done = (
            sem("e_in"), sem("e_out"), sem("e_turned"), sem("etok_ready"), sem("lam_done"))
        h_done = sem("h_done")
        bvar_ready, bstd_ready, bn_ready, qg_ready, o_done = (
            sem("bvar_ready"), sem("bstd_ready"), sem("bn_ready"), sem("qg_ready"), sem("o_done"))
        start_at_base(nc, [h_done, o_done])
        block = ctx.block()
        per = 1 + 1 + 1 + 1
        bn_links = 9

        @block.sync
        def _(sp):
            for dst, name in consts:
                sp.dma_start(dst[:], d[name]).then_inc(consts_in, 16)

        @block.tensor
        def _(pe):
            pe.wait_ge(consts_in, 16 * len(consts))
            with pe.Fori(0, NG) as n:
                norm.tensor(pe, n, misc, ident)
                pe.wait_ge(norm.xt_ready, n + 1)
                for s in range(G):
                    mm = pe.matmul(VB[0:T, E * s:E * s + E], norm.xt[:, T * s:T * s + T], wv[:], start=True, stop=True)
                mm.then_inc(v_done, 1)
                pe.matmul(QK[0:E, 0:TG], wk[:], norm.xt[:], start=True, stop=True).then_inc(k_done, 1)
                pe.wait_ge(e_out, n + 1)
                pe.matmul(LB[0:E, 0:TG], wq[:], norm.xt[:], start=True, stop=True).then_inc(q_done, 1)
                for s in range(G):
                    mm = pe.transpose(EB[0:T, E * s:E * s + E], ek[:, s, :], ident[0:E, 0:E])
                mm.then_inc(e_turned, 1)
                pe.wait_ge(etok_ready, n + 1)
                pe.wait_ge(v_ready, n + 1)
                pe.wait_ge(q_ready, n + 1)
                for s in range(G):
                    mm = pe.matmul(LB[0:E, E * s:E * s + E], etok[:, s, :], vtok[:, s, :], start=True, stop=True)
                mm.then_inc(lam_done, 1)
            with pe.Fori(0, NG) as n:
                pe.wait_ge(bn_ready, 1)
                pe.wait_ge(qg_ready, n + 1)
                pe.wait_ge(h_done, BASE + n)
                for s in range(G):
                    mm = pe.matmul(OB[0:T, E * s:E * s + E], qg[:, T * s:T * s + T],
                                   lam[:, bass.ds(G * n + s, 1), :], start=True, stop=True)
                mm.then_inc(o_done, 1)

        @block.scalar
        def _(act):
            def group(n, last):
                norm.copy_turned(act, n, misc)
                act.wait_ge(v_done, n + 1)
                act.activation(vtok[:], VB[0:T, 0:G * E].rearrange("p (s e) -> p s e", s=G), ACT.Copy).then_inc(v_ready, 1)
                act.wait_ge(e_in, n + 1)
                act.activation(ek[:], ek[:], ACT.Exp).then_inc(e_out, 1)
                if not last:
                    norm.deviation(act, n + 1)
                act.wait_ge(q_done, n + 1)
                act.activation(qall[:, bass.ds(n, 1), :].rearrange("p o t -> p (o t)"), LB[0:E, 0:TG], ACT.Copy).then_inc(q_ready, 1)
                act.wait_ge(e_turned, n + 1)
                act.activation(etok[:], EB[0:T, 0:G * E].rearrange("p (s e) -> p s e", s=G), ACT.Copy).then_inc(etok_ready, 1)

            norm.deviation(act, 0)
            with act.Fori(0, NG - 1) as n:
                group(n, False)
            group(NG - 1, True)

            act.wait_ge(bvar_ready, 1)
            act.activation(bn[:, 3:4], bn[:, 2:3], ACT.Sqrt).then_inc(bstd_ready, 1)
            with act.Fori(0, NG) as n:
                act.wait_ge(o_done, BASE + n)
                act.wait_ge(q_ready, NG)
                act.activation(qg[:], qall[:, bass.ds(n, 1), :].rearrange("p o t -> p (o t)"), ACT.Copy).then_inc(qg_ready, 1)

        @block.vector
        def _(dve):
            setup = Link(dve, link_dve, 0, 2)
            norm.pads(dve, setup)
            dve.wait_ge(consts_in, 16 * len(consts))

            def group(n, last):
                ahead = iter(()) if last else norm.steps(dve, Link(dve, link_norm, n + 1, Norm.LINKS),
                                                         group_of(H, n + 1), n + 1)
                link = Link(dve, link_dve, n, per, 2)
                keys = QK[0:E, 0:TG].rearrange("p (s t) -> p s t", s=G)
                dve.wait_ge(k_done, n + 1)
                link(dve.tensor_reduce(top[:], keys, AX.X, ALU.max))
                dve.tensor_tensor(ek[:], keys, over(top[:], T), ALU.subtract).then_inc(e_in, 1)
                next(ahead, None)
                next(ahead, None)
                dve.wait_ge(e_out, n + 1)
                link(dve.tensor_reduce(den[:], ek[:], AX.X, ALU.add))
                link(dve.reciprocal(den[:], den[:]))
                next(ahead, None)
                dve.wait_ge(lam_done, n + 1)
                link(dve.tensor_tensor(lam[:, bass.ds(G * n, G), :],
                                       LB[0:E, 0:G * E].rearrange("p (s e) -> p s e", s=G),
                                       over(den[:], E), ALU.mult))
                link.done()

            norm.vector(dve, Link(dve, link_norm, 0, Norm.LINKS), group_of(H, 0), 0)
            with dve.Fori(0, NG - 1) as n:
                group(n, False)
            group(NG - 1, True)
            link = Link(dve, link_dve, NG, per, 2)
            size = 1.0 / (S * E)
            flat = lam[:].rearrange("p s e -> p (s e)")
            cflat = cen[:].rearrange("p s e -> p (s e)")
            link(dve.tensor_reduce(bn[:, 0:1], flat, AX.X, ALU.add))
            link(dve.tensor_scalar(bn[:, 0:1], bn[:, 0:1], size, None, ALU.mult))
            link(dve.tensor_scalar(flat, flat, bn[:, 0:1], None, ALU.subtract))
            link(dve.tensor_tensor(cflat, flat, flat, ALU.mult))
            link(dve.tensor_reduce(bn[:, 1:2], cflat, AX.X, ALU.add))
            dve.tensor_scalar(bn[:, 2:3], bn[:, 1:2], size, EPS, ALU.mult, ALU.add).then_inc(bvar_ready, 1)
            dve.wait_ge(bstd_ready, 1)
            link(dve.reciprocal(bn[:, 4:5], bn[:, 3:4]))
            link(dve.tensor_tensor(bn[:, 5:6], bn[:, 4:5], gamma[:], ALU.mult))
            dve.tensor_scalar(flat, flat, bn[:, 5:6], beta[:], ALU.mult, ALU.add).then_inc(bn_ready, 1)
            with dve.Fori(0, NG) as n:
                h = group_of(H, n)
                dve.wait_ge(o_done, BASE + n + 1)
                dve.tensor_tensor(h, h, OB[0:T, 0:G * E].rearrange("p (s e) -> p s e", s=G), ALU.add).then_inc(h_done, 1)
                dve.wait_ge(h_done, BASE + n + 1)


def build_gauss_attention(nc, d, H):
    with Stage(nc) as ctx:
        def sb(name, shape):
            return ctx.enter_context(nc.sbuf_tensor(f"a2_{name}", shape, F32))

        def sem(name):
            return ctx.sem(f"a2_{name}")

        psum = [ctx.enter_context(nc.psum_tensor(f"a2_ps{k}", [128, 512], F32)) for k in range(8)]
        norm = Norm(ctx, nc, "a2n")
        att = Attention(ctx, nc, "a2a", psum, gauss=True)
        ident, wqk, wv = sb("ident", [128, 128]), sb("wqk", [E + 1, 8, 128]), sb("wv", [E + 1, 512])
        scale = sb("scale", [T, E])
        consts = [(ident, "ident"), (wqk, "a2_wqk"), (wv, "a2_wv"), (scale, "a2_scale"),
                  (att.wo, "a2_wo"), (att.gamma, "a2_gamma"), (att.ones, "ones128")]
        TURN = psum[4]
        consts_in, link_dve, link_norm = sem("consts_in"), sem("link_dve"), sem("link_norm")
        proj_done, proj_ready = sem("proj_done"), sem("proj_ready")
        block = ctx.block()
        per = att.links + 1

        @block.sync
        def _(sp):
            for dst, name in consts:
                sp.dma_start(dst[:], d[name]).then_inc(consts_in, 16)

        @block.tensor
        def _(pe):
            pe.wait_ge(consts_in, 16 * len(consts))
            with pe.Fori(0, NG) as n:
                norm.tensor(pe, n, TURN, ident)
                pe.wait_ge(norm.xt_ready, n + 1)
                for j in range(12):
                    if j >= 4:
                        pe.wait_ge(proj_ready, 12 * n + j - 3)
                    if j < 8:
                        mm = pe.matmul(psum[j % 4][:, 0:TG], wqk[:, j, :], norm.xt[:], start=True, stop=True)
                    else:
                        s = j - 8
                        mm = pe.matmul(psum[j % 4][0:T, :], norm.xt[:, T * s:T * s + T], wv[:],
                                       start=True, stop=True)
                    mm.then_inc(proj_done, 1)
                pe.wait_ge(proj_ready, 12 * n + 12)
                att.tensor(pe, n, ident)

        @block.scalar
        def _(act):
            def group(n, last):
                norm.copy_turned(act, n, TURN)
                for j in range(12):
                    act.wait_ge(proj_done, 12 * n + j + 1)
                    bank = psum[j % 4]
                    if j < 4:
                        act.activation(att.q2[:, j, :], bank[:, 0:TG], ACT.Square)
                        act.activation(att.qt[:, j, :], bank[:, 0:TG], ACT.Copy).then_inc(proj_ready, 1)
                    elif j < 8:
                        act.activation(att.k2[:, j - 4, :], bank[:, 0:TG], ACT.Square)
                        act.activation(att.kt[:, j - 4, :], bank[:, 0:TG], ACT.Copy, scale=-2.0).then_inc(proj_ready, 1)
                    else:
                        act.activation(att.v[:, j - 8, :], bank[0:T, :], ACT.Copy).then_inc(proj_ready, 1)
                if not last:
                    norm.deviation(act, n + 1)
                att.scalar(act, n)

            norm.deviation(act, 0)
            with act.Fori(0, NG - 1) as n:
                group(n, False)
            group(NG - 1, True)

        @block.vector
        def _(dve):
            setup = Link(dve, link_dve, 0, 2)
            norm.pads(dve, setup)
            dve.wait_ge(consts_in, 16 * len(consts))

            def normalise(m):
                norm.vector(dve, Link(dve, link_norm, m, Norm.LINKS + 1), group_of(H, m), m, scale)

            def group(n, last):
                link = Link(dve, link_dve, n, per, first=2)
                if not last:
                    dve.wait_ge(norm.turned, n + 1)
                    normalise(n + 1)
                att.vector(dve, link, n)
                h = group_of(H, n)
                dve.wait_ge(att.y_done, n + 1)
                link(dve.tensor_tensor(h, h, att.Y[0:T, 0:G * E].rearrange("p (s e) -> p s e", s=G), ALU.add))
                link.done()

            normalise(0)
            with dve.Fori(0, NG - 1) as n:
                group(n, False)
            group(NG - 1, True)


def build_mlp2(nc, d, H):
    UNITS, X = 5, 4
    with Stage(nc) as ctx:
        def sb(name, shape):
            return ctx.enter_context(nc.sbuf_tensor(f"f2_{name}", shape, F32))

        def sem(name):
            return ctx.sem(f"f2_{name}")

        psum = [ctx.enter_context(nc.psum_tensor(f"f2_ps{k}", [128, 512], F32)) for k in range(8)]
        misc, Y, H1, H2, CB = psum[0], psum[1], psum[2:4], psum[4:6], psum[6:8]
        norm = Norm(ctx, nc, "f2n")
        route = Router(ctx, nc, "f2r", X)
        ident, gate = sb("ident", [128, 128]), sb("gate", [E + 1, X])
        w1, w2, b2 = sb("w1", [E + 1, UNITS, 128]), sb("w2", [128, UNITS, 128]), sb("b2", [128, UNITS])
        w3, b3, pick = sb("w3", [128, UNITS, E]), sb("b3", [UNITS, E]), sb("pick", [UNITS, UNITS, 128])
        r1, r2, hw = sb("r1", [128, 2, TG]), sb("r2", [128, 2, TG]), sb("hw", [128, 2, TG])
        consts = [(ident, "ident"), (gate, "f2_gate"), (w1, "f2_w1"), (w2, "f2_w2"), (b2, "f2_b2"),
                  (w3, "f2_w3"), (b3, "f2_b3"), (pick, "f2_pick")]
        consts_in, link_dve, link_front, xt_carried = (
            sem("consts_in"), sem("link_dve"), sem("link_front"), sem("xt_carried"))
        h1_done, r1_ready, h2_done, r2_ready = sem("h1_done"), sem("r1_ready"), sem("h2_done"), sem("r2_ready")
        c_done, hw_ready, y_part, y_done = sem("c_done"), sem("hw_ready"), sem("y_part"), sem("y_done")
        block = ctx.block()
        per_front = Norm.LINKS + 4 + 4 + 4
        xt = sb("xt", [E + 1, TG])
        pe_at, act_at, dve_at = (3, 4), (1, 3, 4, 5), (0, 0, 1, 3, 4, 4, 4)
        first = 6

        @block.sync
        def _(sp):
            for dst, name in consts:
                sp.dma_start(dst[:], d[name]).then_inc(consts_in, 16)

        @block.tensor
        def _(pe):
            pe.wait_ge(consts_in, 16 * len(consts))
            def front(m):
                norm.tensor(pe, m, misc, ident)
                yield
                pe.wait_ge(norm.xt_ready, m + 1)
                route.logits(pe, misc, norm.xt, gate)
                yield

            def units(n, steps):
                pe.wait_ge(xt_carried, n + 1)
                for e in range(UNITS + 2):
                    base = UNITS * n
                    if e < UNITS:
                        if e >= 2:
                            pe.wait_ge(r1_ready, base + e - 1)
                        pe.matmul(H1[e % 2][:, 0:TG], w1[:, e, :], xt[:], start=True, stop=True).then_inc(h1_done, 1)
                    if 1 <= e <= UNITS:
                        k = e - 1
                        pe.wait_ge(r1_ready, base + k + 1)
                        if k >= 2:
                            pe.wait_ge(r2_ready, base + k - 1)
                            pe.wait_ge(hw_ready, base + k - 1)
                        pe.matmul(H2[k % 2][:, 0:TG], w2[:, k, :], r1[:, k % 2], start=True, stop=True).then_inc(h2_done, 1)
                        if k == 0:
                            pe.wait_ge(route.combt_ready, n + 1)
                        pe.matmul(CB[k % 2][:, 0:TG], pick[:, k, :], route.combt[0:UNITS, :],
                                  start=True, stop=True).then_inc(c_done, 1)
                    if e >= 2:
                        k = e - 2
                        pe.wait_ge(hw_ready, base + k + 1)
                        for s in range(G):
                            mm = pe.matmul(Y[0:T, E * s:E * s + E], hw[:, k % 2, T * s:T * s + T], w3[:, k, :],
                                           start=(k == 0 and s == 0), stop=False, skip_group_check=True)
                        mm.then_inc(y_part, 1)
                    for _ in range(pe_at.count(e)):
                        next(steps, None)
                for s in range(G):
                    mm = pe.matmul(Y[0:T, E * s:E * s + E], route.combt[0:UNITS, T * s:T * s + T], b3[:],
                                   start=False, stop=True, skip_group_check=True)
                mm.then_inc(y_done, 1)

            for _ in front(0):
                pass
            route.turn(pe, 0, misc, ident)
            with pe.Fori(0, NG - 1) as n:
                units(n, front(n + 1))
                route.turn(pe, n + 1, misc, ident)
            units(NG - 1, iter(()))

        @block.scalar
        def _(act):
            act.wait_ge(consts_in, 16 * len(consts))
            def front(m):
                norm.deviation(act, m)
                yield
                norm.copy_turned(act, m, misc)
                yield
                route.exponential(act, 2 * m + 1)
                yield
                route.exponential(act, 2 * m + 2)
                yield

            def carry(m):
                act.wait_ge(norm.xt_ready, m + 1)
                act.activation(xt[:], norm.xt[:], ACT.Copy).then_inc(xt_carried, 1)

            def units(n, steps):
                for e in range(UNITS + 1):
                    base = UNITS * n
                    if e < UNITS:
                        act.wait_ge(h1_done, base + e + 1)
                        if e >= 2:
                            act.wait_ge(h2_done, base + e - 1)
                        act.activation(r1[:, e % 2], H1[e % 2][:, 0:TG], ACT.Relu).then_inc(r1_ready, 1)
                    if e >= 1:
                        k = e - 1
                        act.wait_ge(h2_done, base + k + 1)
                        if k >= 2:
                            act.wait_ge(hw_ready, base + k - 1)
                        act.activation(r2[:, k % 2], H2[k % 2][:, 0:TG], ACT.Relu, bias=b2[:, k:k + 1]).then_inc(r2_ready, 1)
                    for _ in range(act_at.count(e)):
                        next(steps, None)

            for _ in front(0):
                pass
            carry(0)
            route.turned(act, 0, misc)
            with act.Fori(0, NG - 1) as n:
                units(n, front(n + 1))
                carry(n + 1)
                act.wait_ge(y_done, n + 1)
                route.turned(act, n + 1, misc)
            units(NG - 1, iter(()))

        @block.vector
        def _(dve):
            setup = Link(dve, link_dve, 0, first)
            norm.pads(dve, setup)
            route.pads(dve, setup)
            setup(dve.memset(route.comb[:, :, X:X + 1], 1.0))
            setup.done()
            dve.wait_ge(consts_in, 16 * len(consts))
            def front(m):
                link = Link(dve, link_front, m, per_front)
                yield from norm.steps(dve, link, group_of(H, m), m)
                dve.wait_ge(route.logits_done, m + 1)
                logits = misc[0:T, 0:16 * G].rearrange("p (s x) -> p s x", s=G)[:, :, 0:X]
                yield from route.softmax_steps(dve, link, logits, 2 * m + 1, route.val[:, :, 0:X])
                yield from route.choose_steps(dve, link, 2)
                yield from route.share_steps(dve, link, 2 * m + 2, route.comb_ready)
                link.done()
                yield

            def units(n, steps):
                for e in range(UNITS):
                    dve.wait_ge(r2_ready, UNITS * n + e + 1)
                    dve.wait_ge(c_done, UNITS * n + e + 1)
                    if e >= 2:
                        dve.wait_ge(y_part, UNITS * n + e - 1)
                    dve.tensor_tensor(hw[:, e % 2], r2[:, e % 2], CB[e % 2][:, 0:TG], ALU.mult).then_inc(hw_ready, 1)
                    for _ in range(dve_at.count(e)):
                        next(steps, None)
                for _ in steps:
                    assert False, "steps left after the units"
                dve.wait_ge(y_done, n + 1)
                h = group_of(H, n)
                dve.tensor_tensor(h, h, Y[0:T, 0:G * E].rearrange("p (s e) -> p s e", s=G), ALU.add).then_inc(link_dve, 1)
                dve.wait_ge(link_dve, first + n + 1)

            for _ in front(0):
                pass
            with dve.Fori(0, NG - 1) as n:
                units(n, front(n + 1))
            units(NG - 1, iter(()))


def build_diff_attention(nc, d, H):
    CH = 16
    NC = T // CH
    PER = 2 * NC
    with Stage(nc) as ctx:
        def sb(name, shape):
            return ctx.enter_context(nc.sbuf_tensor(f"a3_{name}", shape, F32))

        def sem(name):
            return ctx.sem(f"a3_{name}")

        psum = [ctx.enter_context(nc.psum_tensor(f"a3_ps{k}", [128, 512], F32)) for k in range(8)]
        misc, QP, KP, VB, A, PT = psum[0], psum[1], psum[2], psum[3], psum[4:6], psum[6:8]
        TURN = VB
        norm = Norm(ctx, nc, "a3n")
        ident = sb("ident", [128, 128])
        wq, wk, wv = sb("wq", [E, E]), sb("wk", [E, E]), sb("wv", [E, E])
        wm, bm = sb("wm", [128, 4]), sb("bm", [T, 1])
        qp, kp, vt = sb("qp", [128, 2, T]), sb("kp", [128, 2, T]), sb("vt", [T, G, E])
        diff = sb("diff", [128, 2, CH, T])
        sc = sb("sc", [T, 2, 4, T])
        pt = sb("pt", [T, 2, 4, T])
        sums = sb("sums", [T, 2, 2, 4])
        consts = [(ident, "ident"), (wq, "a3_wq"), (wk, "a3_wk"), (wv, "a3_wv"), (wm, "a3_wm"), (bm, "a3_bm")]
        consts_in, link_dve, link_norm = sem("consts_in"), sem("link_dve"), sem("link_norm")
        q_done, k_done, v_done, qk_ready, v_ready = sem("q_done"), sem("k_done"), sem("v_done"), sem("qk_ready"), sem("v_ready")
        sub_done, relu_done, chunk_done = sem("sub_done"), sem("relu_done"), sem("chunk_done")
        sc_ready, exp_done, p_ready, pt_done, pt_ready, o_done = (
            sem("sc_ready"), sem("exp_done"), sem("p_ready"), sem("pt_done"), sem("pt_ready"), sem("o_done"))
        block = ctx.block()
        per = 2 * 2 + 2 * 2 + 1

        @block.sync
        def _(sp):
            for dst, name in consts:
                sp.dma_start(dst[:], d[name]).then_inc(consts_in, 16)

        @block.tensor
        def _(pe):
            pe.wait_ge(consts_in, 16 * len(consts))
            with pe.Fori(0, NG) as n:
                norm.tensor(pe, n, TURN, ident)
                pe.wait_ge(norm.xt_ready, n + 1)
                x = norm.xt
                for s in range(G):
                    mm = pe.matmul(VB[0:T, E * s:E * s + E], x[0:E, T * s:T * s + T], wv[:], start=True, stop=True)
                mm.then_inc(v_done, 1)
                for bank, w, done in ((QP, wq, q_done), (KP, wk, k_done)):
                    for s in range(G):
                        p = slice(64 * (s % 2), 64 * (s % 2) + 64)
                        mm = pe.matmul(bank[p, T * (s // 2):T * (s // 2) + T], w[:], x[0:E, T * s:T * s + T],
                                       start=True, stop=True, skip_group_check=True)
                    mm.then_inc(done, 1)
                for pair in range(2):
                    for c in range(NC):
                        pe.wait_ge(relu_done, PER * n + NC * pair + c + 1)
                        for k in range(CH):
                            key = CH * c + k
                            mm = pe.matmul(A[pair][0:T, 4 * key:4 * key + 4], diff[:, c % 2, k, :], wm[:],
                                           start=True, stop=True)
                        mm.then_inc(chunk_done, 1)
                for pair in range(2):
                    pe.wait_ge(p_ready, 2 * n + pair + 1)
                    if pair == 0:
                        pe.wait_ge(v_ready, n + 1)
                    for k in range(4):
                        mm = pe.transpose(PT[pair][0:T, T * k:T * k + T], sc[:, pair, k, :], ident[0:T, 0:T])
                    mm.then_inc(pt_done, 1)
                for pair in range(2):
                    pe.wait_ge(pt_ready, 2 * n + pair + 1)
                    for k in range(4):
                        s, g = 2 * pair + k // 2, k % 2
                        out = misc[0:T, E * s:E * s + E].rearrange("p (e g) -> p g e", g=2)[:, g, :]
                        mm = pe.matmul(out, pt[:, pair, k, :], vt[:, s, 32 * g:32 * g + 32], start=True, stop=True)
                mm.then_inc(o_done, 1)

        @block.scalar
        def _(act):
            def group(n, last):
                norm.copy_turned(act, n, TURN)
                act.wait_ge(q_done, n + 1)
                act.activation(qp[:].rearrange("p a t -> p (a t)"), QP[:, 0:2 * T], ACT.Copy)
                act.wait_ge(k_done, n + 1)
                act.activation(kp[:].rearrange("p a t -> p (a t)"), KP[:, 0:2 * T], ACT.Copy).then_inc(qk_ready, 1)
                act.activation(vt[:].rearrange("p s e -> p (s e)"), VB[0:T, 0:G * E], ACT.Copy).then_inc(v_ready, 1)
                for c in range(PER):
                    act.wait_ge(sub_done, PER * n + c + 1)
                    act.activation(diff[:, c % 2], diff[:, c % 2], ACT.Relu).then_inc(relu_done, 1)
                    if c == 3 and not last:
                        norm.deviation(act, n + 1)
                for pair in range(2):
                    act.wait_ge(sc_ready, 2 * n + pair + 1)
                    act.activation(sc[:, pair], sc[:, pair], ACT.Exp).then_inc(exp_done, 1)
                for pair in range(2):
                    act.wait_ge(pt_done, 2 * n + pair + 1)
                    act.activation(pt[:, pair].rearrange("p k t -> p (k t)"), PT[pair][0:T, 0:4 * T],
                                   ACT.Copy).then_inc(pt_ready, 1)

            norm.deviation(act, 0)
            with act.Fori(0, NG - 1) as n:
                group(n, False)
            group(NG - 1, True)

        @block.vector
        def _(dve):
            setup = Link(dve, link_dve, 0, 2)
            norm.pads(dve, setup)
            dve.wait_ge(consts_in, 16 * len(consts))

            def group(n, last):
                link = Link(dve, link_dve, n, per, first=2)
                h = group_of(H, n)
                ahead = iter(()) if last else norm.steps(dve, Link(dve, link_norm, n + 1, Norm.LINKS), group_of(H, n + 1), n + 1)
                dve.wait_ge(qk_ready, n + 1)
                for pair in range(2):
                    for c in range(NC):
                        k = NC * pair + c
                        if k >= 2:
                            dve.wait_ge(chunk_done, PER * n + k - 1)
                        q = qp[:, pair].unsqueeze(1).to_broadcast([128, CH, T])
                        dve.tensor_tensor(diff[:, k % 2], q, over(kp[:, pair, CH * c:CH * c + CH], T),
                                          ALU.subtract).then_inc(sub_done, 1)
                        if k in (1, 2, 5):
                            next(ahead, None)
                for pair in range(2):
                    dve.wait_ge(chunk_done, PER * n + NC * (pair + 1))
                    dst = sc[:, pair]
                    src = A[pair][0:T, 0:4 * T].rearrange("p (k c) -> p c k", c=4)
                    link(dve.tensor_scalar(dst, src, bm[:], 0.0, ALU.add, ALU.max))
                    link(dve.tensor_reduce(sums[:, pair, 0], dst, AX.X, ALU.max))
                    dve.tensor_tensor(dst, dst, over(sums[:, pair, 0], T), ALU.subtract).then_inc(sc_ready, 1)
                for pair in range(2):
                    dst, den = sc[:, pair], sums[:, pair, 1]
                    dve.wait_ge(exp_done, 2 * n + pair + 1)
                    link(dve.tensor_reduce(den, dst, AX.X, ALU.add))
                    link(dve.reciprocal(den, den))
                    dve.tensor_tensor(dst, dst, over(den, T), ALU.mult).then_inc(p_ready, 1)
                    dve.wait_ge(p_ready, 2 * n + pair + 1)
                dve.wait_ge(o_done, n + 1)
                link(dve.tensor_tensor(h, h, misc[0:T, 0:G * E].rearrange("p (s e) -> p s e", s=G), ALU.add))
                link.done()

            norm.vector(dve, Link(dve, link_norm, 0, Norm.LINKS), group_of(H, 0), 0)
            with dve.Fori(0, NG - 1) as n:
                group(n, False)
            group(NG - 1, True)


def build_product_keys(nc, d, H):
    TOP, HALF = 16, 64
    NT = HALF * HALF // 128
    SHIFT = -40.0
    counts = [TOP // (a + 1) for a in range(TOP // 2)]
    starts = [sum(counts[:a]) for a in range(TOP // 2)]
    NCAND = sum(counts) + TOP // 2
    with Stage(nc) as ctx:
        def sb(name, shape, dtype=F32):
            return ctx.enter_context(nc.sbuf_tensor(f"pk_{name}", shape, dtype))

        def sem(name):
            return ctx.sem(f"pk_{name}")

        psum = [ctx.enter_context(nc.psum_tensor(f"pk_ps{k}", [128, 512], F32)) for k in range(8)]
        SC, KV, KT, misc = psum[0:4], psum[4:6], psum[6], psum[7]
        QUERY, SCORES, RANK, RANK_END, TURN, PER_TILE = 0, (1, 4), 7, 52, (55, 59), 2
        norm = Norm(ctx, nc, "pkn")
        att = Attention(ctx, nc, "pka", psum)
        ident = sb("ident", [128, 128])
        wpk, wq, kbd = sb("wpk", [E, 4, 128]), sb("wq", [E, 4, 128]), sb("kbd", [128, 4, 256])
        QK = 16
        sel = sb("sel", [128, 1 + QK // 2, 128], BF16)
        stack = sb("stack", [128, 2, 1 + HALF // QK, TG], BF16)
        MOVES = 3 + 3 * (HALF // QK)
        piece = sb("piece", [128, 2, 3, TG], BF16)
        rest, idle = sb("rest", [128, TG]), sb("idle", [128, 2])
        selw = sb("selw", [128, (1 + QK // 2) * 128])
        qpk = sb("qpk", [128, 4, TG])
        qs = sb("qs", [128, 4, T])
        sim = sb("sim", [T, HEADS, 2, HALF])
        left = sb("left", [T, HEADS, 2, HALF])
        t16 = sb("t16", [T, HEADS, 2, TOP])
        cand, cleft, c16 = sb("cand", [T, HEADS, NCAND]), sb("cleft", [T, HEADS, NCAND]), sb("c16", [T, HEADS, TOP])
        size = sb("size", [T, HEADS, 2, 2])
        thr, spare = sb("thr", [T, 4, HEADS]), sb("spare", [T, 6])
        cexp = sb("cexp", [T, HEADS, TOP])
        rsum = sb("rsum", [T, HEADS])
        rden, next_rden = sb("rden", [T, G, HEADS]), sb("next_rden", [T, G, HEADS])
        shift = sb("shift", [128, 1])
        st, next_st, next_qt = sb("st", [128, HEADS, TG]), sb("next_st", [128, HEADS, TG]), sb("next_qt", [128, 4, TG])
        table = sb("table", [128, 2, NT, 128])
        ex, wt = sb("ex", [128, 4, TG]), sb("wt", [128, 4, TG])
        kvs = sb("kvs", [128, TG])
        ktok = sb("ktok", [T, G, 512])
        consts = [(ident, "ident"), (wpk, "pk_wpk"), (wq, "pk_wq"), (kbd, "pk_kbd"),
                  (att.wo, "pk_wo"), (att.mask, "mask_causal")]
        consts_in, link_dve = sem("consts_in"), sem("link_dve")
        proj_done, proj_ready = sem("proj_done"), sem("proj_ready")
        sim_done, sim_ready, simt_ready, st_done, st_ready = (
            sem("sim_done"), sem("sim_ready"), sem("simt_ready"), sem("st_done"), sem("st_ready"))
        sel_in, sel_ready = sem("sel_in"), sem("sel_ready")
        piece_ready, link_pool, carried = sem("piece_ready"), sem("link_pool"), sem("carried")
        stack_in, cleared = [sem(f"stack_in{u}") for u in range(2)], sem("cleared")
        qs_ready, link_rank, link_att = sem("qs_ready"), sem("link_rank"), sem("link_att")
        den_in, den_out, rden_ready = sem("den_in"), sem("den_out"), sem("rden_ready")
        table_in = [sem(f"table_in{u}") for u in range(2)]
        sc_done, ex_ready, wt_ready, kv_step = sem("sc_done"), sem("ex_ready"), sem("wt_ready"), sem("kv_step")
        kvs_ready, kvt_done, kvn_ready = sem("kvs_ready"), sem("kvt_done"), sem("kvn_ready")
        kt_done, kt_ready = sem("kt_done"), sem("kt_ready")
        start_at_base(nc, [kvs_ready, kvn_ready, carried, *stack_in])
        block = ctx.block()
        RANK_LINKS = 3 + 1 + 3 + 4 + 3

        @block.sync
        def _(sp):
            for dst, name in consts:
                sp.dma_start(dst[:], d[name]).then_inc(consts_in, 16)

            sp.dma_start(selw[:], d["pk_sel"].rearrange("p t k -> p (t k)")).then_inc(sel_in, 16)

            def load(h):
                sp.dma_start(table[:, h % 2], d["pk_table"][h]).then_inc(table_in[h % 2], 16)

            def move(u, count):
                sp.wait_ge(piece_ready, count)
                moves = [(stack[0:64, u, 0], piece[0:64, u, 0]), (stack[64:128, u, 0], piece[0:64, u, 1]),
                         (stack[0:64, u, 1:], piece[0:64, u, 2].unsqueeze(1).to_broadcast([64, HALF // QK, TG]))]
                for q in range(HALF // QK):
                    for j in range(3):
                        to, fr = 64 + QK * j, 64 + QK * q
                        moves.append((stack[to:to + QK, u, 1 + q], piece[fr:fr + QK, u, j]))
                for dst, src in moves:
                    sp.dma_start(dst, src).then_inc(stack_in[u], 16)

            def next_pair(n, pair):
                for u in range(2):
                    sp.wait_ge(kv_step, 256 * n + 64 * pair + 32 * (u + 1))
                    load((2 * pair + 2 + u) % HEADS)
                    move(u, HEADS * n + 2 * pair + 3 + u)

            load(0)
            load(1)
            sp.wait_ge(cleared, 1)
            move(0, 1)
            move(1, 2)
            with sp.Fori(0, NG - 1) as n:
                for pair in range(4):
                    next_pair(n, pair)
            for pair in range(3):
                next_pair(NG - 1, pair)

        @block.gpsimd
        def _(pool):
            pool.wait_ge(sel_in, 16)
            pool.tensor_copy(sel[:].rearrange("p t k -> p (t k)"), selw[:]).then_inc(sel_ready, 1)
            pool.memset(stack[:].rearrange("p u b t -> p (u b t)"), 0.0).then_inc(cleared, 1)
            pool.memset(idle[:], 0.0).then_inc(link_pool, 1)
            pool.wait_ge(link_pool, 1)

            def carry(m):
                pool.wait_ge(st_ready, 2 * G * m + 2 * G)
                pool.wait_ge(rden_ready, G * m + G)
                take_wait()
                pool.tensor_copy(st[:], next_st[:])
                pool.tensor_copy(rden[:], next_rden[:])
                pool.tensor_copy(att.qt[:], next_qt[:]).then_inc(carried, 1)
                pool.wait_ge(carried, BASE + m + 1)

            def take_wait():
                pool.tensor_tensor(idle[:, 0:1], idle[:, 1:2], idle[:, 1:2], ALU.add)

            def pieces(n):
                link = Link(pool, link_pool, n, 4 * HEADS, first=1)
                for h in range(HEADS):
                    u, now = h % 2, st[:, h, :]
                    pool.wait_ge(stack_in[u], BASE + 16 * MOVES * (HEADS // 2 * n + h // 2))
                    take_wait()
                    link(pool.tensor_copy(piece[:, u, 0], now))
                    link(pool.tensor_tensor(rest[:], now, piece[:, u, 0], ALU.subtract))
                    take_wait()
                    link(pool.tensor_copy(piece[:, u, 1], rest[:]))
                    link(pool.tensor_tensor(piece[:, u, 2], rest[:], piece[:, u, 1], ALU.subtract))
                    pool.sem_inc(piece_ready, 1)

            carry(0)
            with pool.Fori(0, NG - 1) as n:
                pieces(n)
                pool.wait_ge(att.s_done, G * n + G)
                carry(n + 1)
            pieces(NG - 1)

        @block.tensor
        def _(pe):
            pe.wait_ge(consts_in, 16 * len(consts))
            pe.wait_ge(sel_ready, 1)

            def sample_steps(k):
                pe.wait_ge(qs_ready, k + 1)
                for p in range(2):
                    if p == 1:
                        pe.wait_ge(sim_ready, 2 * k + 1)
                    for t in range(2):
                        mm = pe.matmul(misc[0:T, 256 * t:256 * t + 256], qs[:, 2 * p + t, :], kbd[:, 2 * p + t, :],
                                       start=True, stop=True)
                    mm.then_inc(sim_done, 1)
                    yield
                for p in range(2):
                    if p == 0:
                        pe.wait_ge(simt_ready, k + 1)
                    else:
                        pe.wait_ge(st_ready, 2 * k + 1)
                    for h in range(4):
                        mm = pe.transpose(misc[:, T * h:T * h + T],
                                          sim[:, 4 * p + h].rearrange("p a b -> p (a b)"), ident[0:T, 0:T])
                    mm.then_inc(st_done, 1)
                    yield

            def project(m):
                norm.tensor(pe, m, misc, ident)
                pe.wait_ge(norm.xt_ready, m + 1)
                for j in range(8):
                    if j >= 4:
                        pe.wait_ge(proj_ready, 8 * m + j - 3)
                    w = (wpk, wq)[j // 4]
                    pe.matmul(psum[j % 4][:, 0:TG], w[:, j % 4, :], norm.xt[0:E, :], start=True,
                              stop=True).then_inc(proj_done, 1)

            def two_heads(n, hh, steps):
                base = 256 * n + 64 * hh
                for j in range(2 * NT + 2):
                    u, t = j // NT, j % NT
                    if j < 2 * NT:
                        if t == 0:
                            pe.wait_ge(stack_in[u], BASE + 16 * MOVES * (HEADS // 2 * n + hh + 1))
                        if j >= 4:
                            pe.wait_ge(wt_ready, base + j - 3)
                        pe.matmul(SC[j % 4][:, 0:TG], sel[:, 0, :], stack[:, u, 0], start=True, stop=False)
                        pe.matmul(SC[j % 4][:, 0:TG], sel[:, 1 + t % (QK // 2), :], stack[:, u, 1 + t // (QK // 2)],
                                  start=False, stop=True).then_inc(sc_done, 1)
                    if j >= 2:
                        v, k = (j - 2) // NT, (j - 2) % NT
                        if k == 0:
                            pe.wait_ge(table_in[v], 64 * n + 16 * hh + 16)
                        pe.wait_ge(wt_ready, base + j - 1)
                        mm = pe.matmul(KV[v][:, 0:TG], table[:, v, k, :], wt[:, (j - 2) % 4], start=(k == 0),
                                       stop=(k == NT - 1))
                        mm.then_inc(kv_step, 1)
                    if j == NT + 8:
                        pe.wait_ge(kvn_ready, BASE + HEADS * n + 2 * hh)
                        turn_kv(n, hh, 0)
                    if j in SCORES + TURN:
                        next(steps, None)
                pe.wait_ge(kvn_ready, BASE + HEADS * n + 2 * hh + 1)
                turn_kv(n, hh, 1)

            def turn_kv(n, hh, u):
                pe.wait_ge(kvs_ready, BASE + HEADS * n + 2 * hh + u + 1)
                for s in range(G):
                    mm = pe.transpose(KT[0:T, 128 * s:128 * s + 128], kvs[:, T * s:T * s + T], ident[:])
                mm.then_inc(kvt_done, 1)

            def heads_and_attention(n, ahead):
                with pe.Fori(0, HEADS // 2) as hh:
                    pe.wait_ge(proj_ready, 8 * n + (16 if ahead else 8))
                    two_heads(n, hh, sample_steps(G * n + G + hh) if ahead else iter(()))
                for s in range(G):
                    if s == 0:
                        pe.wait_ge(kvn_ready, BASE + HEADS * n + HEADS)
                    else:
                        pe.wait_ge(kt_ready, G * n + s)
                    for j in range(4):
                        mm = pe.transpose(KT[:, T * j:T * j + T], ktok[:, s, 128 * j:128 * j + 128], ident[0:T, 0:T])
                    mm.then_inc(kt_done, 1)
                pe.wait_ge(kt_ready, G * n + G)
                pe.wait_ge(carried, BASE + n + 1)
                att.tensor(pe, n, ident)

            project(0)
            with pe.Fori(0, G) as s:
                for _ in sample_steps(s):
                    pass
            pe.wait_ge(st_ready, 2 * G)
            with pe.Fori(0, NG - 1) as n:
                project(n + 1)
                heads_and_attention(n, True)
            heads_and_attention(NG - 1, False)

        @block.scalar
        def _(act):
            def project(m):
                norm.scalar(act, m, misc)
                act.wait_ge(carried, BASE + m)
                for j in range(8):
                    act.wait_ge(proj_done, 8 * m + j + 1)
                    dst = (qpk, next_qt)[j // 4]
                    act.activation(dst[:, j % 4, :], psum[j % 4][:, 0:TG], ACT.Copy).then_inc(proj_ready, 1)

            def sample_steps(m, s):
                k = G * m + s
                act.wait_ge(proj_ready, 8 * m + 8)
                act.activation(qs[:], qpk[:, :, bass.ds(T * s, T)], ACT.Copy).then_inc(qs_ready, 1)
                yield
                for p in range(2):
                    act.wait_ge(sim_done, 2 * k + p + 1)
                    act.activation(sim[:, :, p, :], misc[0:T, :].rearrange("q (h k) -> q h k", h=HEADS),
                                   ACT.Copy).then_inc(sim_ready, 1)
                    yield
                act.wait_ge(den_in, k + 1)
                act.activation(cexp[:], c16[:], ACT.Exp, bias=shift[0:T]).then_inc(den_out, 1)
                yield
                for b in range(2):
                    act.wait_ge(st_done, 2 * k + b + 1)
                    act.activation(next_st[:, 4 * b:4 * b + 4, bass.ds(T * s, T)],
                                   misc[:, 0:4 * T].rearrange("p (h t) -> p h t", h=4), ACT.Copy
                                   ).then_inc(st_ready, 1)
                    yield

            def heads_and_attention(n, ahead):
                with act.Fori(0, HEADS // 2) as hh:
                    steps = sample_steps(n + 1, hh) if ahead else iter(())
                    for u in range(2):
                        base = 256 * n + 64 * hh + 32 * u
                        for t in range(NT):
                            act.wait_ge(sc_done, base + t + 1)
                            if t >= 4:
                                act.wait_ge(wt_ready, base + t - 3)
                            act.activation(ex[:, t % 4], SC[t % 4][:, 0:TG], ACT.Exp,
                                           bias=shift[:]).then_inc(ex_ready, 1)
                            if NT * u + t - 1 in (QUERY - 1, ) + SCORES + (RANK_END, ) + TURN:
                                next(steps, None)
                            if u == 1 and t in (3, NT - 1):
                                v = 0 if t == 3 else 1
                                act.wait_ge(kv_step, 256 * n + 64 * hh + NT * (v + 1))
                                act.activation(kvs[:], KV[v][:, 0:TG], ACT.Copy).then_inc(kvs_ready, 1)
                for s in range(G):
                    act.wait_ge(kt_done, G * n + s + 1)
                    act.activation(att.kt[:, :, T * s:T * s + T], KT[:, 0:4 * T].rearrange("p (j t) -> p j t", j=4),
                                   ACT.Copy).then_inc(kt_ready, 1)
                att.scalar(act, n)

            project(0)
            with act.Fori(0, G) as s:
                for _ in sample_steps(0, s):
                    pass
            with act.Fori(0, NG - 1) as n:
                project(n + 1)
                heads_and_attention(n, True)
            heads_and_attention(NG - 1, False)

        @block.vector
        def _(dve):
            setup = Link(dve, link_dve, 0, 3)
            norm.pads(dve, setup)
            setup(dve.memset(shift[:], SHIFT))
            dve.wait_ge(consts_in, 16 * len(consts))

            def top16(link, k, rows):
                dve.memset(spare[:, k:k + 1], 0.0)
                for i, (v, _, best) in enumerate(rows):
                    last = dve.max(best[:, 0:8], v)
                    if i % PER_TILE == 1 and i < len(rows) - 1:
                        yield
                link.mark(last)
                yield
                link.wait()
                dve.memset(spare[:, k + 1:k + 2], 0.0)
                for i, (v, rest, best) in enumerate(rows):
                    last = dve.match_replace(rest, best[:, 0:8], v, -3e38)
                    if i % PER_TILE == 1 and i < len(rows) - 1:
                        yield
                link.mark(last)
                yield
                link.wait()
                dve.memset(spare[:, k + 2:k + 3], 0.0)
                for i, (_, rest, best) in enumerate(rows):
                    last = dve.max(best[:, 8:16], rest)
                    if i % PER_TILE == 1 and i < len(rows) - 1:
                        yield
                link.mark(last)
                yield
                link.wait()

            def threshold_steps(m, s):
                k = G * m + s
                link = Link(dve, link_rank, k, RANK_LINKS)
                dve.wait_ge(sim_ready, 2 * k + 2)
                yield from top16(link, 0, [(sim[:, h, p], left[:, h, p], t16[:, h, p]) for h in range(HEADS)
                                           for p in range(2)])
                for a, (at, c) in enumerate(zip(starts, counts)):
                    dve.tensor_tensor(cand[:, :, at:at + c], t16[:, :, 1, 0:c],
                                      t16[:, :, 0, a:a + 1].to_broadcast([T, HEADS, c]), ALU.add)
                    if a % PER_TILE == 1:
                        yield
                at = sum(counts)
                link.mark(dve.tensor_tensor(cand[:, :, at:NCAND], t16[:, :, 0, TOP // 2:TOP],
                                            t16[:, :, 1, 0:1].to_broadcast([T, HEADS, TOP // 2]), ALU.add))
                yield
                link.wait()
                yield from top16(link, 3, [(cand[:, h], cleft[:, h], c16[:, h]) for h in range(HEADS)])
                ends = t16[:].rearrange("t h p k -> t (h p) k")[:, :, 0:TOP:TOP - 1]
                link.mark(dve.scalar_tensor_tensor(size[:].rearrange("t h p x -> t (h p) x"), ends, -1.0, ends,
                                                   ALU.mult, ALU.max))
                yield
                link.wait()
                link.mark(dve.tensor_reduce(thr[:, 0], size[:], AX.XY, ALU.add))
                yield
                link.wait()
                dve.tensor_scalar(thr[:, 2], c16[:, :, 0], -87.0, None, ALU.add)
                link.mark(dve.scalar_tensor_tensor(thr[:, 1], thr[:, 0], -1e-6, c16[:, :, TOP - 1], ALU.mult, ALU.add))
                yield
                link.wait()
                link.mark(dve.tensor_tensor(thr[:, 3], thr[:, 1], thr[:, 2], ALU.max))
                yield
                link.wait()
                dve.tensor_tensor(sim[:, :, 0, :], sim[:, :, 0, :], over(thr[:, 3], HALF),
                                  ALU.subtract).then_inc(simt_ready, 1)
                dve.tensor_tensor(c16[:], c16[:], over(thr[:, 3], TOP), ALU.subtract).then_inc(den_in, 1)
                yield
                yield
                yield
                dve.wait_ge(simt_ready, k + 1)
                dve.wait_ge(den_out, k + 1)
                link.mark(dve.scalar_tensor_tensor(cexp[:], c16[:], 0.0, cexp[:], ALU.is_ge, ALU.mult))
                yield
                link.wait()
                link.mark(dve.tensor_reduce(rsum[:], cexp[:], AX.X, ALU.add))
                yield
                link.wait()
                link.mark(dve.reciprocal(rsum[:], rsum[:]))
                yield
                link.wait()
                dve.tensor_copy(next_rden[:, bass.ds(s, 1), :].rearrange("t o h -> t (o h)"), rsum[:]
                                ).then_inc(rden_ready, 1)
                yield
                dve.wait_ge(rden_ready, k + 1)

            def keys_values(n, hh, u):
                dve.wait_ge(kvt_done, HEADS * n + 2 * hh + u + 1)
                dve.wait_ge(carried, BASE + n + 1)
                r = rden[:, :, bass.ds(2 * hh + u, 1)].to_broadcast([T, G, E])
                kv = KT[0:T, :].rearrange("p (s f) -> p s f", s=G)
                c = bass.ds(128 * hh + 64 * u, E)
                dve.tensor_tensor(ktok[:, :, c], kv[:, :, 0:E], r, ALU.mult)
                dve.tensor_tensor(att.v[:, :, c], kv[:, :, E:2 * E], r, ALU.mult).then_inc(kvn_ready, 1)

            def heads_and_attention(n, ahead):
                with dve.Fori(0, HEADS // 2) as hh:
                    steps = threshold_steps(n + 1, hh) if ahead else iter(())
                    for u in range(2):
                        base = 256 * n + 64 * hh + 32 * u
                        for t in range(NT):
                            dve.wait_ge(ex_ready, base + t + 1)
                            if t >= 4:
                                dve.wait_ge(kv_step, base + t - 3)
                            dve.scalar_tensor_tensor(wt[:, t % 4], SC[t % 4][:, 0:TG], 0.0, ex[:, t % 4],
                                                     ALU.is_ge, ALU.mult).then_inc(wt_ready, 1)
                            if u == 1 and t == 10:
                                keys_values(n, hh, 0)
                            if NT * u + t >= RANK:
                                next(steps, None)
                    for _ in steps:
                        assert False, "steps left at the end of the pair of heads"
                    keys_values(n, hh, 1)
                link = Link(dve, link_att, n, att.links + 1)
                att.vector(dve, link, n)
                h = group_of(H, n)
                dve.wait_ge(att.y_done, n + 1)
                link(dve.tensor_tensor(h, h, att.Y[0:T, 0:G * E].rearrange("p (s e) -> p s e", s=G), ALU.add))
                link.done()

            def normalise(m):
                link = Link(dve, link_dve, m, Norm.LINKS, 3)
                norm.vector(dve, link, group_of(H, m), m)
                link.done()

            normalise(0)
            with dve.Fori(0, G) as s:
                for _ in threshold_steps(0, s):
                    pass
            with dve.Fori(0, NG - 1) as n:
                normalise(n + 1)
                heads_and_attention(n, True)
            heads_and_attention(NG - 1, False)


def early_fusion_kernel(nc, d, out):
    with ExitStack() as ctx:
        H = ctx.enter_context(nc.sbuf_tensor("H", [96, 64, 64], F32))
        act_out = ctx.enter_context(nc.semaphore("ft_act_out"))
        f_out = ctx.enter_context(nc.semaphore("ft_f_out"))
        build_tokenizer(nc, d, H, act_out, f_out)
        for stage in (build_attention0, build_mlp0, build_linear_attention, build_mlp1, build_gauss_attention,
                      build_mlp2, build_diff_attention, build_product_keys,):
            stage(nc, d, H)
        store_tokens(nc, H, out)


def store_tokens(nc, H, out):
    with ExitStack() as ctx:
        stored = ctx.enter_context(nc.semaphore("stored"))
        block = ctx.enter_context(nc.Block())

        @block.sync
        def _(sp):
            sp.dma_start(out.rearrange("s t e -> t s e"), H[:]).then_inc(stored, 16)
            sp.wait_ge(stored, 16)


def lay_out(inputs):
    d, a = constants(inputs)
    return d


def constants(inputs):
    import numpy as np

    a = {k: np.asarray(v) for k, v in inputs.items()}
    f = np.float32
    d = {"ident": np.eye(128, dtype=f)}
    d["x"] = np.ascontiguousarray(a["x"].reshape(16, 4, 4096, 3).transpose(0, 1, 3, 2)).reshape(16, 12, 4096)
    d["grid"] = np.ascontiguousarray(a["L0_tok_input_grid"].reshape(4096, 2).transpose(1, 0))
    d["txt"] = np.ascontiguousarray(a["txt"].transpose(1, 0, 2))
    lift = np.zeros((14, 128), f)
    for s in range(4):
        lift[3 * s:3 * s + 3, 32 * s:32 * s + 32] = a["L0_tok_P_w"][2:5]
        lift[12:14, 32 * s:32 * s + 32] = a["L0_tok_P_w"][0:2]
    d["lift_w"] = lift
    d["lift_b"] = np.tile(a["L0_tok_P_b"], 4).reshape(128, 1)
    q1 = np.zeros((4, 32, 4, 32), f)
    q2 = np.zeros((4, 32, 4), f)
    for s in range(4):
        q1[s, :, s, :] = a["L0_tok_Q1_w"]
        q2[s, :, s] = a["L0_tok_Q2_w"][:, 0]
    d["conv_w"] = np.ascontiguousarray(a["L0_tok_conv_w"].transpose(0, 3, 2, 4, 1)).reshape(4, 96, 3, 32)
    d["conv_b"] = np.ascontiguousarray(np.tile(a["L0_tok_conv_b"], (1, 4)).transpose(1, 0))
    d["q1_w"] = q1.reshape(128, 128)
    d["q1_b"] = np.tile(a["L0_tok_Q1_b"], 4).reshape(128, 1)
    d["q2_w"] = q2.reshape(128, 4)
    d["q2_b"] = np.tile(a["L0_tok_Q2_b"], 4).reshape(4, 1)
    d["wr"] = a["L0_tok_spec_wr"].reshape(4, 32, 32, 256)
    d["wi"] = a["L0_tok_spec_wi"].reshape(4, 32, 32, 256)

    ang = 2 * np.pi * np.arange(64)[:, None] * np.arange(16)[None, :] / 64
    co, si = np.cos(ang), np.sin(ang)
    dw = np.zeros((2, 64, 2, 16, 2))
    for h in range(2):
        dw[h, :, h, :, 0] = co
        dw[h, :, h, :, 1] = -si
    d["dft_w"] = dw.reshape(128, 64).astype(f)
    dh = np.zeros((2, 64, 2, 16))
    dh[0, :, 0], dh[1, :, 0], dh[0, :, 1], dh[1, :, 1] = co, si, -si, co
    d["dft_h"] = dh.reshape(128, 32).astype(f)
    ih = np.zeros((8, 16, 2, 2, 16, 4, 16, 2))
    for mh in range(2):
        for y in range(16):
            cc = co[:, 8 * mh:8 * mh + 8].T.reshape(8, 16, 4)
            ss = si[:, 8 * mh:8 * mh + 8].T.reshape(8, 16, 4)
            ih[:, y, mh, 0, :, :, y, 0], ih[:, y, mh, 1, :, :, y, 0] = cc, -ss
            ih[:, y, mh, 0, :, :, y, 1], ih[:, y, mh, 1, :, :, y, 1] = ss, cc
    d["inv_h"] = ih.reshape(128, 4, 16, 128).astype(f)
    iw = np.zeros((4, 16, 2, 4, 64))
    weight = np.where(np.arange(16) == 0, 1.0, 2.0)[:, None] / 4096
    for h in range(4):
        iw[h, :, 0, h, :] = co.T * weight
        iw[h, :, 1, h, :] = -si.T * weight
    d["inv_w"] = iw.reshape(128, 256).astype(f)
    def with_bias(w, b):
        return np.concatenate([w, b.reshape(1, -1)], axis=0)

    def rows(x, n=96):
        return np.ascontiguousarray(np.broadcast_to(x, (n,) + x.shape))

    i, j = np.arange(96)[:, None], np.arange(96)[None, :]
    d["mask_strict"] = np.tile(np.where(j >= i, f(NEG), f(0)), (1, 4))
    d["mask_causal"] = np.tile(np.where(j > i, f(NEG), f(0)), (1, 4))

    d["a0_wqk"] = np.concatenate([with_bias(a["L0_attn_Wq"], a["L0_attn_bq"]),
                                  with_bias(a["L0_attn_Wk"], a["L0_attn_bk"])], axis=1).reshape(65, 8, 128)
    d["a0_wv"] = with_bias(a["L0_attn_Wv"], a["L0_attn_bv"])
    d["a0_wu"] = np.ascontiguousarray(a["L0_attn_Wu"].reshape(4, 128, 64).transpose(1, 0, 2))
    d["a0_bu"] = rows(a["L0_attn_bu"])
    d["upto"] = np.triu(np.ones((96, 96), f))
    d["ones"] = np.ones((96, 96), f)

    def routed(tag, gate_w, gate_b, w1, b1, w2, b2):
        x, _, fl = w1.shape
        n = fl // 128
        d[tag + "_gate"] = with_bias(gate_w, gate_b)
        both = np.concatenate([w1, b1.reshape(x, 1, fl)], axis=1)
        d[tag + "_w1"] = np.ascontiguousarray(both.transpose(1, 0, 2)).reshape(65, x * n, 128)
        d[tag + "_w2"] = np.ascontiguousarray(w2.reshape(x * n, 128, 64).transpose(1, 0, 2))
        d[tag + "_b2"] = b2
        pick = np.repeat(np.repeat(np.eye(x, dtype=f), n, axis=1)[:, :, None], 128, axis=2)
        d[tag + "_pick"] = np.zeros((128, 16, 128), f)
        d[tag + "_pick"][32:32 + 3 * x] = np.concatenate([pick] * 3)

    routed("f0", *[a["L0_ffn_" + k] for k in ("gate_w", "gate_b", "w1", "b1", "w2", "b2")])
    d["f0_gamma"], d["f0_beta"] = rows(a["L0_ffn_gamma"]), rows(a["L0_ffn_beta"])
    routed("f1", *[a["L1_ffn_" + k] for k in ("gate_w", "gate_b", "w1", "b1", "w2", "b2")])

    d["l1_wq"] = with_bias(a["L1_attn_W_qk"][0], a["L1_attn_b_qk"][0])
    d["l1_wk"] = with_bias(a["L1_attn_W_qk"][1], a["L1_attn_b_qk"][1])
    d["l1_wv"] = with_bias(a["L1_attn_W_v"], a["L1_attn_b_v"])
    d["l1_gamma"] = a["L1_attn_gamma"].reshape(64, 1)
    d["l1_beta"] = a["L1_attn_beta"].reshape(64, 1)
    zero = np.zeros((512,), f)
    heads = lambda w: np.ascontiguousarray(w.transpose(1, 0, 2)).reshape(64, 512)
    d["a2_wqk"] = np.concatenate([with_bias(heads(a["L2_attn_W_q"]), zero),
                                  with_bias(heads(a["L2_attn_W_k"]), zero)], axis=1).reshape(65, 8, 128)
    d["a2_wv"] = with_bias(heads(a["L2_attn_W_v"]), zero)
    d["a2_wo"] = np.ascontiguousarray(a["L2_attn_W_o"].transpose(1, 0).reshape(4, 128, 64).transpose(1, 0, 2))
    d["a2_scale"] = rows(a["L2_attn_ln_scale"])
    by_parity = a["L2_attn_gamma"].reshape(4, 2).transpose(1, 0)
    d["a2_gamma"] = rows(np.repeat(by_parity[:, :, None], 96, axis=2).reshape(2, 384))
    d["ones128"] = np.ones((128, 96), f)

    d["f2_gate"] = with_bias(a["L2_ffn_gW"], a["L2_ffn_gb"])
    w1, w2, w3 = np.zeros((65, 5, 128), f), np.zeros((128, 5, 128), f), np.zeros((128, 5, 64), f)
    b2, b3, pick = np.zeros((128, 5), f), np.zeros((5, 64), f), np.zeros((5, 5, 128), f)
    w1[:, 0, 0:64] = with_bias(a["L2_ffn_sW1"], a["L2_ffn_sb1"])
    w2[0:64, 0, :], b2[:, 0], w3[:, 0] = a["L2_ffn_sW2"], a["L2_ffn_sb2"], a["L2_ffn_sW3"]
    b3[4], pick[4, 0] = a["L2_ffn_sb3"], 1
    for x in range(4):
        w1[:, x + 1, :] = with_bias(a["L2_ffn_eW1"][x], a["L2_ffn_eb1"][x])
        w2[:, x + 1, 0:64], b2[0:64, x + 1] = a["L2_ffn_eW2"][x], a["L2_ffn_eb2"][x]
        w3[0:64, x + 1], b3[x], pick[x, x + 1] = a["L2_ffn_eW3"][x], a["L2_ffn_eb3"][x], 1
    d["f2_w1"], d["f2_w2"], d["f2_w3"], d["f2_b2"], d["f2_b3"], d["f2_pick"] = w1, w2, w3, b2, b3, pick

    d["a3_wq"] = np.ascontiguousarray(a["L3_attn_Wq"].transpose(1, 0))
    d["a3_wk"] = np.ascontiguousarray(a["L3_attn_Wk"].transpose(1, 0))
    d["a3_wv"] = np.ascontiguousarray(a["L3_attn_Wv"].reshape(32, 2, 64).transpose(2, 1, 0)).reshape(64, 64)
    wm = np.zeros((4, 32, 4), f)
    for k in range(4):
        wm[k, :, k] = a["L3_attn_w_mlp"]
    d["a3_wm"] = wm.reshape(128, 4)
    d["a3_bm"] = rows(a["L3_attn_b_mlp"])
    d["pk_wpk"] = a["L3_ffn_Wq_pk"].reshape(64, 4, 128)
    d["pk_wq"] = a["L3_ffn_Wq"].reshape(64, 4, 128)
    keys = a["L3_ffn_pk_keys"]
    kbd = np.zeros((4, 32, 4, 4, 64), f)
    for t in range(4):
        for k in range(4):
            kbd[k, :, t, k, :] = keys[t // 2, :, 4 * (t % 2) + k, :].transpose(1, 0)
    d["pk_kbd"] = kbd.reshape(128, 4, 256)
    sel = np.zeros((128, 9, 2, 64), f)
    for i in range(64):
        sel[i, :, :, i] = 1
        sel[64 + i, 0, :, i] = 1
    for i in range(16):
        for k in range(3):
            sel[64 + 16 * k + i, 1 + i // 2, i % 2, :] = 1
    d["pk_sel"] = sel.reshape(128, 9, 128)
    both = np.concatenate([a["L3_ffn_keys_table"], a["L3_ffn_values_table"]], axis=1)
    d["pk_table"] = np.ascontiguousarray(both.reshape(8, 32, 128, 128).transpose(0, 2, 1, 3))
    d["pk_wo"] = np.ascontiguousarray(a["L3_ffn_Wo"].reshape(4, 128, 64).transpose(1, 0, 2))
    return d, a


def kernel(**inputs):
    import numpy as _np
    import concourse.bacc as _bacc
    from concourse import mybir as _mybir
    from concourse.bass_utils import run_bass_kernel_spmd as _run

    nc = _bacc.Bacc("TRN2", target_bir_lowering=False, num_devices=1)
    laid = lay_out(inputs)
    arrays, d = {}, {}
    for name, a in laid.items():
        a = _np.ascontiguousarray(a)
        arrays[f"in_{name}_dram"] = a
        d[name] = nc.dram_tensor(f"in_{name}_dram", a.shape, _mybir.dt.from_np(a.dtype), kind="ExternalInput").ap()
    out = nc.dram_tensor("out_0_dram", (64, 96, 64), _mybir.dt.float32, kind="ExternalOutput").ap()
    early_fusion_kernel(nc, d, out)
    r = _run(nc, [arrays], core_ids=[0])
    return r.results[0]["out_0_dram"]
```
